# Optimizing a Trainium2 kernel written in Bass

```python
import numpy as np
import jax
import jax.numpy as jnp

def _softmax(x, axis=-1):
    return jax.nn.softmax(x, axis=axis)

def _gelu(x):
    return jax.nn.gelu(x, approximate=True)

def _silu(x):
    return jax.nn.silu(x)

def _sigmoid(x):
    return jax.nn.sigmoid(x)

def _layernorm(x, axis=-1, eps=1e-05):
    m = jnp.mean(x, axis=axis, keepdims=True)
    v = jnp.var(x, axis=axis, keepdims=True)
    return (x - m) / jnp.sqrt(v + eps)

def _scatter_add(tgt, idx, src, axis=0):
    return tgt.at[idx].add(src)

def _segment_sum(src, seg, n):
    return jax.ops.segment_sum(src, seg, n)
kernel_name = 'mk_sandwich_d2_jaxref_r8_bfb869'

def setup_inputs(seed: int=0):
    np.random.seed(seed)
    _w = jnp.asarray

    def _L0_attn_setup():
        import jax, jax.numpy as jnp
        import numpy as np
        B, S, D, H = (2, 256, 128, 16)
        DK = D // H
        key = jax.random.key(seed)
        ks = jax.random.split(key, 9)
        s = 0.02
        return {'embeddings': jax.random.normal(ks[0], (B, S, D), jnp.float32), 'Wq': jax.random.normal(ks[1], (H, D, DK), jnp.float32) * s, 'bq': jax.random.normal(ks[2], (H, DK), jnp.float32) * s, 'Wk': jax.random.normal(ks[3], (H, D, DK), jnp.float32) * s, 'bk': jax.random.normal(ks[4], (H, DK), jnp.float32) * s, 'Wv': jax.random.normal(ks[5], (H, D, DK), jnp.float32) * s, 'bv': jax.random.normal(ks[6], (H, DK), jnp.float32) * s, 'Wo': jax.random.normal(ks[7], (D, D), jnp.float32) * s, 'bo': jax.random.normal(ks[8], (D,), jnp.float32) * s}
    _L0_attn_in = _L0_attn_setup()

    def _L0_ffn_setup():
        import jax, jax.numpy as jnp
        import numpy as np
        DIM = 128
        DEPTH = 6
        HEADS = 16
        DIM_HEAD = 64
        WINDOW = 32
        INNER = HEADS * DIM_HEAD
        DIM_INNER = int(DIM * 4 * 2 / 3)
        QK_SCALE = 8.0

        def shift_tokens(t):
            a, s = jnp.split(t, 2, -1)
            s = jnp.pad(s, ((0, 0), (1, 0), (0, 0)))[:, :-1]
            return jnp.concatenate([a, s], -1)

        def l2norm(t):
            return t / jnp.maximum(jnp.linalg.norm(t, axis=-1, keepdims=True), 1e-12)

        def rotate_half(x):
            x1, x2 = jnp.split(x, 2, -1)
            return jnp.concatenate([-x2, x1], -1)

        def rotary_tables(n):
            half = jnp.arange(0, DIM_HEAD, 2, dtype=jnp.float32)
            inv_freq = 1.0 / 10000.0 ** (half / DIM_HEAD)
            t = jnp.arange(n, dtype=jnp.float32)
            freqs = t[:, None] * inv_freq[None, :]
            freqs = jnp.concatenate([freqs, freqs], -1)
            base_scale = (half + 0.4 * DIM_HEAD) / (1.4 * DIM_HEAD)
            power = (t - n // 2) / (WINDOW // 2)
            scale = base_scale[None, :] ** power[:, None]
            scale = jnp.concatenate([scale, scale], -1)
            return (freqs, scale)

        def local_attention(q, k, v):
            b, h, n, d = q.shape
            w = WINDOW
            nw = n // w
            bq = q.reshape(b, h, nw, w, d)
            bk = k.reshape(b, h, nw, w, d)
            bv = v.reshape(b, h, nw, w, d)

            def look(t):
                p = jnp.pad(t, ((0, 0), (0, 0), (1, 0), (0, 0), (0, 0)))
                return jnp.concatenate([p[:, :, :nw], p[:, :, 1:]], axis=3)
            bk2, bv2 = (look(bk), look(bv))
            seq = jnp.arange(n).reshape(nw, w)
            seq_p = jnp.pad(seq, ((1, 0), (0, 0)), constant_values=-1)
            jt = jnp.concatenate([seq_p[:nw], seq_p[1:]], axis=1)
            it = seq[:, :, None]
            jb = jt[:, None, :]
            mask = (it < jb) | (it > jb + w) | (jb == -1)
            sim = jnp.einsum('bhwie,bhwje->bhwij', bq, bk2) * QK_SCALE
            sim = jnp.where(mask, -jnp.finfo(sim.dtype).max, sim)
            attn = jax.nn.softmax(sim, -1)
            out = jnp.einsum('bhwij,bhwje->bhwie', attn, bv2)
            return out.reshape(b, h, n, d)

        def attn_layer(x, Wqkv, qs, ksc, Wo):
            b, n, _ = x.shape
            qkv = x @ Wqkv
            q, k, v = jnp.split(qkv, 3, -1)
            sh = lambda t: t.reshape(b, n, HEADS, DIM_HEAD).transpose(0, 2, 1, 3)
            q, k, v = (sh(q), sh(k), sh(v))
            q = l2norm(q) * qs
            k = l2norm(k) * ksc
            freqs, scale = rotary_tables(n)
            cos, sin = (jnp.cos(freqs), jnp.sin(freqs))
            q = q * cos * scale + rotate_half(q) * sin * scale
            inv = 1.0 / scale
            k = k * cos * inv + rotate_half(k) * sin * inv
            out = local_attention(q, k, v)
            out = out.transpose(0, 2, 1, 3).reshape(b, n, INNER)
            return out @ Wo

        def ffn_layer(x, g, bln, W1, b1, W2, b2):
            mu = x.mean(-1, keepdims=True)
            var = ((x - mu) ** 2).mean(-1, keepdims=True)
            xn = (x - mu) / jnp.sqrt(var + 1e-05) * g + bln
            hg = xn @ W1 + b1
            a, gate = jnp.split(hg, 2, -1)
            return a * jax.nn.gelu(gate, approximate=False) @ W2 + b2
        key = jax.random.key(seed)
        ks = jax.random.split(key, 8)
        B, N = (2, 256)
        init = lambda k, shape: jax.random.normal(k, shape, jnp.float32) * 0.02
        return {'x': jax.random.normal(ks[0], (B, N, DIM), jnp.float32), 'Wqkv': init(ks[1], (DEPTH, DIM, 3 * INNER)), 'q_scale': jnp.ones((DEPTH, DIM_HEAD), jnp.float32), 'k_scale': jnp.ones((DEPTH, DIM_HEAD), jnp.float32), 'Wo': init(ks[2], (DEPTH, INNER, DIM)), 'ln_g': jnp.ones((DEPTH, DIM), jnp.float32), 'ln_b': jnp.zeros((DEPTH, DIM), jnp.float32), 'W1': init(ks[3], (DEPTH, DIM, 2 * DIM_INNER)), 'b1': jnp.zeros((DEPTH, 2 * DIM_INNER), jnp.float32), 'W2': init(ks[4], (DEPTH, DIM_INNER, DIM)), 'b2': jnp.zeros((DEPTH, DIM), jnp.float32)}
    _L0_ffn_in = _L0_ffn_setup()

    def _L1_attn_setup():
        import jax, jax.numpy as jnp
        import numpy as np
        B, N, C, H = (2, 256, 128, 16)
        R1, R2 = (4, 8)
        HEAD_DIM = C // H
        SCALE = float((R1 * R2) ** (-0.5))
        key = jax.random.key(seed)
        ks = jax.random.split(key, 8)
        g = lambda k, shape, s: jax.random.normal(k, shape, jnp.float32) * s
        return {'x': g(ks[0], (B, N, C), 1.0), 'Wq1': g(ks[1], (H * R1, C), C ** (-0.5)), 'Wk1': g(ks[2], (H * R1, C), C ** (-0.5)), 'Wq2': g(ks[3], (H * R2, C), C ** (-0.5)), 'Wk2': g(ks[4], (H * R2, C), C ** (-0.5)), 'Wv': g(ks[5], (C, C), C ** (-0.5)), 'Wo': g(ks[6], (C, C), C ** (-0.5)), 'bo': jnp.zeros((C,), jnp.float32)}
    _L1_attn_in = _L1_attn_setup()

    def _L1_ffn_setup():
        import jax, jax.numpy as jnp
        import numpy as np
        EMBED = 128
        HEADS = 16
        HEAD_DIM = EMBED // HEADS
        NUM_EXPERTS = 8
        TOP_K = 2
        HIDDEN = (int(2 * (4 * EMBED) / 3) + 63) // 64 * 64
        SEQ = 256
        BATCH = 2
        ROPE_BASE = 10000.0
        EPS = 1e-06

        def _rope_tables(seq_len, dim):
            inv_freq = 1.0 / ROPE_BASE ** (np.arange(0, dim, 2, dtype=np.float32) / dim)
            t = np.arange(seq_len, dtype=np.float32)
            freqs = np.einsum('i,j->ij', t, inv_freq)
            emb = np.concatenate([freqs, freqs], axis=-1)
            return (jnp.asarray(np.cos(emb)), jnp.asarray(np.sin(emb)))

        def _rotate_half(x):
            x1, x2 = jnp.split(x, 2, axis=-1)
            return jnp.concatenate([-x2, x1], axis=-1)

        def _rmsnorm(x, w):
            return x * jax.lax.rsqrt(jnp.mean(x * x, axis=-1, keepdims=True) + EPS) * w

        def _attention(x, wq, wk, wv, wo):
            B, S, _ = x.shape
            q = (x @ wq).reshape(B, S, HEADS, HEAD_DIM).transpose(0, 2, 1, 3)
            k = (x @ wk).reshape(B, S, HEADS, HEAD_DIM).transpose(0, 2, 1, 3)
            v = (x @ wv).reshape(B, S, HEADS, HEAD_DIM).transpose(0, 2, 1, 3)
            cos, sin = _rope_tables(S, HEAD_DIM)
            cos = cos[None, None]
            sin = sin[None, None]
            q = q * cos + _rotate_half(q) * sin
            k = k * cos + _rotate_half(k) * sin
            scale = HEAD_DIM ** (-0.5)
            scores = jnp.einsum('bhqd,bhkd->bhqk', q, k) * scale
            causal = jnp.triu(jnp.ones((S, S), bool), k=1)
            scores = jnp.where(causal, -jnp.inf, scores)
            attn = jax.nn.softmax(scores, axis=-1)
            out = jnp.einsum('bhqk,bhkd->bhqd', attn, v)
            out = out.transpose(0, 2, 1, 3).reshape(B, S, EMBED)
            return out @ wo

        def _moe(x, w_router, wg, wu, wd):
            B, S, E = x.shape
            xf = x.reshape(-1, E)
            logits = xf @ w_router
            probs = jax.nn.softmax(logits, axis=-1)
            topw, topi = jax.lax.top_k(probs, TOP_K)
            topw = topw / jnp.sum(topw, axis=-1, keepdims=True)
            combine = jnp.sum(jax.nn.one_hot(topi, NUM_EXPERTS, dtype=xf.dtype) * topw[..., None], axis=1)
            g = jax.nn.silu(jnp.einsum('td,xdh->txh', xf, wg))
            u = jnp.einsum('td,xdh->txh', xf, wu)
            eo = jnp.einsum('txh,xhd->txd', g * u, wd)
            out = jnp.einsum('txd,tx->td', eo, combine)
            return out.reshape(B, S, E)
        key = jax.random.key(seed)
        ks = jax.random.split(key, 12)
        s = 0.02
        return {'x': jax.random.normal(ks[0], (BATCH, SEQ, EMBED), jnp.float32), 'wq': jax.random.normal(ks[1], (EMBED, EMBED), jnp.float32) * s, 'wk': jax.random.normal(ks[2], (EMBED, EMBED), jnp.float32) * s, 'wv': jax.random.normal(ks[3], (EMBED, EMBED), jnp.float32) * s, 'wo': jax.random.normal(ks[4], (EMBED, EMBED), jnp.float32) * s, 'w_router': jax.random.normal(ks[5], (EMBED, NUM_EXPERTS), jnp.float32) * s, 'wg': jax.random.normal(ks[6], (NUM_EXPERTS, EMBED, HIDDEN), jnp.float32) * s, 'wu': jax.random.normal(ks[7], (NUM_EXPERTS, EMBED, HIDDEN), jnp.float32) * s, 'wd': jax.random.normal(ks[8], (NUM_EXPERTS, HIDDEN, EMBED), jnp.float32) * s, 'g1': jnp.ones((EMBED,), jnp.float32), 'g2': jnp.ones((EMBED,), jnp.float32)}
    _L1_ffn_in = _L1_ffn_setup()
    _d = {'L0_attn_embeddings': _L0_attn_in['embeddings'], 'L0_attn_Wq': _L0_attn_in['Wq'], 'L0_attn_bq': _L0_attn_in['bq'], 'L0_attn_Wk': _L0_attn_in['Wk'], 'L0_attn_bk': _L0_attn_in['bk'], 'L0_attn_Wv': _L0_attn_in['Wv'], 'L0_attn_bv': _L0_attn_in['bv'], 'L0_attn_Wo': _L0_attn_in['Wo'], 'L0_attn_bo': _L0_attn_in['bo'], 'L0_ffn_Wqkv': _L0_ffn_in['Wqkv'], 'L0_ffn_q_scale': _L0_ffn_in['q_scale'], 'L0_ffn_k_scale': _L0_ffn_in['k_scale'], 'L0_ffn_Wo': _L0_ffn_in['Wo'], 'L0_ffn_ln_g': _L0_ffn_in['ln_g'], 'L0_ffn_ln_b': _L0_ffn_in['ln_b'], 'L0_ffn_W1': _L0_ffn_in['W1'], 'L0_ffn_b1': _L0_ffn_in['b1'], 'L0_ffn_W2': _L0_ffn_in['W2'], 'L0_ffn_b2': _L0_ffn_in['b2'], 'L1_attn_Wq1': _L1_attn_in['Wq1'], 'L1_attn_Wk1': _L1_attn_in['Wk1'], 'L1_attn_Wq2': _L1_attn_in['Wq2'], 'L1_attn_Wk2': _L1_attn_in['Wk2'], 'L1_attn_Wv': _L1_attn_in['Wv'], 'L1_attn_Wo': _L1_attn_in['Wo'], 'L1_attn_bo': _L1_attn_in['bo'], 'L1_ffn_wq': _L1_ffn_in['wq'], 'L1_ffn_wk': _L1_ffn_in['wk'], 'L1_ffn_wv': _L1_ffn_in['wv'], 'L1_ffn_wo': _L1_ffn_in['wo'], 'L1_ffn_w_router': _L1_ffn_in['w_router'], 'L1_ffn_wg': _L1_ffn_in['wg'], 'L1_ffn_wu': _L1_ffn_in['wu'], 'L1_ffn_wd': _L1_ffn_in['wd'], 'L1_ffn_g1': _L1_ffn_in['g1'], 'L1_ffn_g2': _L1_ffn_in['g2']}
    _x0 = _d['L0_attn_embeddings']
    _d['L0_attn_embeddings'] = jax.random.normal(jax.random.fold_in(jax.random.key(seed), 1), (4, 1024, 128), dtype=_x0.dtype)
    del _x0
    return _d

def reference(L0_attn_embeddings, L0_attn_Wq, L0_attn_bq, L0_attn_Wk, L0_attn_bk, L0_attn_Wv, L0_attn_bv, L0_attn_Wo, L0_attn_bo, L0_ffn_Wqkv, L0_ffn_q_scale, L0_ffn_k_scale, L0_ffn_Wo, L0_ffn_ln_g, L0_ffn_ln_b, L0_ffn_W1, L0_ffn_b1, L0_ffn_W2, L0_ffn_b2, L1_attn_Wq1, L1_attn_Wk1, L1_attn_Wq2, L1_attn_Wk2, L1_attn_Wv, L1_attn_Wo, L1_attn_bo, L1_ffn_wq, L1_ffn_wk, L1_ffn_wv, L1_ffn_wo, L1_ffn_w_router, L1_ffn_wg, L1_ffn_wu, L1_ffn_wd, L1_ffn_g1, L1_ffn_g2):

    def _L0_attn_ref(embeddings, Wq, bq, Wk, bk, Wv, bv, Wo, bo):
        import jax, jax.numpy as jnp
        import numpy as np
        B, S, D, H = (2, 256, 128, 16)
        DK = D // H
        b, s, d = embeddings.shape
        dk = Wq.shape[-1]
        q = jnp.einsum('bsd,hdk->bhsk', embeddings, Wq) + bq[None, :, None, :]
        k = jnp.einsum('bsd,hdk->bhsk', embeddings, Wk) + bk[None, :, None, :]
        v = jnp.einsum('bsd,hdk->bhsk', embeddings, Wv) + bv[None, :, None, :]
        scores = jnp.einsum('bhqk,bhsk->bhqs', q, k) / jnp.sqrt(jnp.float32(dk))
        causal_mask = jnp.triu(jnp.ones((s, s), dtype=bool), k=1)
        scores = jnp.where(causal_mask, jnp.float32(-1000000000.0), scores)
        weights = jax.nn.softmax(scores, axis=-1)
        ctx = jnp.einsum('bhqs,bhsk->bhqk', weights, v)
        concat = ctx.transpose(0, 2, 1, 3).reshape(b, s, d)
        return concat @ Wo + bo

    def _L0_ffn_ref(x, Wqkv, q_scale, k_scale, Wo, ln_g, ln_b, W1, b1, W2, b2):
        import jax, jax.numpy as jnp
        import numpy as np
        DIM = 128
        DEPTH = 6
        HEADS = 16
        DIM_HEAD = 64
        WINDOW = 32
        INNER = HEADS * DIM_HEAD
        DIM_INNER = int(DIM * 4 * 2 / 3)
        QK_SCALE = 8.0

        def shift_tokens(t):
            a, s = jnp.split(t, 2, -1)
            s = jnp.pad(s, ((0, 0), (1, 0), (0, 0)))[:, :-1]
            return jnp.concatenate([a, s], -1)

        def l2norm(t):
            return t / jnp.maximum(jnp.linalg.norm(t, axis=-1, keepdims=True), 1e-12)

        def rotate_half(x):
            x1, x2 = jnp.split(x, 2, -1)
            return jnp.concatenate([-x2, x1], -1)

        def rotary_tables(n):
            half = jnp.arange(0, DIM_HEAD, 2, dtype=jnp.float32)
            inv_freq = 1.0 / 10000.0 ** (half / DIM_HEAD)
            t = jnp.arange(n, dtype=jnp.float32)
            freqs = t[:, None] * inv_freq[None, :]
            freqs = jnp.concatenate([freqs, freqs], -1)
            base_scale = (half + 0.4 * DIM_HEAD) / (1.4 * DIM_HEAD)
            power = (t - n // 2) / (WINDOW // 2)
            scale = base_scale[None, :] ** power[:, None]
            scale = jnp.concatenate([scale, scale], -1)
            return (freqs, scale)

        def local_attention(q, k, v):
            b, h, n, d = q.shape
            w = WINDOW
            nw = n // w
            bq = q.reshape(b, h, nw, w, d)
            bk = k.reshape(b, h, nw, w, d)
            bv = v.reshape(b, h, nw, w, d)

            def look(t):
                p = jnp.pad(t, ((0, 0), (0, 0), (1, 0), (0, 0), (0, 0)))
                return jnp.concatenate([p[:, :, :nw], p[:, :, 1:]], axis=3)
            bk2, bv2 = (look(bk), look(bv))
            seq = jnp.arange(n).reshape(nw, w)
            seq_p = jnp.pad(seq, ((1, 0), (0, 0)), constant_values=-1)
            jt = jnp.concatenate([seq_p[:nw], seq_p[1:]], axis=1)
            it = seq[:, :, None]
            jb = jt[:, None, :]
            mask = (it < jb) | (it > jb + w) | (jb == -1)
            sim = jnp.einsum('bhwie,bhwje->bhwij', bq, bk2) * QK_SCALE
            sim = jnp.where(mask, -jnp.finfo(sim.dtype).max, sim)
            attn = jax.nn.softmax(sim, -1)
            out = jnp.einsum('bhwij,bhwje->bhwie', attn, bv2)
            return out.reshape(b, h, n, d)

        def attn_layer(x, Wqkv, qs, ksc, Wo):
            b, n, _ = x.shape
            qkv = x @ Wqkv
            q, k, v = jnp.split(qkv, 3, -1)
            sh = lambda t: t.reshape(b, n, HEADS, DIM_HEAD).transpose(0, 2, 1, 3)
            q, k, v = (sh(q), sh(k), sh(v))
            q = l2norm(q) * qs
            k = l2norm(k) * ksc
            freqs, scale = rotary_tables(n)
            cos, sin = (jnp.cos(freqs), jnp.sin(freqs))
            q = q * cos * scale + rotate_half(q) * sin * scale
            inv = 1.0 / scale
            k = k * cos * inv + rotate_half(k) * sin * inv
            out = local_attention(q, k, v)
            out = out.transpose(0, 2, 1, 3).reshape(b, n, INNER)
            return out @ Wo

        def ffn_layer(x, g, bln, W1, b1, W2, b2):
            mu = x.mean(-1, keepdims=True)
            var = ((x - mu) ** 2).mean(-1, keepdims=True)
            xn = (x - mu) / jnp.sqrt(var + 1e-05) * g + bln
            hg = xn @ W1 + b1
            a, gate = jnp.split(hg, 2, -1)
            return a * jax.nn.gelu(gate, approximate=False) @ W2 + b2
        for i in range(DEPTH):
            x = attn_layer(shift_tokens(x), Wqkv[i], q_scale[i], k_scale[i], Wo[i]) + x
            x = ffn_layer(shift_tokens(x), ln_g[i], ln_b[i], W1[i], b1[i], W2[i], b2[i]) + x
        return x

    def _L1_attn_ref(x, Wq1, Wk1, Wq2, Wk2, Wv, Wo, bo):
        import jax, jax.numpy as jnp
        import numpy as np
        B, N, C, H = (2, 256, 128, 16)
        R1, R2 = (4, 8)
        HEAD_DIM = C // H
        SCALE = float((R1 * R2) ** (-0.5))
        b, n, c = x.shape
        q1 = (x @ Wq1.T).reshape(b, n, H, R1)
        k1 = (x @ Wk1.T).reshape(b, n, H, R1)
        q2 = (x @ Wq2.T).reshape(b, n, H, R2)
        k2 = (x @ Wk2.T).reshape(b, n, H, R2)
        v = (x @ Wv.T).reshape(b, n, H, HEAD_DIM)
        A1 = jnp.einsum('bnhr,bmhr->bhnm', q1, k1)
        A2 = jnp.einsum('bnhr,bmhr->bhnm', q2, k2)
        logits = A1 * A2 * SCALE
        causal = jnp.triu(jnp.ones((n, n), dtype=bool), 1)
        logits = jnp.where(causal[None, None], -jnp.inf, logits)
        attn = jax.nn.softmax(logits, axis=-1)
        out = jnp.einsum('bhnm,bmhd->bnhd', attn, v).reshape(b, n, c)
        return out @ Wo.T + bo

    def _L1_ffn_ref(x, wq, wk, wv, wo, w_router, wg, wu, wd, g1, g2):
        import jax, jax.numpy as jnp
        import numpy as np
        EMBED = 128
        HEADS = 16
        HEAD_DIM = EMBED // HEADS
        NUM_EXPERTS = 8
        TOP_K = 2
        HIDDEN = (int(2 * (4 * EMBED) / 3) + 63) // 64 * 64
        SEQ = 256
        BATCH = 2
        ROPE_BASE = 10000.0
        EPS = 1e-06

        def _rope_tables(seq_len, dim):
            inv_freq = 1.0 / ROPE_BASE ** (np.arange(0, dim, 2, dtype=np.float32) / dim)
            t = np.arange(seq_len, dtype=np.float32)
            freqs = np.einsum('i,j->ij', t, inv_freq)
            emb = np.concatenate([freqs, freqs], axis=-1)
            return (jnp.asarray(np.cos(emb)), jnp.asarray(np.sin(emb)))

        def _rotate_half(x):
            x1, x2 = jnp.split(x, 2, axis=-1)
            return jnp.concatenate([-x2, x1], axis=-1)

        def _rmsnorm(x, w):
            return x * jax.lax.rsqrt(jnp.mean(x * x, axis=-1, keepdims=True) + EPS) * w

        def _attention(x, wq, wk, wv, wo):
            B, S, _ = x.shape
            q = (x @ wq).reshape(B, S, HEADS, HEAD_DIM).transpose(0, 2, 1, 3)
            k = (x @ wk).reshape(B, S, HEADS, HEAD_DIM).transpose(0, 2, 1, 3)
            v = (x @ wv).reshape(B, S, HEADS, HEAD_DIM).transpose(0, 2, 1, 3)
            cos, sin = _rope_tables(S, HEAD_DIM)
            cos = cos[None, None]
            sin = sin[None, None]
            q = q * cos + _rotate_half(q) * sin
            k = k * cos + _rotate_half(k) * sin
            scale = HEAD_DIM ** (-0.5)
            scores = jnp.einsum('bhqd,bhkd->bhqk', q, k) * scale
            causal = jnp.triu(jnp.ones((S, S), bool), k=1)
            scores = jnp.where(causal, -jnp.inf, scores)
            attn = jax.nn.softmax(scores, axis=-1)
            out = jnp.einsum('bhqk,bhkd->bhqd', attn, v)
            out = out.transpose(0, 2, 1, 3).reshape(B, S, EMBED)
            return out @ wo

        def _moe(x, w_router, wg, wu, wd):
            B, S, E = x.shape
            xf = x.reshape(-1, E)
            logits = xf @ w_router
            probs = jax.nn.softmax(logits, axis=-1)
            topw, topi = jax.lax.top_k(probs, TOP_K)
            topw = topw / jnp.sum(topw, axis=-1, keepdims=True)
            combine = jnp.sum(jax.nn.one_hot(topi, NUM_EXPERTS, dtype=xf.dtype) * topw[..., None], axis=1)
            g = jax.nn.silu(jnp.einsum('td,xdh->txh', xf, wg))
            u = jnp.einsum('td,xdh->txh', xf, wu)
            eo = jnp.einsum('txh,xhd->txd', g * u, wd)
            out = jnp.einsum('txd,tx->td', eo, combine)
            return out.reshape(B, S, E)
        h = x + _attention(_rmsnorm(x, g1), wq, wk, wv, wo)
        y = h + _moe(_rmsnorm(h, g2), w_router, wg, wu, wd)
        return y
    x = L0_attn_embeddings
    x = x + _layernorm(_L0_attn_ref(_layernorm(x, axis=-1), L0_attn_Wq, L0_attn_bq, L0_attn_Wk, L0_attn_bk, L0_attn_Wv, L0_attn_bv, L0_attn_Wo, L0_attn_bo), axis=-1)
    x = x + _layernorm(_L0_ffn_ref(_layernorm(x, axis=-1), L0_ffn_Wqkv, L0_ffn_q_scale, L0_ffn_k_scale, L0_ffn_Wo, L0_ffn_ln_g, L0_ffn_ln_b, L0_ffn_W1, L0_ffn_b1, L0_ffn_W2, L0_ffn_b2), axis=-1)
    x = x + _layernorm(_L1_attn_ref(_layernorm(x, axis=-1), L1_attn_Wq1, L1_attn_Wk1, L1_attn_Wq2, L1_attn_Wk2, L1_attn_Wv, L1_attn_Wo, L1_attn_bo), axis=-1)
    x = x + _layernorm(_L1_ffn_ref(_layernorm(x, axis=-1), L1_ffn_wq, L1_ffn_wk, L1_ffn_wv, L1_ffn_wo, L1_ffn_w_router, L1_ffn_wg, L1_ffn_wu, L1_ffn_wd, L1_ffn_g1, L1_ffn_g2), axis=-1)
    return x

_drawn_inputs = setup_inputs


def setup_inputs(seed=0):
    import zlib

    import numpy as np

    out = dict(_drawn_inputs(seed))
    spreads = {'L0_ffn_q_scale': (1.0, 0.6),
     'L0_ffn_k_scale': (1.0, 0.6),
     'L0_ffn_ln_g': (1.0, 0.6),
     'L0_ffn_ln_b': (0.0, 0.8),
     'L0_ffn_b1': (0.0, 0.8),
     'L0_ffn_b2': (0.0, 0.1),
     'L1_attn_bo': (0.0, 0.1),
     'L1_ffn_g1': (1.0, 0.6),
     'L1_ffn_g2': (1.0, 0.6)}
    factors = {'L0_attn_Wq': 5.583,
     'L0_attn_bq': 8.0,
     'L0_attn_Wk': 5.617,
     'L0_attn_bk': 8.0,
     'L0_ffn_W1': 4.222,
     'L0_ffn_W2': 4.461,
     'L1_ffn_wq': 8.0,
     'L1_ffn_wk': 8.0,
     'L1_ffn_wv': 5.668,
     'L1_ffn_wo': 5.928,
     'L1_ffn_w_router': 8.0,
     'L1_ffn_wg': 8.0,
     'L1_ffn_wu': 8.0,
     'L1_ffn_wd': 8.0}
    for name, (base, spread) in spreads.items():
        noise = np.random.default_rng([zlib.crc32(name.encode()), seed]).standard_normal(out[name].shape)
        drawn = base * np.exp(spread * noise) if base else spread * noise
        out[name] = jnp.asarray(drawn.astype(out[name].dtype))
    for name, factor in factors.items():
        out[name] = (out[name] * factor).astype(out[name].dtype)
    return out
```

```python
import concourse.bass as bass
from concourse import mybir
from contextlib import ExitStack

FP32 = mybir.dt.float32
BF16 = mybir.dt.bfloat16
ALU = mybir.AluOpType
ACT = mybir.ActivationFunctionType
AX = mybir.AxisListType

P = 128
B, S, D = 4, 1024, 128
NT = B * S // P
TB = S // P
CH = 4
CW = CH * P
NC_ = NT // CH
HALVES = S // CW
H = 16
HG = 4
NG = H // HG
VC = 32
EPS_LN = 1e-5
EPS_RMS = 1e-6
NEG = -1e30




class Signal:

    def __init__(self, sem):
        self.sem, self.base, self.per = sem, 1, 0

    def loop(self, per):
        self.per = per
        return self

    def at(self, turn, count):
        return turn * self.per + (self.base + count)

    def end(self, turns):
        self.base += turns * self.per


class Chain:

    def __init__(self, eng, signal, turn):
        self.eng, self.of, self.turn, self.count = eng, signal, turn, 0

    def link(self, ins):
        ins.then_inc(self.of.sem, 1)
        self.count += 1

    def wait(self):
        self.eng.wait_ge(self.of.sem, self.of.at(self.turn, self.count))


def row_stats(e, chain, st, work, n):
    me, me2, mo, mo2 = (st[:, 0:n, k] for k in (1, 2, 4, 5))
    chain.wait()
    e.tensor_tensor(work[:, 2, 0:n], me, mo, ALU.add)
    e.tensor_tensor(work[:, 3, 0:n], me, mo, ALU.subtract)
    chain.link(e.tensor_tensor(work[:, 4, 0:n], me2, mo2, ALU.add))
    chain.wait()
    e.tensor_scalar(work[:, 0, 0:n], work[:, 2, 0:n], 0.5, None, ALU.mult)
    e.tensor_scalar(work[:, 4, 0:n], work[:, 4, 0:n], 1.0 / D, None, ALU.mult)
    chain.link(e.scalar_tensor_tensor(out=work[:, 5, 0:n], in0=work[:, 3, 0:n], scalar=0.25, in1=work[:, 3, 0:n],
                                      op0=ALU.mult, op1=ALU.mult))
    chain.wait()
    chain.link(e.tensor_tensor(work[:, 1, 0:n], work[:, 4, 0:n], work[:, 5, 0:n], ALU.add))


def ask_root(e, chain, roots, out, var, eps):
    chain.wait()
    e.tensor_scalar(out, var, eps, None, ALU.add).then_inc(roots.asked.sem, 1)
    roots.count += 1
    e.wait_ge(roots.given.sem, roots.given.at(chain.turn, roots.count))


class Roots:

    def __init__(self, c, per):
        self.asked, self.given, self.count = c.new_signal("root_asked", per), c.new_signal("root_given", per), 0

    def give(self, pool, c, turn, count, value):
        pool.wait_ge(self.asked.sem, self.asked.at(turn, count))
        pool.tensor_tensor(value, value, c.half[:, 0:value.shape[1]], ALU.pow).then_inc(self.given.sem, 1)

    def end(self, turns):
        self.asked.end(turns)
        self.given.end(turns)


class Core:

    def __init__(self, nc, ins, ctx):
        self.nc, self.ins, self.ctx, self.signals, self.new = nc, ins, ctx, {}, []
        sb = self.keep
        self.x = sb("x_res", [P, NT, D], FP32)
        self.xl = sb("x_norm", [P, NT, D], FP32)
        self.heads_out = sb("heads_out", [P, B * NG, TB, D // NG], FP32)
        self.ident = sb("ident", [P, P], FP32)
        self.identb = sb("identb", [P, P], BF16)
        self.mask_k = sb("mask_k", [P, P], BF16)
        self.mask_q = sb("mask_q", [P, P], BF16)
        self.ones = sb("ones_row", [1, P], FP32)
        self.half = sb("minus_half", [P, 64], FP32)
        self.one = sb("one", [P, 32], FP32)

    def keep(self, name, shape, dt):
        return self.ctx.enter_context(self.nc.sbuf_tensor(name, shape, dt))

    def new_signal(self, name, per):
        if name not in self.signals:
            self.signals[name] = Signal(self.ctx.enter_context(self.nc.semaphore(name)))
            self.new.append(self.signals[name])
        return self.signals[name].loop(per)

    def lift(self, eng):
        for s in self.new:
            eng.sem_inc(s.sem, 1)
        self.new = []


def setup(c, x_dram):
    nc = c.nc
    loaded = c.new_signal("x_loaded", 16)
    made = c.new_signal("constants_made", 1)
    with nc.Block() as block:
        @block.sync
        def _(sp):
            c.lift(sp)
            sp.dma_start(c.x[:], x_dram.rearrange("(t p) d -> p t d", p=P)).then_inc(loaded.sem, 16)
            sp.wait_ge(loaded.sem, loaded.base + 16)

        @block.gpsimd
        def _(pool):
            for n, m in enumerate((c.ident, c.identb, c.mask_k, c.mask_q)):
                pool.memset(m[:], 0.0).then_inc(made.sem, 1)
            pool.memset(c.ones[:], 1.0).then_inc(made.sem, 1)
            pool.memset(c.half[:], -0.5).then_inc(made.sem, 1)
            pool.memset(c.one[:], 1.0).then_inc(made.sem, 1)
            pool.wait_ge(made.sem, made.base + 7)
            for m in (c.ident, c.identb):
                pool.affine_select(out=m[:], in_=m[:], compare_op=ALU.not_equal, fill=1.0, base=0,
                                   pattern=[[-1, P]], channel_multiplier=1).then_inc(made.sem, 1)
            pool.affine_select(out=c.mask_k[:], in_=c.mask_k[:], compare_op=ALU.is_ge, fill=NEG, base=0,
                               pattern=[[-1, P]], channel_multiplier=1).then_inc(made.sem, 1)
            pool.affine_select(out=c.mask_q[:], in_=c.mask_q[:], compare_op=ALU.is_ge, fill=NEG, base=0,
                               pattern=[[1, P]], channel_multiplier=-1).then_inc(made.sem, 1)
            pool.wait_ge(made.sem, made.base + 11)


def store_out(c, out_dram):
    nc = c.nc
    stored = c.new_signal("x_stored", 16)
    with nc.Block() as block:
        @block.sync
        def _(sp):
            c.lift(sp)
            sp.dma_start(out_dram.rearrange("(t p) d -> p t d", p=P), c.x[:]).then_inc(stored.sem, 16)
            sp.wait_ge(stored.sem, stored.base + 16)


def project(c, kind, scr):
    nc, ins = c.nc, c.ins
    low = kind == "low_rank"
    units = [(g, op) for g in range(NG if low else 1) for op in range(2)]
    NU = len(units)
    NCHAIN = {"mha": 4, "low_rank": 4, "rope": 6}[kind]
    scale = {"mha": 8 ** -0.5, "low_rank": 32 ** -0.5, "rope": 1.0}[kind]
    with ExitStack() as st_:
        def sb(name, shape, dt=FP32):
            return st_.enter_context(nc.sbuf_tensor(f"{name}_{kind}", shape, dt))

        def ps(name, shape, dt=FP32):
            return st_.enter_context(nc.psum_tensor(f"{name}_{kind}", shape, dt))

        wq, wk, wv = sb("wq", [P, P]), sb("wk", [P, P]), sb("wv", [P, P])
        w1 = [sb("wq1", [P, 64]), sb("wk1", [P, 64])]
        wide = [[sb(f"wide_{a}{b}", [P, NG, P]) for b in "12"] for a in "qk"]
        wvp = sb("wvp", [P, H * VC])
        vrow = sb("vrow", [1, H * VC])
        bvrow = sb("bvrow", [1, P])
        bias = sb("bias", [P, 2])
        gain = sb("gain", [P, 1])
        cs = [sb(f"table{n}", [P, S]) for n in range(4)]
        stats = sb("stats", [P, CH, 6])
        work = sb("work", [P, 9, CH])
        xn = sb("xn", [P, CH, D])
        xnT = sb("xnT", [P, CW])
        val = [sb(f"val{n}", [P, CW]) for n in range(2)]
        part = [sb(f"part{n}", [P, CW]) for n in range(2)]
        rest = [sb(f"rest{n}", [P, CW]) for n in range(2)]
        split = [sb(f"split{n}", [P, 3, CW], BF16) for n in range(2)]
        vout = [sb(f"vout{n}", [P, CH, H * VC]) for n in range(2)]
        pT = ps("pT", [P, CW])
        pA = [ps(f"pA{n}", [P, CW]) for n in range(2)]
        pB = [ps(f"pB{n}", [P, CW]) for n in range(2)]
        pV = [ps(f"pV{n}", [P, CW]) for n in range(2)]

        loaded = c.new_signal("weights_loaded", 0)
        prep = c.new_signal("weights_prepared", 0)
        chain = c.new_signal("norm_chain", NCHAIN)
        roots = Roots(c, 2 if kind == "rope" else 1)
        normed = c.new_signal("normed", 1)
        turned = c.new_signal("turned", 1)
        xT_ready = c.new_signal("xT_ready", 1)
        a_ready = c.new_signal("proj_ready", NU)
        first = c.new_signal("first_part", NU)
        vals = c.new_signal("val_ready", NU)
        dchain = c.new_signal("val_chain", NU)
        s1 = c.new_signal("split1_ready", NU)
        r1 = c.new_signal("rest_ready", NU)
        s2 = c.new_signal("split2_ready", NU)
        s3 = c.new_signal("split3_ready", NU)
        stored = [c.new_signal(f"split_stored{n}", 16 * NU // 2) for n in range(2)]
        v_ready = c.new_signal("v_ready", CH)
        v_out = c.new_signal("v_copied", CH)
        v_stored = c.new_signal("v_stored", 16 * NG)
        block = st_.enter_context(nc.Block())
        lb, pb = loaded.base, prep.base

        @block.sync
        def _(sp):
            c.lift(sp)
            n = 0
            loads = [(wv, ins[f"{kind}_wv"])]
            if low:
                loads += [(w1[0], ins["low_rank_wq1"]), (w1[1], ins["low_rank_wk1"]), (wq, ins["low_rank_wq2"]),
                          (wk, ins["low_rank_wk2"])]
            else:
                loads += [(wq, ins[f"{kind}_wq"]), (wk, ins[f"{kind}_wk"])]
            if kind == "mha":
                loads += [(bias[:, 0:1], ins["mha_bq"]), (bias[:, 1:2], ins["mha_bk"]), (bvrow, ins["mha_bv"])]
            if kind == "rope":
                loads += [(gain, ins["rope_g"])] + [(cs[t], ins[f"rope_table{t}"]) for t in range(4)]
            for dst, src in loads:
                sp.dma_start(dst[:], src).then_inc(loaded.sem, 16)
                n += 16
            assert n == 16 * len(loads)
            with sp.Fori(0, B) as b:
                for half in range(HALVES):
                    i = b * HALVES + half
                    for u, (g, op) in enumerate(units):
                        sp.wait_ge(s3.sem, s3.at(i, u + 1))
                        r = (b * NG + g) * P if low else b * P
                        sp.dma_start(scr[kind][op, bass.ds(r, P), :, half * CW:(half + 1) * CW],
                                     split[u % 2][:]).then_inc(stored[u % 2].sem, 16)
                    sp.wait_ge(v_out.sem, v_out.at(i, CH))
                    for g in range(NG):
                        sp.dma_start(scr["v"][bass.ds((b * NG + g) * S + half * CW, CW), :].rearrange("(t p) n -> p t n", p=P),
                                     vout[half][:, :, g * HG * VC:(g + 1) * HG * VC]).then_inc(v_stored.sem, 16)
            for n in range(2):
                sp.wait_ge(stored[n].sem, stored[n].at(NC_, 0))
            sp.wait_ge(v_stored.sem, v_stored.at(NC_, 0))

        n_loads = {"mha": 6, "low_rank": 5, "rope": 8}[kind]

        @block.gpsimd
        def _(pool):
            pool.memset(wvp[:], 0.0).then_inc(prep.sem, 1)
            pool.memset(vrow[:], 0.0).then_inc(prep.sem, 1)
            pool.wait_ge(loaded.sem, lb + 16 * n_loads)
            pool.wait_ge(prep.sem, pb + 2)
            pool.tensor_copy(wvp[:].rearrange("p (h c) -> p h c", c=VC)[:, :, 0:8],
                             wv[:].rearrange("p (h c) -> p h c", c=8)).then_inc(prep.sem, 1)
            vr = vrow[:].rearrange("p (h c) -> p h c", c=VC)
            pool.memset(vr[:, :, 8:9], 1.0).then_inc(prep.sem, 1)
            if kind == "mha":
                pool.tensor_copy(vr[:, :, 0:8], bvrow[:].rearrange("p (h c) -> p h c", c=8)).then_inc(prep.sem, 1)
                pool.tensor_scalar(bias[:, 0:1], bias[:, 0:1], scale, None, ALU.mult).then_inc(prep.sem, 1)
            if low:
                for op in range(2):
                    for g in range(NG):
                        pool.tensor_copy(wide[op][0][:, g, :].rearrange("p (h r s) -> p h r s", r=4, s=8),
                                         w1[op][:, g * 16:g * 16 + 16].rearrange("p (h r) -> p h r", r=4).unsqueeze(3)
                                         .broadcast_to([P, HG, 4, 8])).then_inc(prep.sem, 1)
                        pool.tensor_copy(wide[op][1][:, g, :].rearrange("p (h r s) -> p h r s", r=4, s=8),
                                         (wq, wk)[op][:, g * 32:g * 32 + 32].rearrange("p (h s) -> p h s", s=8)
                                         .unsqueeze(2).broadcast_to([P, HG, 4, 8])).then_inc(prep.sem, 1)
            if kind == "rope":
                for op in range(2):
                    src = (wq, wk)[op][:].rearrange("p (h a d) -> p h a d", a=2, d=4)
                    dst = wide[0][op][:, 0, :].rearrange("p (h a d) -> p h a d", a=2, d=4)
                    pool.tensor_scalar(dst[:, :, 0, :], src[:, :, 1, :], -1.0, None, ALU.mult).then_inc(prep.sem, 1)
                    pool.tensor_copy(dst[:, :, 1, :], src[:, :, 0, :]).then_inc(prep.sem, 1)
            with pool.Fori(0, NC_) as i:
                roots.give(pool, c, i, 1, work[:, 6, :])
                if kind == "rope":
                    roots.give(pool, c, i, 2, work[:, 8, :])

        n_prep = {"mha": 6, "low_rank": 4 + 16, "rope": 4 + 4}[kind]

        @block.vector
        def _(dve):
            dve.wait_ge(loaded.sem, lb + 16 * n_loads)
            dve.wait_ge(prep.sem, pb + n_prep)
            with dve.Fori(0, B) as b:
                for half in range(HALVES):
                    i = b * HALVES + half
                    ch = Chain(dve, chain, i)
                    for t in range(CH):
                        ins_ = dve.bn_stats(stats[:, t, :], c.x[:, i * CH + t, :])
                    ch.link(ins_)
                    row_stats(dve, ch, stats, work, CH)
                    roots.count = 0
                    ask_root(dve, ch, roots, work[:, 6, :], work[:, 1, :], EPS_LN)
                    dve.wait_ge(turned.sem, turned.at(i, 0))
                    if kind == "rope":
                        for t in range(CH):
                            ins_ = dve.tensor_scalar(c.xl[:, i * CH + t, :], c.x[:, i * CH + t, :], work[:, 0, t:t + 1],
                                                     work[:, 6, t:t + 1], ALU.subtract, ALU.mult)
                        ch.link(dve.scalar_tensor_tensor(out=work[:, 7, :], in0=work[:, 6, :], scalar=1.0,
                                                         in1=work[:, 6, :], op0=ALU.mult, op1=ALU.mult))
                        ch.wait()
                        ch.link(dve.tensor_tensor(work[:, 7, :], work[:, 7, :], work[:, 1, :], ALU.mult))
                        ask_root(dve, ch, roots, work[:, 8, :], work[:, 7, :], EPS_RMS)
                        for t in range(CH):
                            ins_ = dve.tensor_scalar(xn[:, t, :], c.xl[:, i * CH + t, :], work[:, 8, t:t + 1], None, ALU.mult)
                    else:
                        for t in range(CH):
                            ins_ = dve.tensor_scalar(xn[:, t, :], c.x[:, i * CH + t, :], work[:, 0, t:t + 1],
                                                     work[:, 6, t:t + 1], ALU.subtract, ALU.mult)
                    ins_.then_inc(normed.sem, 1)
                    assert ch.count == NCHAIN, ch.count
                    for u, (g, op) in enumerate(units):
                        w = u % 2
                        if u >= 2:
                            dve.wait_ge(s1.sem, s1.at(i, u - 1))
                        else:
                            dve.wait_ge(s1.sem, s1.at(i, u - 1) if u else s1.at(i, 0))
                        if kind != "mha":
                            dve.wait_ge(first.sem, first.at(i, u + 1))
                            dve.wait_ge(a_ready.sem, a_ready.at(i, u + 1))
                        if kind == "mha":
                            dve.wait_ge(a_ready.sem, a_ready.at(i, u + 1))
                            dve.tensor_scalar(val[w][:], pA[w][:], (scale, 1.0)[op], bias[:, op:op + 1], ALU.mult,
                                              ALU.add).then_inc(vals.sem, 1)
                        elif low:
                            dve.tensor_tensor(val[w][:], pB[w][:], part[w][:], ALU.mult).then_inc(vals.sem, 1)
                        else:
                            dve.tensor_tensor(rest[w][:], pB[w][:], cs[2 * op + 1][:, half * CW:(half + 1) * CW],
                                              ALU.mult)
                            dve.tensor_tensor(val[w][:], part[w][:], cs[2 * op][:, half * CW:(half + 1) * CW],
                                              ALU.mult).then_inc(dchain.sem, 1)
                            dve.wait_ge(dchain.sem, dchain.at(i, u + 1))
                            dve.tensor_tensor(val[w][:], val[w][:], rest[w][:], ALU.add).then_inc(vals.sem, 1)
                        dve.wait_ge(s1.sem, s1.at(i, u + 1))
                        dve.tensor_tensor(rest[w][:], val[w][:], split[w][:, 0, :], ALU.subtract).then_inc(r1.sem, 1)
                        dve.wait_ge(s2.sem, s2.at(i, u + 1))
                        dve.tensor_tensor(split[w][:, 2, :], rest[w][:], split[w][:, 1, :], ALU.subtract).then_inc(s3.sem, 1)

        @block.tensor
        def _(pe):
            pe.wait_ge(loaded.sem, lb + 16 * n_loads)
            pe.wait_ge(prep.sem, pb + n_prep)
            with pe.Fori(0, B) as b:
                for half in range(HALVES):
                    i = b * HALVES + half
                    pe.wait_ge(normed.sem, normed.at(i, 1))
                    pe.wait_ge(xT_ready.sem, xT_ready.at(i, 0))
                    for t in range(CH):
                        ins_ = pe.transpose(pT[:, t * P:(t + 1) * P], xn[:, t, :], c.ident[:])
                    ins_.then_inc(turned.sem, 1)
                    pe.wait_ge(xT_ready.sem, xT_ready.at(i, 1))
                    for u, (g, op) in enumerate(units):
                        w = u % 2
                        pe.wait_ge(vals.sem, vals.at(i, u - 1) if u else vals.at(i, 0))
                        if low:
                            pe.matmul(pA[w][:], wide[op][0][:, g, :], xnT[:], start=True, stop=True)
                            ins_ = pe.matmul(pB[w][:], wide[op][1][:, g, :], xnT[:], start=True, stop=True)
                        elif kind == "rope":
                            pe.matmul(pA[w][:], (wq, wk)[op][:], xnT[:], start=True, stop=True)
                            ins_ = pe.matmul(pB[w][:], wide[0][op][:, 0, :], xnT[:], start=True, stop=True)
                        else:
                            ins_ = pe.matmul(pA[w][:], (wq, wk)[op][:], xnT[:], start=True, stop=True)
                        ins_.then_inc(a_ready.sem, 1)
                    for t in range(CH):
                        pe.wait_ge(v_out.sem, v_out.at(i, t - 1) if t else v_out.at(i, 0))
                        pe.matmul(pV[t % 2][:], xnT[:, t * P:(t + 1) * P], wvp[:], start=True, stop=False)
                        pe.matmul(pV[t % 2][:], c.ones[:], vrow[:], start=False, stop=True).then_inc(v_ready.sem, 1)

        @block.scalar
        def _(act):
            act.wait_ge(loaded.sem, lb + 16 * n_loads)
            with act.Fori(0, B) as b:
                for half in range(HALVES):
                    i = b * HALVES + half
                    act.wait_ge(turned.sem, turned.at(i, 1))
                    act.wait_ge(v_ready.sem, v_ready.at(i, 0))
                    act.activation(xnT[:], pT[:], ACT.Copy, scale=gain[:] if kind == "rope" else 1.0).then_inc(xT_ready.sem, 1)
                    for u, (g, op) in enumerate(units):
                        w = u % 2
                        if kind != "mha":
                            act.wait_ge(a_ready.sem, a_ready.at(i, u + 1))
                            act.wait_ge(vals.sem, vals.at(i, u - 1) if u else vals.at(i, 0))
                            act.activation(part[w][:], pA[w][:], ACT.Copy,
                                           scale=scale if op == 0 else 1.0).then_inc(first.sem, 1)
                        act.wait_ge(vals.sem, vals.at(i, u + 1))
                        act.wait_ge(stored[w].sem, stored[w].at(i, 16 * (u // 2)))
                        act.activation(split[w][:, 0, :], val[w][:], ACT.Copy).then_inc(s1.sem, 1)
                        act.wait_ge(r1.sem, r1.at(i, u + 1))
                        act.activation(split[w][:, 1, :], rest[w][:], ACT.Copy).then_inc(s2.sem, 1)
                    act.wait_ge(v_stored.sem, v_stored.at(i, 0))
                    for t in range(CH):
                        act.wait_ge(v_ready.sem, v_ready.at(i, t + 1))
                        act.activation(vout[half][:, t, :], pV[t % 2][:], ACT.Copy).then_inc(v_out.sem, 1)

        loaded.base += 16 * n_loads
        prep.base += n_prep
        for s in (chain, normed, turned, xT_ready, a_ready, vals, s1, r1, s2, s3, *stored, v_ready, v_out, v_stored):
            s.end(NC_)
        roots.end(NC_)
        if kind != "mha":
            first.end(NC_)
        if kind == "rope":
            dchain.end(NC_)


SLOTS = ((0, 0), (0, 1), (1, 0), (1, 1), (0, 2), (2, 0))


def attend(c, kind, scr):
    nc = c.nc
    low = kind == "low_rank"
    dk = 32 if low else 8
    per = 3 if low else 6
    passes = len(SLOTS) // per
    rows = per * dk
    TURNS = B * NG
    pieces = []
    for h in range(HG):
        for qt in range(TB):
            if qt < CH:
                pieces.append((h, qt, qt, 0, (qt + 1) * P))
            else:
                pieces.append((h, qt, qt, 0, CW))
                pieces.append((h, qt + CH, qt, CW, (qt + 1) * P))
    NPIECE = len(pieces)
    steps = [(qc, kt, hp) for qc in range(HALVES) for kt in range(CH * (qc + 1)) for hp in range(HG // 2)]
    NS = len(steps)
    START, AHEAD = 4, 3
    LAST0 = 2 * CH - 1
    TURN0 = LAST0 + 3
    PEAK = START + NPIECE // AHEAD
    with ExitStack() as st_:
        def sb(name, shape, dt=FP32):
            return st_.enter_context(nc.sbuf_tensor(f"{name}_{kind}", shape, dt))

        def ps(name, shape, dt=FP32):
            return st_.enter_context(nc.psum_tensor(f"{name}_{kind}", shape, dt))

        q = [sb(f"q{n}", [rows + 2, passes, HG, S], BF16) for n in range(2)]
        k = [sb(f"k{n}", [rows + 2, passes, HG, S], BF16) for n in range(2)]
        v = [sb(f"v{n}", [P, TB, HG * VC]) for n in range(2)]
        peaks = sb("peaks", [P, HG, TB + CH])
        peak = sb("peak", [P, HG, TB])
        npk = sb("npk", [P, 4, HG * TB], BF16)
        npkT = sb("npkT", [2 * HG * TB, P], BF16)
        prob = [sb(f"prob{n}", [P, 2, CW]) for n in range(2)]
        outT = [sb(f"outT{n}", [P, CW]) for n in range(2)]
        rec = sb("rec", [P, CH, HG])
        s1 = [ps(f"s1_{n}", [P, CW]) for n in range(2)]
        s2 = [ps(f"s2_{n}", [P, 2, CW]) for n in range(2)]
        o = ps("o", [P, CW])
        m = ps("m", [P, CH, HG * VC])
        mb = m[:].rearrange("p a b -> p (a b)").bitcast(BF16)[:, 0:P]

        ones_set = c.new_signal("ones_set", 0)
        NL = 16 * (2 * len(SLOTS) + 1)
        loaded = [c.new_signal(f"stack_loaded{n}", NL) for n in range(2)]
        peak_in = [c.new_signal(f"peak_rows{n}", 32) for n in range(2)]
        scored = c.new_signal("scored", NPIECE)
        peaked = c.new_signal("peaked", NPIECE)
        pchain = c.new_signal("peak_chain", 2)
        negated = c.new_signal("negated", 1)
        peak_T = c.new_signal("peak_turned", 1)
        peak_c = c.new_signal("peak_copied", 1)
        s_ready = c.new_signal("s_ready", NS)
        exped = c.new_signal("exped", NS)
        pv = c.new_signal("pv_done", NS)
        o_copied = c.new_signal("o_copied", HALVES)
        o_turned = c.new_signal("o_turned", HALVES)
        rchain = c.new_signal("rec_chain", HALVES)
        o_out = c.new_signal("o_normalized", HALVES)
        block = st_.enter_context(nc.Block())
        ones_base = ones_set.base

        def turns(eng, ahead, body):
            ahead(0, 0, 0)
            with eng.Fori(0, TURNS // 2 - 1) as i:
                for w in range(2):
                    body(2 * i + w, w, i, True)
            body(TURNS - 2, 0, TURNS // 2 - 1, True)
            body(TURNS - 1, 1, TURNS // 2 - 1, False)

        def next_set(w, idx):
            return 1 - w, idx + w

        @block.sync
        def _(sp):
            c.lift(sp)
            sp.wait_ge(ones_set.sem, ones_base + 5)

            def load(n, w):
                for op, dst in ((0, q[w]), (1, k[w])):
                    for sl, parts in enumerate(SLOTS):
                        src = scr[kind][op, bass.ds(n * HG * dk, HG * dk), parts[op], :].rearrange("(h d) t -> d h t", d=dk)
                        r = (sl % per) * dk
                        sp.dma_start(dst[r:r + dk, sl // per, :, :], src).then_inc(loaded[w].sem, 16)
                sp.dma_start(v[w][:], scr["v"][bass.ds(n * S, S), :].rearrange("(t p) n -> p t n", p=P)) \
                    .then_inc(loaded[w].sem, 16)

            def peak_rows(n, w, idx):
                sp.wait_ge(peak_c.sem, peak_c.at(n, 1))
                for part in range(2):
                    sp.dma_start(q[w][rows + part:rows + part + 1, passes - 1, :, :],
                                 npkT[part * HG * TB:(part + 1) * HG * TB, :]).then_inc(peak_in[w].sem, 16)

            def body(n, w, idx, more):
                if more:
                    w1, idx1 = next_set(w, idx)
                    if not (isinstance(n, int) and n == 0):
                        sp.wait_ge(pv.sem, pv.at(n, 0))
                        load(n + 1, w1)
                    peak_rows(n + 1, w1, idx1)

            load(0, 0)
            turns(sp, peak_rows, body)
            for w in range(2):
                sp.wait_ge(peak_in[w].sem, peak_in[w].at(TURNS // 2, 0))

        @block.gpsimd
        def _(pool):
            pool.memset(npk[:], 0.0).then_inc(ones_set.sem, 1)
            for w in range(2):
                pool.memset(k[w][:], 1.0).then_inc(ones_set.sem, 1)
                pool.memset(q[w][:], 0.0).then_inc(ones_set.sem, 1)

        @block.tensor
        def _(pe):
            def piece(n, w, idx, j):
                h, place, qt, k0, k1 = pieces[j]
                if j == 0:
                    pe.wait_ge(loaded[w].sem, loaded[w].at(idx, NL))
                pe.wait_ge(peaked.sem, peaked.at(n, max(j - 1, 0)))
                diag = k1 == (qt + 1) * P
                dst = s1[j % 2]
                for r in range(passes):
                    ins_ = pe.matmul(dst[:, 0:k1 - k0], q[w][0:rows, r, h, qt * P:(qt + 1) * P], k[w][0:rows, r, h, k0:k1],
                                     start=r == 0, stop=r == passes - 1 and not diag)
                if diag:
                    ins_ = pe.matmul(dst[:, k1 - k0 - P:k1 - k0], c.identb[:], c.mask_k[:], start=False, stop=True)
                ins_.then_inc(scored.sem, 1)

            def turn_peaks(n):
                pe.wait_ge(negated.sem, negated.at(n, 1))
                pe.transpose(mb, npk[:].rearrange("p a b -> p (a b)"), c.identb[:]).then_inc(peak_T.sem, 1)

            def ahead(n, w, idx):
                for j in range(NPIECE):
                    piece(n, w, idx, j)
                turn_peaks(n)

            def score(n, w, idx, s):
                qc, kt, hp = steps[s]
                if s == 0:
                    pe.wait_ge(peak_in[w].sem, peak_in[w].at(idx, 32))
                pe.wait_ge(exped.sem, exped.at(n, max(s - 1, 0)))
                off = max(kt * P - qc * CW, 0)
                diag = kt >= qc * CH
                for j in range(2):
                    h = 2 * hp + j
                    for r in range(passes):
                        kr = rows + 2 if r == passes - 1 else rows
                        ins_ = pe.matmul(s2[s % 2][:, j, off:CW], k[w][0:kr, r, h, kt * P:(kt + 1) * P],
                                         q[w][0:kr, r, h, qc * CW + off:(qc + 1) * CW], start=r == 0,
                                         stop=r == passes - 1 and not diag)
                    if diag:
                        ins_ = pe.matmul(s2[s % 2][:, j, off:off + P], c.identb[:], c.mask_q[:], start=False, stop=True)
                ins_.then_inc(s_ready.sem, 1)

            def mix(n, w, s):
                qc, kt, hp = steps[s]
                off = max(kt * P - qc * CW, 0)
                pe.wait_ge(exped.sem, exped.at(n, s + 1))
                if kt == 0 and hp == 0:
                    pe.wait_ge(o_copied.sem, o_copied.at(n, qc))
                for j in range(2):
                    h = 2 * hp + j
                    ins_ = pe.matmul(o[h * VC:(h + 1) * VC, off:CW], v[w][:, kt, h * VC:(h + 1) * VC],
                                     prob[s % 2][:, j, off:CW], start=kt == 0, stop=kt == CH * (qc + 1) - 1)
                ins_.then_inc(pv.sem, 1)

            def turn_out(n, qc, more):
                pe.wait_ge(o_copied.sem, o_copied.at(n, qc + 1))
                pe.wait_ge(o_out.sem, o_out.at(n, qc))
                if more:
                    pe.wait_ge(peak_c.sem, peak_c.at(n, 1 + qc))
                for t in range(CH):
                    ins_ = pe.transpose(m[:, t, :], outT[qc][:, t * P:(t + 1) * P], c.ident[:])
                ins_.then_inc(o_turned.sem, 1)

            def body(n, w, idx, more):
                w1, idx1 = next_set(w, idx)
                for s in range(NS):
                    if more and START <= s < PEAK:
                        for j in range((s - START) * AHEAD, (s - START + 1) * AHEAD):
                            piece(n + 1, w1, idx1, j)
                    score(n, w, idx, s)
                    if s:
                        mix(n, w, s - 1)
                    if s == TURN0:
                        turn_out(n, 0, more)
                    if s == PEAK and more:
                        pe.wait_ge(o_out.sem, o_out.at(n, 1))
                        turn_peaks(n + 1)
                mix(n, w, NS - 1)
                turn_out(n, 1, more)

            turns(pe, ahead, body)

        @block.vector
        def _(dve):
            def piece(n, j):
                h, place, qt, k0, k1 = pieces[j]
                if j == 0:
                    dve.wait_ge(negated.sem, negated.at(n, 0))
                dve.wait_ge(scored.sem, scored.at(n, j + 1))
                dve.reduce_max(peaks[:, h, place:place + 1], s1[j % 2][:, 0:k1 - k0], AX.X).then_inc(peaked.sem, 1)

            def negate(n):
                ch = Chain(dve, pchain, n)
                dve.wait_ge(peaked.sem, peaked.at(n, NPIECE))
                dve.tensor_copy(peak[:, :, 0:CH], peaks[:, :, 0:CH])
                ch.link(dve.tensor_tensor(peak[:, :, CH:TB], peaks[:, :, CH:TB], peaks[:, :, TB:TB + CH], ALU.max))
                ch.wait()
                dve.wait_ge(ones_set.sem, ones_base + 5)
                dve.wait_ge(peak_T.sem, peak_T.at(n, 0))
                ch.link(dve.tensor_scalar(npk[:, 0, :], peak[:].rearrange("p h t -> p (h t)"), -1.0, None, ALU.mult))
                ch.wait()
                dve.scalar_tensor_tensor(out=npk[:, 1, :], in0=peak[:].rearrange("p h t -> p (h t)"), scalar=-1.0,
                                         in1=npk[:, 0, :], op0=ALU.mult, op1=ALU.subtract).then_inc(negated.sem, 1)

            def ahead(n, w, idx):
                for j in range(NPIECE):
                    piece(n, j)
                negate(n)

            def normalize(n, qc):
                dve.wait_ge(o_turned.sem, o_turned.at(n, qc + 1))
                mv = m[:].rearrange("p t (h c) -> p t h c", c=VC)
                dve.reciprocal(rec[:], mv[:, :, :, 8]).then_inc(rchain.sem, 1)
                dve.wait_ge(rchain.sem, rchain.at(n, qc + 1))
                dve.tensor_tensor(c.heads_out[:, n, qc * CH:(qc + 1) * CH, :].rearrange("p t (h d) -> p t h d", h=HG),
                                  mv[:, :, :, 0:8], rec[:].unsqueeze(3).broadcast_to([P, CH, HG, 8]), ALU.mult) \
                    .then_inc(o_out.sem, 1)

            def body(n, w, idx, more):
                for s in range(NS):
                    if more and START <= s < PEAK:
                        for j in range((s - START) * AHEAD, (s - START + 1) * AHEAD):
                            piece(n + 1, j)
                    if s == TURN0:
                        normalize(n, 0)
                    if s == PEAK and more:
                        negate(n + 1)
                normalize(n, 1)

            turns(dve, ahead, body)

        @block.scalar
        def _(act):
            def copy_peaks(n, w):
                act.wait_ge(peak_T.sem, peak_T.at(n, 1))
                act.activation(npkT[:], mb[0:2 * HG * TB, :], ACT.Copy).then_inc(peak_c.sem, 1)

            def ahead(n, w, idx):
                copy_peaks(n, w)

            def copy_out(n, qc):
                act.wait_ge(pv.sem, pv.at(n, LAST0 + 1 if qc == 0 else NS))
                act.wait_ge(o_turned.sem, o_turned.at(n, qc))
                act.activation(outT[qc][:], o[:], ACT.Copy).then_inc(o_copied.sem, 1)

            def body(n, w, idx, more):
                for s in range(NS):
                    qc, kt, hp = steps[s]
                    off = max(kt * P - qc * CW, 0)
                    act.wait_ge(s_ready.sem, s_ready.at(n, s + 1))
                    act.wait_ge(pv.sem, pv.at(n, max(s - 1, 0)))
                    act.activation(prob[s % 2][:, :, off:CW], s2[s % 2][:, :, off:CW], ACT.Exp).then_inc(exped.sem, 1)
                    if s == LAST0 + 1:
                        copy_out(n, 0)
                    if s == PEAK and more:
                        act.wait_ge(peak_in[w].sem, peak_in[w].at(idx, 32))
                        copy_peaks(n + 1, w)
                copy_out(n, 1)

            act.preload_act_table(ACT.Exp)
            turns(act, ahead, body)

        ones_set.base += 5
        for w in range(2):
            loaded[w].end(TURNS // 2)
            peak_in[w].end(TURNS // 2)
        for s in (scored, peaked, pchain, negated, peak_T, peak_c, s_ready, exped, pv, o_copied, o_turned, rchain, o_out):
            s.end(TURNS)


def post(c, kind):
    nc, ins = c.nc, c.ins
    NCHAIN = 5
    last = kind == "rope"
    with ExitStack() as st_:
        def sb(name, shape, dt=FP32):
            return st_.enter_context(nc.sbuf_tensor(f"{name}_post_{kind}", shape, dt))

        def ps(name, shape, dt=FP32):
            return st_.enter_context(nc.psum_tensor(f"{name}_post_{kind}", shape, dt))

        wo = sb("wo", [P, D])
        bo = sb("bo", [1, D])
        hs = sb("hs", [P, CH, D])
        hT = sb("hT", [P, CW])
        y = sb("y", [P, CH, D])
        stats = sb("stats", [P, CH, 6])
        work = sb("work", [P, 9, CH])
        pT = ps("pT", [P, CW])
        pO = [ps(f"pO{n}", [P, CH, D]) for n in range(2)]
        loaded = c.new_signal("wo_loaded", 0)
        zeroed = c.new_signal("bo_zeroed", 0)
        lb, zb = loaded.base, zeroed.base
        gathered = c.new_signal("heads_gathered", 1)
        turned = c.new_signal("heads_turned", 1)
        hT_ready = c.new_signal("hT_ready", 1)
        wo_done = c.new_signal("wo_done", 1)
        chain = c.new_signal("post_chain", NCHAIN)
        roots = Roots(c, 1)
        added = c.new_signal("post_added", 1)
        block = st_.enter_context(nc.Block())

        @block.sync
        def _(sp):
            c.lift(sp)
            sp.dma_start(wo[:], ins[f"{kind}_wo"]).then_inc(loaded.sem, 16)
            if not last:
                sp.dma_start(bo[:], ins[f"{kind}_bo"]).then_inc(loaded.sem, 16)

        nl = 16 if last else 32

        if not last:
            @block.gpsimd
            def _(pool):
                with pool.Fori(0, NC_) as i:
                    roots.give(pool, c, i, 1, work[:, 6, :])

        @block.scalar
        def _(act):
            with act.Fori(0, B) as b:
                for half in range(HALVES):
                    i = b * HALVES + half
                    act.wait_ge(turned.sem, turned.at(i, 0))
                    act.activation(hs[:].rearrange("p t (g d) -> p g t d", g=NG),
                                   c.heads_out[:, bass.ds(b * NG, NG), half * CH:(half + 1) * CH, :], ACT.Copy) \
                        .then_inc(gathered.sem, 1)
                    act.wait_ge(turned.sem, turned.at(i, 1))
                    act.wait_ge(wo_done.sem, wo_done.at(i, 0))
                    act.activation(hT[:], pT[:], ACT.Copy).then_inc(hT_ready.sem, 1)

        @block.tensor
        def _(pe):
            pe.wait_ge(loaded.sem, lb + nl)
            with pe.Fori(0, B) as b:
                for half in range(HALVES):
                    i = b * HALVES + half
                    pe.wait_ge(gathered.sem, gathered.at(i, 1))
                    pe.wait_ge(hT_ready.sem, hT_ready.at(i, 0))
                    for t in range(CH):
                        ins_ = pe.transpose(pT[:, t * P:(t + 1) * P], hs[:, t, :], c.ident[:])
                    ins_.then_inc(turned.sem, 1)
                    pe.wait_ge(hT_ready.sem, hT_ready.at(i, 1))
                    pe.wait_ge(added.sem, added.at(i, 0))
                    for t in range(CH):
                        ins_ = pe.matmul(pO[half][:, t, :], hT[:, t * P:(t + 1) * P], wo[:], start=True, stop=last)
                        if not last:
                            ins_ = pe.matmul(pO[half][:, t, :], c.ones[:], bo[:], start=False, stop=True)
                    ins_.then_inc(wo_done.sem, 1)

        @block.vector
        def _(dve):
            with dve.Fori(0, B) as b:
                for half in range(HALVES):
                    i = b * HALVES + half
                    dve.wait_ge(wo_done.sem, wo_done.at(i, 1))
                    if last:
                        xl = c.xl[:, bass.ds(i * CH, CH), :]
                        dve.tensor_tensor(xl, pO[half][:], xl, ALU.add).then_inc(added.sem, 1)
                        continue
                    layernorm_add(dve, Chain(dve, chain, i), roots, pO[half], y, stats, work, c.x, i, added)

        loaded.base += nl
        for s in (gathered, turned, hT_ready, wo_done, added):
            s.end(NC_)
        if not last:
            chain.end(NC_)
            roots.end(NC_)


def layernorm_add(dve, ch, roots, src, y, stats, work, x, i, added, more=False):
    for t in range(CH):
        ins_ = dve.bn_stats(stats[:, t, :], src[:, t, :])
    ch.link(ins_)
    row_stats(dve, ch, stats, work, CH)
    if not more:
        roots.count = 0
    ask_root(dve, ch, roots, work[:, 6, :], work[:, 1, :], EPS_LN)
    for t in range(CH):
        ins_ = dve.tensor_scalar(y[:, t, :], src[:, t, :], work[:, 0, t:t + 1], work[:, 6, t:t + 1], ALU.subtract, ALU.mult)
    ch.link(ins_)
    ch.wait()
    rows = x[:, bass.ds(i * CH, CH), :]
    dve.tensor_tensor(rows, rows, y[:], ALU.add).then_inc(added.sem, 1)


DEPTH = 6
WIN = 32
NWT = P // WIN
DH = 64
HP = H // 2
NF = 3
QKC = 4


def enter_local(c, xw):
    nc = c.nc
    with ExitStack() as st_:
        def sb(name, shape, dt=FP32):
            return st_.enter_context(nc.sbuf_tensor(f"{name}_enter", shape, dt))

        stats, work = sb("stats", [P, CH, 6]), sb("work", [P, 9, CH])
        chain, roots = c.new_signal("enter_chain", 4), Roots(c, 1)
        block = st_.enter_context(nc.Block())

        @block.gpsimd
        def _(pool):
            c.lift(pool)
            with pool.Fori(0, NC_) as i:
                roots.give(pool, c, i, 1, work[:, 6, :])

        @block.vector
        def _(dve):
            with dve.Fori(0, B) as b:
                for half in range(HALVES):
                    i = b * HALVES + half
                    ch = Chain(dve, chain, i)
                    for t in range(CH):
                        ins_ = dve.bn_stats(stats[:, t, :], c.x[:, i * CH + t, :])
                    ch.link(ins_)
                    row_stats(dve, ch, stats, work, CH)
                    roots.count = 0
                    ask_root(dve, ch, roots, work[:, 6, :], work[:, 1, :], EPS_LN)
                    for t in range(CH):
                        dve.tensor_scalar(xw[:, b * (TB + 1) + (1 + half * CH + t), :], c.x[:, i * CH + t, :],
                                          work[:, 0, t:t + 1], work[:, 6, t:t + 1], ALU.subtract, ALU.mult)

        chain.end(NC_)
        roots.end(NC_)


def leave_local(c, xw):
    nc = c.nc
    with ExitStack() as st_:
        def sb(name, shape, dt=FP32):
            return st_.enter_context(nc.sbuf_tensor(f"{name}_leave", shape, dt))

        stats, work, y = sb("stats", [P, CH, 6]), sb("work", [P, 9, CH]), sb("y", [P, CH, D])
        chain, roots, added = c.new_signal("leave_chain", 5), Roots(c, 1), c.new_signal("leave_added", 1)
        block = st_.enter_context(nc.Block())

        @block.gpsimd
        def _(pool):
            c.lift(pool)
            with pool.Fori(0, NC_) as i:
                roots.give(pool, c, i, 1, work[:, 6, :])

        @block.vector
        def _(dve):
            with dve.Fori(0, B) as b:
                for half in range(HALVES):
                    i = b * HALVES + half
                    layernorm_add(dve, Chain(dve, chain, i), roots, xw[:, bass.ds(b * (TB + 1) + (1 + half * CH), CH), :], y,
                                  stats, work, c.x, i, added)

        chain.end(NC_)
        roots.end(NC_)
        added.end(NC_)


def local_stack(c, xw, x1w):
    nc, ins = c.nc, c.ins
    with ExitStack() as st_:
        def sb(name, shape, dt=FP32):
            return st_.enter_context(nc.sbuf_tensor(f"{name}_local", shape, dt))

        def ps(name, shape, dt=FP32):
            return st_.enter_context(nc.psum_tensor(f"{name}_local", shape, dt))

        wqkv = sb("wqkv", [P, 3 * H * DH])
        wo = sb("wo", [P, HP, D])
        w1 = sb("w1", [P, 2, NF * P])
        w2 = sb("w2", [P, NF, D])
        b1 = sb("b1", [P, 2, NF])
        b2 = sb("b2", [1, D])
        gain, shift_ = sb("gain", [P, 1]), sb("shift", [P, 1])
        qks = sb("qks", [P, 2, DH])
        base = [sb(f"base{n}", [P, TB, DH]) for n in range(4)]
        tab = sb("tab", [P, TB, 5, DH])
        cur = sb("cur", [P, 5, DH])
        mask = sb("mask", [P, TB, DH], BF16)
        down1 = sb("down1", [P, P])
        last1 = sb("last1", [P, P])
        xin = sb("xin", [P, 2, D])
        xsT = sb("xsT", [P, WIN + P])
        raw = sb("raw", [P, QKC, CW])
        sq = sb("sq", [P, QKC, CW])
        rot = sb("rot", [P, QKC, CW])
        qk = sb("qk", [P, QKC, CW])
        ssq = sb("ssq", [P, 2 * H])
        inv = sb("inv", [P, 2 * H])
        qT = sb("qT", [P, HP, P])
        kT = sb("kT", [P, HP, WIN + P])
        pr = sb("pr", [P, HP, 2, DH])
        mx, tot = sb("mx", [P, H]), sb("tot", [P, H])
        PT = sb("PT", [P, HP, P])
        v2 = sb("v2", [P, NWT, HP * DH])
        att = sb("att", [P, H * DH])
        aoT = sb("aoT", [P, HP, P])
        xs1, xn1, xnT = sb("xs1", [P, 1, D]), sb("xn1", [P, D]), sb("xnT", [P, P])
        stats, work = sb("stats", [P, 1, 6]), sb("work", [P, 9, 1])
        gl, hid = sb("gl", [P, NF, P]), sb("hid", [P, NF, P])
        turn_table = sb("turn_table", [1, 1])
        pA = [ps(f"pA{n}", [P, CW]) for n in range(2)]
        pS = ps("pS", [P, 2, HP, DH])
        xs_in = pS[:, 0].rearrange("p b d -> p (b d)")[:, 0:P]
        pT = [ps(f"pT{n}", [P, CH, P]) for n in range(2)]
        pC = [ps(f"pC{n}", [P, CH, P]) for n in range(2)]

        G = lambda n, k=1: c.new_signal(n, k)
        base_in, made = G("local_tables", 0), G("local_made", 0)
        NWL = 16 * 10
        wts, tabs = G("layer_weights", NWL), G("layer_tables", 6)
        xin_ready, xs_built, xtail, xsT_ready = G("xin_ready"), G("xs_built"), G("xtail"), G("xsT_ready")
        qk_done, raw_ready, sq_ready, rot_ready = G("qk_done", QKC), G("raw_ready", QKC), G("sq_ready", QKC), G("rot_ready", QKC)
        cur_ready = G("cur_ready")
        u_ready, added_rot, summed = G("u_ready", QKC), G("rot_added", 1), G("ssq_summed", 2)
        qroots, qk_ready = Roots2(c, "qk_root"), G("qk_ready")
        t_done, t_copied, ktail = G("qkT_done", 4), G("qkT_copied", 4), G("ktail")
        s_done, mxd, sub_ready, exp_ready, totd, inv_ready = (G("ls_done"), G("ls_max", 2), G("ls_sub", 2), G("ls_exp", 2), G("ls_sum"),
                                                              G("ls_inv"))
        PT_done, PT_ready, pv_done, att_ready = G("PT_done", 2), G("PT_ready", 2), G("lpv_done"), G("att_ready")
        aT_done, aoT_ready = G("attT_done", 2), G("aoT_ready", 2)
        v_done, v_ready = G("v2_done", NWT), G("v2_ready", NWT)
        wo_done, x1_ready, sh_done, n_ready, nT_done, xnT_ready = (G("lwo_done"), G("x1_ready"), G("shifted"), G("n_ready"),
                                                                   G("nT_done"), G("lxnT_ready"))
        cchain, croots = G("ffn_chain", 5), Roots2(c, "ffn_root")
        w1_done, gl_ready, h_ready, w2_done, x2_done = G("w1_done"), G("gelu_ready"), G("hidden_ready"), G("w2_done"), G("x2_done")
        block = st_.enter_context(nc.Block())
        mb = made.base

        def layers(eng, start, body):
            with eng.Fori(0, DEPTH) as L:
                start(L)
                n = L * NT
                body(n, 0, None, None)
                body(n, 1, 0, None)
                with eng.Fori(2, NT - 1) as t:
                    body(n, t, t - 1, t - 2)
                body(n, NT - 1, NT - 2, NT - 3)
                body(n, None, NT - 1, NT - 2)
                body(n, None, None, NT - 1)

        def row(t):
            return t + t // TB + 1

        def wait_layer(eng, L):
            eng.wait_ge(wts.sem, wts.at(L, NWL))

        @block.sync
        def _(sp):
            c.lift(sp)
            for n in range(4):
                sp.dma_start(base[n][:], ins[f"local_table{n}"].rearrange("(t p) d -> p t d", p=P)).then_inc(base_in.sem, 16)
            sp.wait_ge(base_in.sem, base_in.base + 64)
            with sp.Fori(0, DEPTH) as L:
                sp.wait_ge(x2_done.sem, x2_done.at(L * NT, 0))
                one = bass.ds(L, 1)
                for dst, src in ((wqkv[:], ins["local_wqkv"][one].rearrange("o p n -> (o p) n")),
                                 (wo[:], ins["local_wo"][one].rearrange("o (c p) n -> p (o c) n", p=P)),
                                 (w1[:], ins["local_w1"][one].rearrange("o p a n -> (o p) a n")),
                                 (w2[:], ins["local_w2"][one].rearrange("o (c p) n -> p (o c) n", p=P)),
                                 (b1[:], ins["local_b1"][one].rearrange("o p a n -> (o p) a n")),
                                 (b2[:], ins["local_b2"][one]),
                                 (gain[:], ins["local_g"][one].rearrange("o p n -> (o p) n")),
                                 (shift_[:], ins["local_b"][one].rearrange("o p n -> (o p) n")),
                                 (qks[:, 0, :], ins["local_qs"][one].broadcast_to([P, DH])),
                                 (qks[:, 1, :], ins["local_ks"][one].broadcast_to([P, DH]))):
                    sp.dma_start(dst, src).then_inc(wts.sem, 16)

        @block.gpsimd
        def _(pool):
            pool.memset(mask[:], 0.0).then_inc(made.sem, 1)
            for m in (down1, last1):
                pool.memset(m[:], 0.0).then_inc(made.sem, 1)
            pool.memset(xsT[:], 0.0).then_inc(made.sem, 1)
            pool.memset(kT[:], 0.0).then_inc(made.sem, 1)
            pool.memset(tab[:, 0, 4, :], 0.0).then_inc(made.sem, 1)
            pool.memset(tab[:, 1:TB, 4, :], 1.0).then_inc(made.sem, 1)
            done = 7

            def select(m, fill, op, base_, pattern, slope):
                nonlocal done
                pool.wait_ge(made.sem, mb + done)
                pool.affine_select(out=m, in_=m, compare_op=op, fill=fill, base=base_, pattern=pattern,
                                   channel_multiplier=slope).then_inc(made.sem, 1)
                done += 1

            select(down1[:], 1.0, ALU.not_equal, 1, [[-1, P]], 1)
            select(last1[:], 1.0, ALU.not_equal, -(P - 1), [[-1, P]], 1)
            for w in range(NWT):
                part = mask[w * WIN:(w + 1) * WIN]
                select(part, NEG, ALU.is_ge, 0, [[0, TB], [1, DH]], -1)
                select(part, NEG, ALU.is_ge, WIN, [[0, TB], [-1, DH]], 1)
            pool.wait_ge(made.sem, mb + done)
            pool.memset(mask[0:WIN, 0, 0:WIN], NEG).then_inc(made.sem, 1)
            assert done == 17

            def start(L):
                pool.wait_ge(tabs.sem, tabs.at(L, 6))

            def body(n, ta, tb, tc):
                if ta is not None:
                    pool.wait_ge(v_done.sem, v_done.at(n + ta, 0))
                    pool.tensor_tensor(xsT[:, 0:WIN], xsT[:, P:P + WIN], c.one[:, 0:WIN], ALU.mult).then_inc(xtail.sem, 1)
                for j in range(QKC):
                    if ta is not None:
                        pool.wait_ge(raw_ready.sem, raw_ready.at(n + ta, j + 1))
                        if j == 0:
                            pool.wait_ge(added_rot.sem, added_rot.at(n + ta, 0))
                            pool.wait_ge(cur_ready.sem, cur_ready.at(n + ta, 1))
                        rw = raw[:, j, :].rearrange("p (h d) -> p h d", d=DH)
                        ro = rot[:, j, :].rearrange("p (h d) -> p h d", d=DH)
                        half = DH // 2
                        for a in range(2):
                            tb_ = cur[:, 2 * (j // 2) + 1, a * half:(a + 1) * half].unsqueeze(1) \
                                .broadcast_to([P, CW // DH, half])
                            ins_ = pool.tensor_tensor(ro[:, :, a * half:(a + 1) * half],
                                                      rw[:, :, (1 - a) * half:(2 - a) * half], tb_, ALU.mult)
                        ins_.then_inc(rot_ready.sem, 1)
                    if j == 0 and tc is not None:
                        croots.give(pool, c, n + tc, work[:, 6, :])
                if ta is not None:
                    qroots.give(pool, c, n + ta, inv[:])
                    pool.wait_ge(s_done.sem, s_done.at(n + ta, 0))
                    pool.tensor_tensor(kT[:, :, 0:WIN], kT[:, :, P:P + WIN],
                                       cur[:, 4, 0:WIN].unsqueeze(1).broadcast_to([P, HP, WIN]), ALU.mult).then_inc(ktail.sem, 1)

            layers(pool, start, body)

        @block.tensor
        def _(pe):
            pe.wait_ge(made.sem, mb + 18)

            def start(L):
                wait_layer(pe, L)

            def project_qk(n, t, j):
                if j == 0:
                    pe.wait_ge(xsT_ready.sem, xsT_ready.at(n + t, 1))
                    pe.wait_ge(v_ready.sem, v_ready.at(n + t, 0))
                elif j >= 2:
                    pe.wait_ge(u_ready.sem, u_ready.at(n + t, j - 1))
                    pe.wait_ge(sq_ready.sem, sq_ready.at(n + t, j - 1))
                pe.matmul(pA[(j + 1) % 2][:], xsT[:, WIN:WIN + P], wqkv[:, j * CW:(j + 1) * CW], start=True, stop=True) \
                    .then_inc(qk_done.sem, 1)

            def turn_qk(n, t, g):
                if g < 2:
                    pe.wait_ge(aoT_ready.sem, aoT_ready.at(n + t, 0))
                else:
                    pe.wait_ge(t_copied.sem, t_copied.at(n + t, g - 1))
                src = qk[:, 2 * (g // 2):2 * (g // 2) + 2, :].rearrange("p a (b d) -> p (a b) d", d=P)
                for p in range(4):
                    ins_ = pe.transpose(pT[g % 2][:, p, :], src[:, 4 * (g % 2) + p, :], c.ident[:])
                ins_.then_inc(t_done.sem, 1)

            def values(n, t, w):
                wv = wqkv[:, 2 * H * DH:3 * H * DH].rearrange("p (b a d) -> p a b d", a=2, d=DH)
                if w < 2:
                    pe.wait_ge(u_ready.sem, u_ready.at(n + t, 3 + w))
                    pe.wait_ge(sq_ready.sem, sq_ready.at(n + t, 3 + w))
                else:
                    pe.wait_ge(v_ready.sem, v_ready.at(n + t, w - 1))
                for a in range(2):
                    ins_ = pe.matmul(pA[(w + 1) % 2][a * DH:(a + 1) * DH, :], xsT[:, w * WIN:w * WIN + DH], wv[:, a],
                                     start=True, stop=True)
                ins_.then_inc(v_done.sem, 1)

            def body(n, ta, tb, tc):
                if ta is not None:
                    pe.wait_ge(xin_ready.sem, xin_ready.at(n + ta, 1))
                    pe.wait_ge(att_ready.sem, att_ready.at(n + ta - 1 if not (isinstance(ta, int) and ta == 0) else n, 0))
                    pe.matmul(xs_in[0:D // 2], xin[:, 1, 0:D // 2], c.ident[:], start=True, stop=True)
                    pe.matmul(xs_in[D // 2:D], xin[:, 1, D // 2:D], down1[:], start=True, stop=False)
                    pe.matmul(xs_in[D // 2:D], xin[:, 0, D // 2:D], last1[:], start=False, stop=True).then_inc(xs_built.sem, 1)
                if tc is not None:
                    pe.wait_ge(aoT_ready.sem, aoT_ready.at(n + tc, 2))
                    pe.wait_ge(h_ready.sem, h_ready.at(n + tc, 0))
                    for p in range(HP):
                        ins_ = pe.matmul(pC[0][:, 0, :], aoT[:, p, :], wo[:, p, :], start=p == 0, stop=p == HP - 1)
                    ins_.then_inc(wo_done.sem, 1)
                if ta is not None:
                    project_qk(n, ta, 0)
                if tb is not None:
                    pe.wait_ge(qk_ready.sem, qk_ready.at(n + tb, 1))
                    turn_qk(n, tb, 0)
                    turn_qk(n, tb, 1)
                if tc is not None:
                    pe.wait_ge(x1_ready.sem, x1_ready.at(n + tc, 1))
                    pe.wait_ge(x2_done.sem, x2_done.at(n + tc, 0))
                    pe.matmul(pC[1][:, 0, 0:D // 2], down1[:], x1w[:, row(tc), D // 2:D], start=True, stop=False)
                    pe.matmul(pC[1][:, 0, 0:D // 2], last1[:], x1w[:, row(tc) - 1, D // 2:D], start=False, stop=True) \
                        .then_inc(sh_done.sem, 1)
                if tb is not None:
                    turn_qk(n, tb, 2)
                    turn_qk(n, tb, 3)
                if ta is not None:
                    project_qk(n, ta, 1)
                if tb is not None:
                    pe.wait_ge(att_ready.sem, att_ready.at(n + tb, 0))
                    mk = mask[:, tb % TB, :].unsqueeze(1).broadcast_to([P, HP, DH])
                    for a in range(2):
                        if a == 1:
                            pe.wait_ge(t_copied.sem, t_copied.at(n + tb, 4))
                        pe.matmul(pS[:, a], c.identb[:], mk, start=True, stop=False, skip_group_check=True)
                    for p in range(HP):
                        for w in range(NWT):
                            for a in range(2):
                                lo = a * DH
                                ins_ = pe.matmul(pS[w * WIN:(w + 1) * WIN, a, p, :], qT[lo:lo + DH, p, w * WIN:(w + 1) * WIN],
                                                 kT[lo:lo + DH, p, w * WIN:w * WIN + DH], start=False,
                                                 stop=True, skip_group_check=True)
                    ins_.then_inc(s_done.sem, 1)
                if ta is not None:
                    project_qk(n, ta, 2)
                if tc is not None:
                    pe.wait_ge(n_ready.sem, n_ready.at(n + tc, 1))
                    pe.transpose(pC[0][:, 0, :], xn1[:], c.ident[:]).then_inc(nT_done.sem, 1)
                if ta is not None:
                    project_qk(n, ta, 3)
                if tc is not None:
                    pe.wait_ge(xnT_ready.sem, xnT_ready.at(n + tc, 1))
                    for a in range(2):
                        for f in range(NF):
                            ins_ = pe.matmul(pC[a][:, f, :], w1[:, a, f * P:(f + 1) * P], xnT[:], start=True, stop=True)
                    ins_.then_inc(w1_done.sem, 1)
                if tb is not None:
                    pe.wait_ge(t_copied.sem, t_copied.at(n + tb, 4))
                    for p in range(HP):
                        if p % 4 == 0:
                            pe.wait_ge(exp_ready.sem, exp_ready.at(n + tb, p // 4 + 1))
                        ins_ = pe.transpose(pT[p // 4][:, p % 4, :], pr[:, p, :, :].rearrange("p a d -> p (a d)"), c.ident[:])
                        if p % 4 == 3:
                            ins_.then_inc(PT_done.sem, 1)
                if ta is not None:
                    values(n, ta, 0)
                    values(n, ta, 1)
                if tb is not None:
                    pe.wait_ge(PT_ready.sem, PT_ready.at(n + tb, 2))
                    pe.wait_ge(v_ready.sem, v_ready.at(n + tb, NWT))
                    pe.matmul(pS[:, 0, 0, 0:2], c.identb[:], c.identb[:, 0:2], start=True, stop=True)
                    for p in range(HP):
                        for w in range(NWT):
                            for a in range(2):
                                lo = a * DH
                                ins_ = pe.matmul(pS[w * WIN:(w + 1) * WIN, a, p, :], PT[lo:lo + DH, p, w * WIN:(w + 1) * WIN],
                                                 v2[lo:lo + DH, w, p * DH:(p + 1) * DH], start=True, stop=True)
                    ins_.then_inc(pv_done.sem, 1)
                if tc is not None:
                    pe.wait_ge(h_ready.sem, h_ready.at(n + tc, 1))
                    for f in range(NF):
                        pe.matmul(pC[1][:, 0, :], hid[:, f, :], w2[:, f, :], start=f == 0, stop=False)
                    pe.matmul(pC[1][:, 0, :], c.ones[:], b2[:], start=False, stop=True).then_inc(w2_done.sem, 1)
                if ta is not None:
                    values(n, ta, 2)
                if tb is not None:
                    pe.wait_ge(att_ready.sem, att_ready.at(n + tb, 1))
                    pe.wait_ge(PT_ready.sem, PT_ready.at(n + tb, 2))
                    for p in range(HP):
                        ins_ = pe.transpose(pT[p // 4][:, p % 4, :], att[:, p * P:(p + 1) * P], c.ident[:])
                        if p % 4 == 3:
                            ins_.then_inc(aT_done.sem, 1)
                if ta is not None:
                    values(n, ta, 3)

            layers(pe, start, body)

        @block.scalar
        def _(act):
            def start(L):
                wait_layer(act, L)
                act.wait_ge(x2_done.sem, x2_done.at(L * NT, 0))

            def piece(n, t, j):
                act.wait_ge(qk_done.sem, qk_done.at(n + t, j + 1))
                act.wait_ge(rot_ready.sem, rot_ready.at(n + t, 0))
                act.wait_ge(summed.sem, summed.at(n + t, 0))
                act.activation(raw[:, j, :], pA[(j + 1) % 2][:], ACT.Copy).then_inc(raw_ready.sem, 1)
                act.activation(sq[:, j, :], pA[(j + 1) % 2][:], ACT.Square).then_inc(sq_ready.sem, 1)

            def turned_qk(n, t, g):
                act.wait_ge(t_done.sem, t_done.at(n + t, g + 1))
                dst = (qT[:, 4 * (g % 2):4 * (g % 2) + 4, :] if g < 2 else
                       kT[:, 4 * (g % 2):4 * (g % 2) + 4, WIN:WIN + P])
                act.activation(dst, pT[g % 2][:], ACT.Copy).then_inc(t_copied.sem, 1)

            def value(n, t, w):
                act.wait_ge(v_done.sem, v_done.at(n + t, w + 1))
                act.activation(v2[:, w, :], pA[(w + 1) % 2][:], ACT.Copy).then_inc(v_ready.sem, 1)

            def fetch(n, t):
                act.wait_ge(xs_built.sem, xs_built.at(n + t, 0))
                act.activation(xin[:], xw[:, bass.ds(row(t) - 1, 2), :], ACT.Copy).then_inc(xin_ready.sem, 1)

            def body(n, ta, tb, tc):
                if ta is not None:
                    if isinstance(ta, int) and ta == 0:
                        fetch(n, 0)
                    act.wait_ge(xs_built.sem, xs_built.at(n + ta, 1))
                    act.wait_ge(xtail.sem, xtail.at(n + ta, 1))
                    act.activation(xsT[:, WIN:WIN + P], xs_in, ACT.Copy).then_inc(xsT_ready.sem, 1)
                if tb is not None:
                    turned_qk(n, tb, 0)
                    turned_qk(n, tb, 1)
                if ta is not None:
                    piece(n, ta, 0)
                if tb is not None:
                    act.wait_ge(ktail.sem, ktail.at(n + tb, 1))
                    turned_qk(n, tb, 2)
                    turned_qk(n, tb, 3)
                if ta is not None:
                    piece(n, ta, 1)
                if tc is not None:
                    act.wait_ge(nT_done.sem, nT_done.at(n + tc, 1))
                    act.activation(xnT[:], pC[0][:, 0, :], ACT.Identity, scale=gain[:], bias=shift_[:]).then_inc(xnT_ready.sem, 1)
                if ta is not None:
                    piece(n, ta, 2)
                if tb is not None:
                    for g in range(2):
                        act.wait_ge(sub_ready.sem, sub_ready.at(n + tb, g + 1))
                        half = pr[:, 4 * g:4 * g + 4]
                        act.activation(half, half, ACT.Exp).then_inc(exp_ready.sem, 1)
                if ta is not None:
                    piece(n, ta, 3)
                if tb is not None:
                    for g in range(2):
                        act.wait_ge(PT_done.sem, PT_done.at(n + tb, g + 1))
                        act.activation(PT[:, 4 * g:4 * g + 4, :], pT[g][:], ACT.Copy).then_inc(PT_ready.sem, 1)
                if tc is not None:
                    act.wait_ge(w1_done.sem, w1_done.at(n + tc, 1))
                    for f in range(NF):
                        ins_ = act.activation(gl[:, f, :], pC[1][:, f, :], ACT.Gelu, bias=b1[:, 1, f:f + 1])
                    ins_.then_inc(gl_ready.sem, 1)
                act.activation(turn_table[:], c.ones[0:1, 0:1], ACT.Exp)
                if ta is not None and not (isinstance(ta, int) and ta == NT - 1):
                    fetch(n, ta + 1)
                if ta is not None:
                    if tb is not None:
                        act.wait_ge(pv_done.sem, pv_done.at(n + tb, 1))
                    for w in range(NWT - 1):
                        value(n, ta, w)
                if tb is not None:
                    for g in range(2):
                        act.wait_ge(aT_done.sem, aT_done.at(n + tb, g + 1))
                        if g == 0 and tc is not None:
                            act.wait_ge(wo_done.sem, wo_done.at(n + tc, 1))
                        act.activation(aoT[:, 4 * g:4 * g + 4, :], pT[g][:], ACT.Copy).then_inc(aoT_ready.sem, 1)
                if ta is not None:
                    value(n, ta, NWT - 1)

            layers(act, start, body)

        @block.vector
        def _(dve):
            dve.wait_ge(base_in.sem, base_in.base + 64)
            dve.wait_ge(made.sem, mb + 18)

            def start(L):
                wait_layer(dve, L)
                for op in range(2):
                    dve.tensor_tensor(tab[:, :, 2 * op, :], base[2 * op][:], qks[:, op, :].unsqueeze(1).broadcast_to([P, TB, DH]),
                                      ALU.mult).then_inc(tabs.sem, 1)
                    half = DH // 2
                    for a in range(2):
                        dve.tensor_tensor(tab[:, :, 2 * op + 1, a * half:(a + 1) * half],
                                          base[2 * op + 1][:, :, a * half:(a + 1) * half],
                                          qks[:, op, (1 - a) * half:(2 - a) * half].unsqueeze(1).broadcast_to([P, TB, half]),
                                          ALU.mult).then_inc(tabs.sem, 1)
                dve.wait_ge(tabs.sem, tabs.at(L, 6))

            def turn_piece(n, t, j):
                if j == 0:
                    dve.wait_ge(t_done.sem, t_done.at(n + t, 0))
                    dve.wait_ge(cur_ready.sem, cur_ready.at(n + t, 1))
                dve.wait_ge(qk_done.sem, qk_done.at(n + t, j + 1))
                dve.wait_ge(sq_ready.sem, sq_ready.at(n + t, j + 1))
                cosine = cur[:, 2 * (j // 2), :].unsqueeze(1).broadcast_to([P, CW // DH, DH])
                dve.tensor_tensor(qk[:, j, :].rearrange("p (h d) -> p h d", d=DH),
                                  pA[(j + 1) % 2][:].rearrange("p (h d) -> p h d", d=DH), cosine, ALU.mult).then_inc(u_ready.sem, 1)

            def squares(n, t, a):
                dve.wait_ge(sq_ready.sem, sq_ready.at(n + t, 2 * a + 2))
                if a == 0:
                    dve.wait_ge(qk_ready.sem, qk_ready.at(n + t, 0))
                dve.reduce_sum(ssq[:, a * H:(a + 1) * H], sq[:, 2 * a:2 * a + 2, :].rearrange("p a (h d) -> p (a h) d", d=DH),
                               AX.X).then_inc(summed.sem, 1)

            def body(n, ta, tb, tc):
                if ta is not None:
                    dve.wait_ge(rot_ready.sem, rot_ready.at(n + ta, 0))
                    dve.wait_ge(u_ready.sem, u_ready.at(n + ta, 0))
                    dve.wait_ge(ktail.sem, ktail.at(n + ta, 0))
                    dve.tensor_scalar(cur[:], tab[:, ta % TB], 1.0, None, ALU.mult).then_inc(cur_ready.sem, 1)
                if tc is not None:
                    ch = Chain(dve, cchain, n + tc)
                    dve.wait_ge(wo_done.sem, wo_done.at(n + tc, 1))
                    dve.tensor_tensor(x1w[:, row(tc), :], pC[0][:, 0, :], xw[:, row(tc), :], ALU.add).then_inc(x1_ready.sem, 1)
                    dve.wait_ge(x1_ready.sem, x1_ready.at(n + tc, 1))
                    dve.tensor_scalar(xs1[:, 0, 0:D // 2], x1w[:, row(tc), 0:D // 2], 1.0, None, ALU.mult)
                    dve.wait_ge(sh_done.sem, sh_done.at(n + tc, 1))
                    ch.link(dve.tensor_copy(xs1[:, 0, D // 2:D], pC[1][:, 0, 0:D // 2]))
                    ch.wait()
                    ins_ = dve.bn_stats(stats[:, 0, :], xs1[:, 0, :])
                    croot_stats(dve, ch, ins_, stats, work)
                    ch.wait()
                    croots.request(dve, work[:, 6, :], work[:, 1, :], EPS_LN, ALU.add)
                if ta is not None:
                    turn_piece(n, ta, 0)
                if tc is not None:
                    croots.receive(dve, n + tc)
                    dve.tensor_scalar(xn1[:], xs1[:, 0, :], work[:, 0, 0:1], work[:, 6, 0:1], ALU.subtract, ALU.mult) \
                        .then_inc(n_ready.sem, 1)
                if ta is not None:
                    turn_piece(n, ta, 1)
                    squares(n, ta, 0)
                if tb is not None:
                    dve.wait_ge(s_done.sem, s_done.at(n + tb, 1))
                    for g in range(2):
                        part = pS[:, :, 4 * g:4 * g + 4, :]
                        mg = mx[:].rearrange("p (a b) -> p a b", a=2)[:, :, 4 * g:4 * g + 4]
                        dve.reduce_max(mg, part, AX.X).then_inc(mxd.sem, 1)
                        dve.wait_ge(mxd.sem, mxd.at(n + tb, g + 1))
                        dve.tensor_tensor(pr[:, 4 * g:4 * g + 4].rearrange("p b a d -> p a b d"), part,
                                          mg.unsqueeze(3).broadcast_to([P, 2, HP // 2, DH]), ALU.subtract) \
                            .then_inc(sub_ready.sem, 1)
                if ta is not None:
                    turn_piece(n, ta, 2)
                    turn_piece(n, ta, 3)
                    squares(n, ta, 1)
                    dve.wait_ge(summed.sem, summed.at(n + ta, 2))
                    qroots.request(dve, inv[:], ssq[:], 1e-24, ALU.max)
                if tb is not None:
                    dve.wait_ge(exp_ready.sem, exp_ready.at(n + tb, 2))
                    prv = pr[:].rearrange("p b a d -> p a b d")
                    dve.reduce_sum(tot[:].rearrange("p (a b) -> p a b", a=2), prv, AX.X).then_inc(totd.sem, 1)
                    dve.wait_ge(totd.sem, totd.at(n + tb, 1))
                    dve.reciprocal(tot[:], tot[:]).then_inc(inv_ready.sem, 1)
                if tc is not None:
                    dve.wait_ge(gl_ready.sem, gl_ready.at(n + tc, 1))
                    for f in range(NF):
                        ins_ = dve.scalar_tensor_tensor(out=hid[:, f, :], in0=pC[0][:, f, :], scalar=b1[:, 0, f:f + 1],
                                                        in1=gl[:, f, :], op0=ALU.add, op1=ALU.mult)
                    ins_.then_inc(h_ready.sem, 1)
                if tb is not None:
                    dve.wait_ge(pv_done.sem, pv_done.at(n + tb, 1))
                    dve.wait_ge(inv_ready.sem, inv_ready.at(n + tb, 1))
                    dve.tensor_tensor(att[:].rearrange("p (b a d) -> p a b d", a=2, d=DH), pS[:],
                                      tot[:].rearrange("p (a b) -> p a b", a=2).unsqueeze(3).broadcast_to([P, 2, HP, DH]),
                                      ALU.mult).then_inc(att_ready.sem, 1)
                if tc is not None:
                    dve.wait_ge(w2_done.sem, w2_done.at(n + tc, 1))
                    dve.tensor_tensor(xw[:, row(tc), :], pC[1][:, 0, :], x1w[:, row(tc), :], ALU.add).then_inc(x2_done.sem, 1)
                if ta is not None:
                    dve.wait_ge(rot_ready.sem, rot_ready.at(n + ta, QKC))
                    dve.wait_ge(u_ready.sem, u_ready.at(n + ta, QKC))
                    dve.tensor_tensor(qk[:], qk[:], rot[:], ALU.add).then_inc(added_rot.sem, 1)
                    qroots.receive(dve, n + ta)
                    dve.wait_ge(added_rot.sem, added_rot.at(n + ta, 1))
                    qv = qk[:].rearrange("p a (h d) -> p (a h) d", d=DH)
                    dve.tensor_tensor(qv, qv, inv[:].unsqueeze(2).broadcast_to([P, 2 * H, DH]), ALU.mult).then_inc(qk_ready.sem, 1)

            layers(dve, start, body)


def croot_stats(dve, ch, ins_, stats, work):
    ch.link(ins_)
    row_stats(dve, ch, stats, work, 1)


class Roots2:

    def __init__(self, c, name):
        self.asked, self.given = c.new_signal(f"{name}_asked", 1), c.new_signal(f"{name}_given", 1)

    def request(self, e, out, value, floor, op):
        e.tensor_scalar(out, value, floor, None, op).then_inc(self.asked.sem, 1)

    def receive(self, e, turn):
        e.wait_ge(self.given.sem, self.given.at(turn, 1))

    def ask(self, e, chain, turn, out, value, floor, op):
        chain.wait()
        self.request(e, out, value, floor, op)
        self.receive(e, turn)

    def give(self, pool, c, turn, value):
        pool.wait_ge(self.asked.sem, self.asked.at(turn, 1))
        pool.tensor_tensor(value, value, c.half[:, 0:value.shape[1]], ALU.pow).then_inc(self.given.sem, 1)


def local(c):
    nc = c.nc
    with ExitStack() as st_:
        xw = st_.enter_context(nc.sbuf_tensor("xw", [P, B * (TB + 1), D], FP32))
        x1w = st_.enter_context(nc.sbuf_tensor("x1w", [P, B * (TB + 1), D], FP32))
        zeroed = c.new_signal("pads_zeroed", 1)
        with nc.Block() as block:
            @block.gpsimd
            def _(pool):
                c.lift(pool)
                for a in (xw, x1w):
                    pool.memset(a[:], 0.0).then_inc(zeroed.sem, 1)
                pool.wait_ge(zeroed.sem, zeroed.base + 2)
        enter_local(c, xw)
        local_stack(c, xw, x1w)
        leave_local(c, xw)


NE, HID = 8, 384
HC = HID // P


def experts(c):
    nc, ins = c.nc, c.ins
    NCHAIN = 23
    with ExitStack() as st_:
        def sb(name, shape, dt=FP32):
            return st_.enter_context(nc.sbuf_tensor(f"{name}_moe", shape, dt))

        def ps(name, shape, dt=FP32):
            return st_.enter_context(nc.psum_tensor(f"{name}_moe", shape, dt))

        wg, wu, wd = sb("wg", [P, NE, HID]), sb("wu", [P, NE, HID]), sb("wd", [P, NE * HC, D])
        wr, gain = sb("wr", [P, NE]), sb("gain", [P, 1])
        lower = sb("lower", [P, NE, NE])
        xn, xnT = sb("xn", [P, CH, D]), sb("xnT", [P, CW])
        stats, work = sb("stats", [P, CH, 6]), sb("work", [P, 9, CH])
        lg, ex, wt = sb("lg", [P, CH, NE]), sb("ex", [P, CH, NE]), sb("wt", [P, CH, NE])
        top, tot, comb = sb("top", [P, CH]), sb("tot", [P, CH]), sb("comb", [P, CH, NE])
        gt, eq = sb("gt", [P, CH, NE, NE]), sb("eq", [P, CH, NE, NE])
        rank = sb("rank", [P, CH, NE])
        act_g = [sb(f"act_g{n}", [P, CW]) for n in range(2)]
        hid = [[sb(f"hid{n}{m}", [P, CW]) for m in range(HC)] for n in range(2)]
        acc, y = sb("acc", [P, CH, D]), sb("y", [P, CH, D])
        pT, pR = ps("pT", [P, CW]), ps("pR", [P, CH, NE])
        pG = [ps(f"pG{n}", [P, CW]) for n in range(2)]
        pU = [ps(f"pU{n}", [P, CW]) for n in range(2)]
        pD = [ps(f"pD{n}", [P, CH, D]) for n in range(2)]

        loaded, made = c.new_signal("moe_loaded", 0), c.new_signal("moe_made", 0)
        chain = c.new_signal("moe_chain", NCHAIN)
        roots = Roots(c, 2)
        normed, turned, xT_ready = c.new_signal("moe_normed", 1), c.new_signal("moe_turned", 1), c.new_signal("moe_xT_ready", 1)
        routed, shifted, expd = c.new_signal("routed", 1), c.new_signal("logits_shifted", 1), c.new_signal("logits_exped", 1)
        up = c.new_signal("up_done", NE * HC)
        gated = c.new_signal("gated", NE * HC)
        hid_ready = c.new_signal("hid_ready", NE * HC)
        down = c.new_signal("down_done", NE)
        taken = c.new_signal("down_taken", NE)
        added = c.new_signal("moe_added", 1)
        block = st_.enter_context(nc.Block())

        @block.sync
        def _(sp):
            c.lift(sp)
            for dst, src in ((wr, ins["moe_wr"]), (gain, ins["moe_g"]), (wg, ins["moe_wg"].rearrange("x d h -> d x h")),
                             (wu, ins["moe_wu"].rearrange("x d h -> d x h")),
                             (wd, ins["moe_wd"].rearrange("x (c p) d -> p (x c) d", p=P))):
                sp.dma_start(dst[:], src).then_inc(loaded.sem, 16)
            sp.wait_ge(loaded.sem, loaded.base + 80)

        @block.gpsimd
        def _(pool):
            pool.memset(lower[:], 1.0).then_inc(made.sem, 1)
            pool.wait_ge(made.sem, made.base + 1)
            pool.affine_select(out=lower[:], in_=lower[:], compare_op=ALU.is_ge, fill=0.0, base=-1,
                               pattern=[[1, NE], [-1, NE]], channel_multiplier=0).then_inc(made.sem, 1)
            with pool.Fori(0, NC_) as i:
                roots.give(pool, c, i, 1, work[:, 8, :])
                roots.give(pool, c, i, 2, work[:, 6, :])

        @block.scalar
        def _(act):
            act.wait_ge(loaded.sem, loaded.base + 80)
            with act.Fori(0, NC_) as i:
                act.wait_ge(turned.sem, turned.at(i, 1))
                act.wait_ge(up.sem, up.at(i, 0))
                act.activation(xnT[:], pT[:], ACT.Copy, scale=gain[:]).then_inc(xT_ready.sem, 1)
                act.wait_ge(shifted.sem, shifted.at(i, 1))
                act.activation(ex[:], wt[:], ACT.Exp).then_inc(expd.sem, 1)
                for u in range(NE * HC):
                    act.wait_ge(up.sem, up.at(i, u + 1))
                    act.wait_ge(hid_ready.sem, hid_ready.at(i, max(u - 1, 0)))
                    act.activation(act_g[u % 2][:], pG[u % 2][:], ACT.Silu).then_inc(gated.sem, 1)

        @block.tensor
        def _(pe):
            pe.wait_ge(loaded.sem, loaded.base + 80)
            with pe.Fori(0, NC_) as i:
                pe.wait_ge(normed.sem, normed.at(i, 1))
                for t in range(CH):
                    ins_ = pe.transpose(pT[:, t * P:(t + 1) * P], xn[:, t, :], c.ident[:])
                ins_.then_inc(turned.sem, 1)
                pe.wait_ge(xT_ready.sem, xT_ready.at(i, 1))
                for t in range(CH):
                    ins_ = pe.matmul(pR[:, t, :], xnT[:, t * P:(t + 1) * P], wr[:], start=True, stop=True)
                ins_.then_inc(routed.sem, 1)

                def go_down(x):
                    pe.wait_ge(hid_ready.sem, hid_ready.at(i, (x + 1) * HC))
                    pe.wait_ge(taken.sem, taken.at(i, max(x - 1, 0)))
                    for t in range(CH):
                        for m in range(HC):
                            ins_ = pe.matmul(pD[x % 2][:, t, :], hid[x % 2][m][:, t * P:(t + 1) * P], wd[:, x * HC + m, :],
                                             start=m == 0, stop=m == HC - 1)
                    ins_.then_inc(down.sem, 1)

                for x in range(NE):
                    for m in range(HC):
                        u = x * HC + m
                        pe.wait_ge(hid_ready.sem, hid_ready.at(i, max(u - 1, 0)))
                        pe.matmul(pG[u % 2][:], wg[:, x, m * P:(m + 1) * P], xnT[:], start=True, stop=True)
                        pe.matmul(pU[u % 2][:], wu[:, x, m * P:(m + 1) * P], xnT[:], start=True, stop=True) \
                            .then_inc(up.sem, 1)
                    if x:
                        go_down(x - 1)
                go_down(NE - 1)

        @block.vector
        def _(dve):
            dve.wait_ge(made.sem, made.base + 2)
            with dve.Fori(0, NC_) as i:
                ch = Chain(dve, chain, i)

                def step(ins_):
                    ch.link(ins_)
                    ch.wait()

                for t in range(CH):
                    ins_ = dve.bn_stats(stats[:, t, :], c.xl[:, i * CH + t, :])
                ch.link(ins_)
                row_stats(dve, ch, stats, work, CH)
                ch.wait()
                step(dve.tensor_tensor(work[:, 7, :], work[:, 0, :], work[:, 0, :], ALU.mult))
                step(dve.tensor_tensor(work[:, 7, :], work[:, 7, :], work[:, 1, :], ALU.add))
                roots.count = 0
                ask_root(dve, ch, roots, work[:, 8, :], work[:, 7, :], EPS_RMS)
                dve.wait_ge(turned.sem, turned.at(i, 0))
                for t in range(CH):
                    ins_ = dve.tensor_scalar(xn[:, t, :], c.xl[:, i * CH + t, :], work[:, 8, t:t + 1], None, ALU.mult)
                ins_.then_inc(normed.sem, 1)
                dve.wait_ge(routed.sem, routed.at(i, 1))
                step(dve.tensor_copy(lg[:], pR[:]))
                step(dve.reduce_max(top[:], lg[:], AX.X))
                dve.tensor_tensor(wt[:], lg[:], top[:].unsqueeze(2).broadcast_to([P, CH, NE]), ALU.subtract) \
                    .then_inc(shifted.sem, 1)
                other = lg[:].unsqueeze(2).broadcast_to([P, CH, NE, NE])
                own = lg[:].unsqueeze(3).broadcast_to([P, CH, NE, NE])
                for t in range(CH):
                    dve.tensor_tensor(gt[:, t], other[:, t], own[:, t], ALU.is_gt)
                    ins_ = dve.tensor_tensor(eq[:, t], other[:, t], own[:, t], ALU.is_equal)
                step(ins_)
                for t in range(CH):
                    ins_ = dve.tensor_tensor(eq[:, t], eq[:, t], lower[:], ALU.mult)
                step(ins_)
                step(dve.tensor_tensor(gt[:], gt[:], eq[:], ALU.add))
                step(dve.reduce_sum(rank[:], gt[:], AX.X))
                step(dve.tensor_scalar(rank[:], rank[:], 1.5, None, ALU.is_lt))
                dve.wait_ge(expd.sem, expd.at(i, 1))
                step(dve.tensor_tensor(wt[:], ex[:], rank[:], ALU.mult))
                step(dve.reduce_sum(tot[:], wt[:], AX.X))
                step(dve.reciprocal(tot[:], tot[:]))
                step(dve.tensor_tensor(comb[:], wt[:], tot[:].unsqueeze(2).broadcast_to([P, CH, NE]), ALU.mult))

                def take(x):
                    dve.wait_ge(down.sem, down.at(i, x + 1))
                    if x:
                        dve.wait_ge(taken.sem, taken.at(i, x))
                    for t in range(CH):
                        if x == 0:
                            ins_ = dve.tensor_scalar(acc[:, t, :], pD[0][:, t, :], comb[:, t, 0:1], None, ALU.mult)
                        else:
                            ins_ = dve.scalar_tensor_tensor(out=acc[:, t, :], in0=pD[x % 2][:, t, :],
                                                            scalar=comb[:, t, x:x + 1], in1=acc[:, t, :],
                                                            op0=ALU.mult, op1=ALU.add)
                    ins_.then_inc(taken.sem, 1)

                for x in range(NE):
                    for m in range(HC):
                        u = x * HC + m
                        dve.wait_ge(gated.sem, gated.at(i, u + 1))
                        if m == 0:
                            dve.wait_ge(down.sem, down.at(i, max(x - 1, 0)))
                        dve.tensor_tensor(hid[x % 2][m][:], pU[u % 2][:], act_g[u % 2][:], ALU.mult).then_inc(hid_ready.sem, 1)
                    if x:
                        take(x - 1)
                take(NE - 1)
                dve.wait_ge(taken.sem, taken.at(i, NE))
                step(dve.tensor_tensor(acc[:], acc[:], c.xl[:, bass.ds(i * CH, CH), :], ALU.add))
                layernorm_add(dve, ch, roots, acc, y, stats, work, c.x, i, added, more=True)
                assert ch.count == NCHAIN, ch.count


def build(nc, ins, out, until=99):
    ctx = ExitStack()
    with ctx:
        c = Core(nc, ins, ctx)
        scr = {"mha": nc.dram_tensor("scratch_mha", (2, B * NG * HG * 8, 3, S), BF16, kind="Internal").ap(),
               "low_rank": nc.dram_tensor("scratch_low", (2, B * NG * HG * 32, 3, S), BF16, kind="Internal").ap(),
               "v": nc.dram_tensor("scratch_v", (B * NG * S, HG * VC), FP32, kind="Internal").ap()}
        scr["rope"] = scr["mha"]
        setup(c, ins["x"])
        for n, kind in enumerate(("mha", "local", "low_rank", "rope")):
            if n >= until:
                break
            if kind == "local":
                local(c)
                continue
            project(c, kind, scr)
            attend(c, kind, scr)
            post(c, kind)
            if kind == "rope":
                experts(c)
        store_out(c, out)


def local_layouts(f):
    import numpy as np

    half = np.arange(0, DH, 2, dtype=np.float32)
    t = np.arange(S, dtype=np.float32)
    freqs = t[:, None] * (np.float32(1.0) / np.float32(10000.0) ** (half / np.float32(DH)))[None, :]
    freqs = np.concatenate([freqs, freqs], -1).astype(np.float32)
    base = (half + np.float32(0.4 * DH)) / np.float32(1.4 * DH)
    scale = base[None, :].astype(np.float32) ** ((t - S // 2) / np.float32(WIN // 2))[:, None].astype(np.float32)
    scale = np.concatenate([scale, scale], -1)
    sign = np.where(np.arange(DH) < DH // 2, -1.0, 1.0).astype(np.float32)
    cos, sin = np.cos(freqs), np.sin(freqs) * sign
    inv = np.float32(1.0) / scale
    HI = 341

    def pad(w, axis):
        wide = list(w.shape)
        wide[axis] = NF * P - HI
        return np.concatenate([w, np.zeros(wide, w.dtype)], axis)

    w1 = pad(f("L0_ffn_W1").reshape(-1, D, 2, HI), 3)
    b1 = pad(f("L0_ffn_b1").reshape(-1, 2, HI), 2).reshape(-1, 2, NF, P).transpose(0, 3, 1, 2)
    return {
        "local_wqkv": f("L0_ffn_Wqkv"), "local_wo": f("L0_ffn_Wo"), "local_w1": w1, "local_b1": b1,
        "local_w2": pad(f("L0_ffn_W2"), 1), "local_b2": f("L0_ffn_b2"), "local_g": f("L0_ffn_ln_g").reshape(-1, D, 1),
        "local_b": f("L0_ffn_ln_b").reshape(-1, D, 1), "local_qs": f("L0_ffn_q_scale"), "local_ks": f("L0_ffn_k_scale"),
        "local_table0": cos * scale * np.float32(8.0), "local_table1": sin * scale * np.float32(8.0),
        "local_table2": cos * inv, "local_table3": sin * inv,
    }


def layouts(inputs):
    import numpy as np

    f = lambda n: np.asarray(inputs[n])
    heads_last = lambda w: np.ascontiguousarray(w.transpose(1, 0, 2).reshape(D, -1))
    t = np.arange(S, dtype=np.float32)
    inv = (1.0 / np.float32(10000.0) ** (np.arange(0, 8, 2, dtype=np.float32) / np.float32(8))).astype(np.float32)
    emb = np.einsum("i,j->ij", t, inv)
    emb = np.concatenate([emb, emb], -1)
    cos, sin = (np.tile(g(emb).T.astype(np.float32), (H, 1)) for g in (np.cos, np.sin))
    qs = np.float32(8 ** -0.5)
    return {
        "x": f("L0_attn_embeddings").reshape(B * S, D),
        "mha_wq": heads_last(f("L0_attn_Wq")), "mha_wk": heads_last(f("L0_attn_Wk")), "mha_wv": heads_last(f("L0_attn_Wv")),
        "mha_bq": f("L0_attn_bq").reshape(P, 1), "mha_bk": f("L0_attn_bk").reshape(P, 1),
        "mha_bv": f("L0_attn_bv").reshape(1, P), "mha_wo": f("L0_attn_Wo"), "mha_bo": f("L0_attn_bo").reshape(1, D),
        "low_rank_wq1": f("L1_attn_Wq1").T, "low_rank_wk1": f("L1_attn_Wk1").T, "low_rank_wq2": f("L1_attn_Wq2").T,
        "low_rank_wk2": f("L1_attn_Wk2").T, "low_rank_wv": f("L1_attn_Wv").T, "low_rank_wo": f("L1_attn_Wo").T,
        "low_rank_bo": f("L1_attn_bo").reshape(1, D),
        "rope_wq": f("L1_ffn_wq"), "rope_wk": f("L1_ffn_wk"), "rope_wv": f("L1_ffn_wv"), "rope_wo": f("L1_ffn_wo"),
        **local_layouts(f),
        "moe_wr": f("L1_ffn_w_router"), "moe_g": f("L1_ffn_g2").reshape(D, 1), "moe_wg": f("L1_ffn_wg"),
        "moe_wu": f("L1_ffn_wu"), "moe_wd": f("L1_ffn_wd"),
        "rope_g": f("L1_ffn_g1").reshape(D, 1),
        "rope_table0": cos * qs, "rope_table1": sin * qs, "rope_table2": cos, "rope_table3": sin,
    }


def program(nc, shapes, until=99):
    ins = {n: nc.dram_tensor(f"in_{n}", s, FP32, kind="ExternalInput").ap() for n, s in shapes.items()}
    out = nc.dram_tensor("out_x", (B * S, D), FP32, kind="ExternalOutput").ap()
    build(nc, ins, out, until)


def kernel(**inputs):
    import numpy as np
    import concourse.bacc as bacc
    from concourse.bass_utils import run_bass_kernel_spmd

    arrays = {n: np.ascontiguousarray(a) for n, a in layouts(inputs).items()}
    nc = bacc.Bacc("TRN2", target_bir_lowering=False, num_devices=1)
    program(nc, {n: a.shape for n, a in arrays.items()})
    r = run_bass_kernel_spmd(nc, [{f"in_{n}": a for n, a in arrays.items()}], core_ids=[0])
    return r.results[0]["out_x"].reshape(B, S, D)
```

```python
import concourse.bass as bass
from concourse import mybir
from contextlib import ExitStack

FP32 = mybir.dt.float32
BF16 = mybir.dt.bfloat16
ALU = mybir.AluOpType
ACT = mybir.ActivationFunctionType
AX = mybir.AxisListType

P = 128
B, S, D = 4, 1024, 128
NT = B * S // P
TB = S // P
CH = 4
CW = CH * P
NC_ = NT // CH
HALVES = S // CW
H = 16
HG = 4
NG = H // HG
VC = 32
EPS_LN = 1e-5
EPS_RMS = 1e-6
NEG = -1e30




class Signal:

    def __init__(self, sem):
        self.sem, self.base, self.per = sem, 1, 0

    def loop(self, per):
        self.per = per
        return self

    def at(self, turn, count):
        return turn * self.per + (self.base + count)

    def end(self, turns):
        self.base += turns * self.per


class Chain:

    def __init__(self, eng, signal, turn):
        self.eng, self.of, self.turn, self.count = eng, signal, turn, 0

    def link(self, ins):
        ins.then_inc(self.of.sem, 1)
        self.count += 1

    def wait(self):
        self.eng.wait_ge(self.of.sem, self.of.at(self.turn, self.count))


def row_stats(e, chain, st, work, n):
    me, me2, mo, mo2 = (st[:, 0:n, k] for k in (1, 2, 4, 5))
    chain.wait()
    e.tensor_tensor(work[:, 2, 0:n], me, mo, ALU.add)
    e.tensor_tensor(work[:, 3, 0:n], me, mo, ALU.subtract)
    chain.link(e.tensor_tensor(work[:, 4, 0:n], me2, mo2, ALU.add))
    chain.wait()
    e.tensor_scalar(work[:, 0, 0:n], work[:, 2, 0:n], 0.5, None, ALU.mult)
    e.tensor_scalar(work[:, 4, 0:n], work[:, 4, 0:n], 1.0 / D, None, ALU.mult)
    chain.link(e.scalar_tensor_tensor(out=work[:, 5, 0:n], in0=work[:, 3, 0:n], scalar=0.25, in1=work[:, 3, 0:n],
                                      op0=ALU.mult, op1=ALU.mult))
    chain.wait()
    chain.link(e.tensor_tensor(work[:, 1, 0:n], work[:, 4, 0:n], work[:, 5, 0:n], ALU.add))


def ask_root(e, chain, roots, out, var, eps):
    chain.wait()
    e.tensor_scalar(out, var, eps, None, ALU.add).then_inc(roots.asked.sem, 1)
    roots.count += 1
    e.wait_ge(roots.given.sem, roots.given.at(chain.turn, roots.count))


class Roots:

    def __init__(self, c, per):
        self.asked, self.given, self.count = c.new_signal("root_asked", per), c.new_signal("root_given", per), 0

    def give(self, pool, c, turn, count, value):
        pool.wait_ge(self.asked.sem, self.asked.at(turn, count))
        pool.tensor_tensor(value, value, c.half[:, 0:value.shape[1]], ALU.pow).then_inc(self.given.sem, 1)

    def end(self, turns):
        self.asked.end(turns)
        self.given.end(turns)


class Core:

    def __init__(self, nc, ins, ctx):
        self.nc, self.ins, self.ctx, self.signals, self.new = nc, ins, ctx, {}, []
        sb = self.keep
        self.x = sb("x_res", [P, NT, D], FP32)
        self.xl = sb("x_norm", [P, NT, D], FP32)
        self.heads_out = sb("heads_out", [P, B * NG, TB, D // NG], FP32)
        self.ident = sb("ident", [P, P], FP32)
        self.identb = sb("identb", [P, P], BF16)
        self.mask_k = sb("mask_k", [P, P], BF16)
        self.mask_q = sb("mask_q", [P, P], BF16)
        self.ones = sb("ones_row", [1, P], FP32)
        self.half = sb("minus_half", [P, 64], FP32)
        self.one = sb("one", [P, 32], FP32)

    def keep(self, name, shape, dt):
        return self.ctx.enter_context(self.nc.sbuf_tensor(name, shape, dt))

    def new_signal(self, name, per):
        if name not in self.signals:
            self.signals[name] = Signal(self.ctx.enter_context(self.nc.semaphore(name)))
            self.new.append(self.signals[name])
        return self.signals[name].loop(per)

    def lift(self, eng):
        for s in self.new:
            eng.sem_inc(s.sem, 1)
        self.new = []


def setup(c, x_dram):
    nc = c.nc
    loaded = c.new_signal("x_loaded", 16)
    made = c.new_signal("constants_made", 1)
    with nc.Block() as block:
        @block.sync
        def _(sp):
            c.lift(sp)
            sp.dma_start(c.x[:], x_dram.rearrange("(t p) d -> p t d", p=P)).then_inc(loaded.sem, 16)
            sp.wait_ge(loaded.sem, loaded.base + 16)

        @block.gpsimd
        def _(pool):
            for n, m in enumerate((c.ident, c.identb, c.mask_k, c.mask_q)):
                pool.memset(m[:], 0.0).then_inc(made.sem, 1)
            pool.memset(c.ones[:], 1.0).then_inc(made.sem, 1)
            pool.memset(c.half[:], -0.5).then_inc(made.sem, 1)
            pool.memset(c.one[:], 1.0).then_inc(made.sem, 1)
            pool.wait_ge(made.sem, made.base + 7)
            for m in (c.ident, c.identb):
                pool.affine_select(out=m[:], in_=m[:], compare_op=ALU.not_equal, fill=1.0, base=0,
                                   pattern=[[-1, P]], channel_multiplier=1).then_inc(made.sem, 1)
            pool.affine_select(out=c.mask_k[:], in_=c.mask_k[:], compare_op=ALU.is_ge, fill=NEG, base=0,
                               pattern=[[-1, P]], channel_multiplier=1).then_inc(made.sem, 1)
            pool.affine_select(out=c.mask_q[:], in_=c.mask_q[:], compare_op=ALU.is_ge, fill=NEG, base=0,
                               pattern=[[1, P]], channel_multiplier=-1).then_inc(made.sem, 1)
            pool.wait_ge(made.sem, made.base + 11)


def store_out(c, out_dram):
    nc = c.nc
    stored = c.new_signal("x_stored", 16)
    with nc.Block() as block:
        @block.sync
        def _(sp):
            c.lift(sp)
            sp.dma_start(out_dram.rearrange("(t p) d -> p t d", p=P), c.x[:]).then_inc(stored.sem, 16)
            sp.wait_ge(stored.sem, stored.base + 16)


def project(c, kind, scr):
    nc, ins = c.nc, c.ins
    low = kind == "low_rank"
    units = [(g, op) for g in range(NG if low else 1) for op in range(2)]
    NU = len(units)
    NCHAIN = {"mha": 4, "low_rank": 4, "rope": 6}[kind]
    scale = {"mha": 8 ** -0.5, "low_rank": 32 ** -0.5, "rope": 1.0}[kind]
    with ExitStack() as st_:
        def sb(name, shape, dt=FP32):
            return st_.enter_context(nc.sbuf_tensor(f"{name}_{kind}", shape, dt))

        def ps(name, shape, dt=FP32):
            return st_.enter_context(nc.psum_tensor(f"{name}_{kind}", shape, dt))

        wq, wk, wv = sb("wq", [P, P]), sb("wk", [P, P]), sb("wv", [P, P])
        w1 = [sb("wq1", [P, 64]), sb("wk1", [P, 64])]
        wide = [[sb(f"wide_{a}{b}", [P, NG, P]) for b in "12"] for a in "qk"]
        wvp = sb("wvp", [P, H * VC])
        vrow = sb("vrow", [1, H * VC])
        bvrow = sb("bvrow", [1, P])
        bias = sb("bias", [P, 2])
        gain = sb("gain", [P, 1])
        cs = [sb(f"table{n}", [P, S]) for n in range(4)]
        stats = sb("stats", [P, CH, 6])
        work = sb("work", [P, 9, CH])
        xn = sb("xn", [P, CH, D])
        xnT = sb("xnT", [P, CW])
        val = [sb(f"val{n}", [P, CW]) for n in range(2)]
        part = [sb(f"part{n}", [P, CW]) for n in range(2)]
        rest = [sb(f"rest{n}", [P, CW]) for n in range(2)]
        turned_part = [sb(f"turned_part{n}", [P, CW]) for n in range(2)]
        split = [sb(f"split{n}", [P, 3, CW], BF16) for n in range(4)]
        vout = [sb(f"vout{n}", [P, CH, H * VC]) for n in range(2)]
        pT = ps("pT", [P, CW])
        pA = [ps(f"pA{n}", [P, CW]) for n in range(2)]
        pB = [ps(f"pB{n}", [P, CW]) for n in range(2)]
        pV = [ps(f"pV{n}", [P, CW]) for n in range(2)]

        loaded = c.new_signal("weights_loaded", 0)
        prep = c.new_signal("weights_prepared", 0)
        chain = c.new_signal("norm_chain", NCHAIN)
        roots = Roots(c, 2 if kind == "rope" else 1)
        normed = c.new_signal("normed", 1)
        turned = c.new_signal("turned", 1)
        xT_ready = c.new_signal("xT_ready", 1)
        a_ready = c.new_signal("proj_ready", NU)
        first = c.new_signal("first_part", NU)
        vals = c.new_signal("val_ready", NU)
        dchain = c.new_signal("val_chain", NU)
        s1 = c.new_signal("split1_ready", NU)
        r1 = c.new_signal("rest_ready", NU)
        s2 = c.new_signal("split2_ready", NU)
        s3 = c.new_signal("split3_ready", NU)
        stores = 1 if low else NG
        stored = [c.new_signal(f"split_stored{n}", 16 * stores * NU // 2) for n in range(4)]
        v_ready = c.new_signal("v_ready", CH)
        v_out = c.new_signal("v_copied", CH)
        v_stored = c.new_signal("v_stored", 16 * NG)

        def place(half, u):
            return (half * NU + u) % 4

        block = st_.enter_context(nc.Block())
        lb, pb = loaded.base, prep.base

        @block.sync
        def _(sp):
            c.lift(sp)
            n = 0
            loads = [(wv, ins[f"{kind}_wv"])]
            if low:
                loads += [(w1[0], ins["low_rank_wq1"]), (w1[1], ins["low_rank_wk1"]), (wq, ins["low_rank_wq2"]),
                          (wk, ins["low_rank_wk2"])]
            else:
                loads += [(wq, ins[f"{kind}_wq"]), (wk, ins[f"{kind}_wk"])]
            if kind == "mha":
                loads += [(bias[:, 0:1], ins["mha_bq"]), (bias[:, 1:2], ins["mha_bk"]), (bvrow, ins["mha_bv"])]
            if kind == "rope":
                loads += [(gain, ins["rope_g"])] + [(cs[t], ins[f"rope_table{t}"]) for t in range(4)]
            for dst, src in loads:
                sp.dma_start(dst[:], src).then_inc(loaded.sem, 16)
                n += 16
            assert n == 16 * len(loads)
            with sp.Fori(0, B) as b:
                for half in range(HALVES):
                    i = b * HALVES + half
                    for u, (g, op) in enumerate(units):
                        sp.wait_ge(s3.sem, s3.at(i, u + 1))
                        rows = P // stores
                        for m in range(stores):
                            turn = b * NG + (g if low else m)
                            sp.dma_start(scr[kind][op, bass.ds(turn, 1), :, :, half * CW:(half + 1) * CW]
                                         .rearrange("o p r t -> (o r) p t"),
                                         split[place(half, u)][m * rows:(m + 1) * rows]) \
                                .then_inc(stored[place(half, u)].sem, 16)
                    sp.wait_ge(v_out.sem, v_out.at(i, CH))
                    for g in range(NG):
                        sp.dma_start(scr["v"][bass.ds((b * NG + g) * S + half * CW, CW), :].rearrange("(t p) n -> p t n", p=P),
                                     vout[half][:, :, g * HG * VC:(g + 1) * HG * VC]).then_inc(v_stored.sem, 16)
            for n in range(4):
                sp.wait_ge(stored[n].sem, stored[n].at(B, 0))
            sp.wait_ge(v_stored.sem, v_stored.at(NC_, 0))

        n_loads = {"mha": 6, "low_rank": 5, "rope": 8}[kind]

        @block.gpsimd
        def _(pool):
            pool.memset(wvp[:], 0.0).then_inc(prep.sem, 1)
            pool.memset(vrow[:], 0.0).then_inc(prep.sem, 1)
            pool.wait_ge(loaded.sem, lb + 16 * n_loads)
            pool.wait_ge(prep.sem, pb + 2)
            pool.tensor_copy(wvp[:].rearrange("p (h c) -> p h c", c=VC)[:, :, 0:8],
                             wv[:].rearrange("p (h c) -> p h c", c=8)).then_inc(prep.sem, 1)
            vr = vrow[:].rearrange("p (h c) -> p h c", c=VC)
            pool.memset(vr[:, :, 8:9], 1.0).then_inc(prep.sem, 1)
            if kind == "mha":
                pool.tensor_copy(vr[:, :, 0:8], bvrow[:].rearrange("p (h c) -> p h c", c=8)).then_inc(prep.sem, 1)
                pool.tensor_scalar(bias[:, 0:1], bias[:, 0:1], scale, None, ALU.mult).then_inc(prep.sem, 1)
            if low:
                for op in range(2):
                    for g in range(NG):
                        pool.tensor_copy(wide[op][0][:, g, :].rearrange("p (r s h) -> p r s h", r=4, s=8),
                                         w1[op][:, g * 16:g * 16 + 16].rearrange("p (h r) -> p r h", r=4).unsqueeze(2)
                                         .broadcast_to([P, 4, 8, HG])).then_inc(prep.sem, 1)
                        pool.tensor_copy(wide[op][1][:, g, :].rearrange("p (r s h) -> p r s h", r=4, s=8),
                                         (wq, wk)[op][:, g * 32:g * 32 + 32].rearrange("p (h s) -> p s h", s=8)
                                         .unsqueeze(1).broadcast_to([P, 4, 8, HG])).then_inc(prep.sem, 1)
            if kind == "rope":
                for op in range(2):
                    src = (wq, wk)[op][:].rearrange("p (g a d) -> p g a d", g=NG, a=2)
                    dst = wide[0][op][:, 0, :].rearrange("p (g a d) -> p g a d", g=NG, a=2)
                    pool.tensor_scalar(dst[:, :, 0, :], src[:, :, 1, :], -1.0, None, ALU.mult).then_inc(prep.sem, 1)
                    pool.tensor_copy(dst[:, :, 1, :], src[:, :, 0, :]).then_inc(prep.sem, 1)
            with pool.Fori(0, NC_) as i:
                roots.give(pool, c, i, 1, work[:, 6, :])
                if kind == "rope":
                    roots.give(pool, c, i, 2, work[:, 8, :])

        n_prep = {"mha": 6, "low_rank": 4 + 16, "rope": 4 + 4}[kind]

        @block.vector
        def _(dve):
            dve.wait_ge(loaded.sem, lb + 16 * n_loads)
            dve.wait_ge(prep.sem, pb + n_prep)

            def norm(i):
                ch = Chain(dve, chain, i)
                for t in range(CH):
                    ins_ = dve.bn_stats(stats[:, t, :], c.x[:, i * CH + t, :])
                ch.link(ins_)
                row_stats(dve, ch, stats, work, CH)
                roots.count = 0
                ask_root(dve, ch, roots, work[:, 6, :], work[:, 1, :], EPS_LN)
                dve.wait_ge(turned.sem, turned.at(i, 0))
                if kind == "rope":
                    for t in range(CH):
                        ins_ = dve.tensor_scalar(c.xl[:, i * CH + t, :], c.x[:, i * CH + t, :], work[:, 0, t:t + 1],
                                                 work[:, 6, t:t + 1], ALU.subtract, ALU.mult)
                    ch.link(dve.scalar_tensor_tensor(out=work[:, 7, :], in0=work[:, 6, :], scalar=1.0,
                                                     in1=work[:, 6, :], op0=ALU.mult, op1=ALU.mult))
                    ch.wait()
                    ch.link(dve.tensor_tensor(work[:, 7, :], work[:, 7, :], work[:, 1, :], ALU.mult))
                    ask_root(dve, ch, roots, work[:, 8, :], work[:, 7, :], EPS_RMS)
                    for t in range(CH):
                        ins_ = dve.tensor_scalar(xn[:, t, :], c.xl[:, i * CH + t, :], work[:, 8, t:t + 1], None, ALU.mult)
                else:
                    for t in range(CH):
                        ins_ = dve.tensor_scalar(xn[:, t, :], c.x[:, i * CH + t, :], work[:, 0, t:t + 1],
                                                 work[:, 6, t:t + 1], ALU.subtract, ALU.mult)
                ins_.then_inc(normed.sem, 1)
                assert ch.count == NCHAIN, ch.count

            def value(i, half, u):
                g, op = units[u]
                w = u % 2
                dve.wait_ge(s1.sem, s1.at(i, max(u - 1, 0)))
                dve.wait_ge(r1.sem, r1.at(i, max(u - 1, 0)))
                dve.wait_ge(a_ready.sem, a_ready.at(i, u + 1))
                if kind != "mha":
                    dve.wait_ge(first.sem, first.at(i, u + 1))
                if kind == "mha":
                    dve.tensor_scalar(val[w][:], pA[w][:], (scale, 1.0)[op], bias[:, op:op + 1], ALU.mult,
                                      ALU.add).then_inc(vals.sem, 1)
                elif low:
                    dve.tensor_tensor(val[w][:], pB[w][:], part[w][:], ALU.mult).then_inc(vals.sem, 1)
                else:
                    dve.tensor_tensor(turned_part[w][:], pB[w][:], cs[2 * op + 1][:, half * CW:(half + 1) * CW], ALU.mult)
                    dve.tensor_tensor(val[w][:], part[w][:], cs[2 * op][:, half * CW:(half + 1) * CW],
                                      ALU.mult).then_inc(dchain.sem, 1)
                    dve.wait_ge(dchain.sem, dchain.at(i, u + 1))
                    dve.tensor_tensor(val[w][:], val[w][:], turned_part[w][:], ALU.add).then_inc(vals.sem, 1)

            def units_of(i, half):
                value(i, half, 0)
                for u in range(NU + 1):
                    if u + 1 < NU:
                        value(i, half, u + 1)
                    if u < NU:
                        dve.wait_ge(s1.sem, s1.at(i, u + 1))
                        dve.wait_ge(s2.sem, s2.at(i, max(u - 1, 0)))
                        dve.wait_ge(s3.sem, s3.at(i, max(u - 1, 0)))
                        dve.tensor_tensor(rest[u % 2][:], val[u % 2][:], split[place(half, u)][:, 0, :],
                                          ALU.subtract).then_inc(r1.sem, 1)
                    if u > 0:
                        dve.wait_ge(s2.sem, s2.at(i, u))
                        dve.wait_ge(r1.sem, r1.at(i, u))
                        sp_ = split[place(half, u - 1)]
                        dve.tensor_tensor(sp_[:, 2, :], rest[(u - 1) % 2][:], sp_[:, 1, :], ALU.subtract).then_inc(s3.sem, 1)

            norm(0)
            with dve.Fori(0, B - 1) as b:
                for half in range(HALVES):
                    units_of(b * HALVES + half, half)
                    norm(b * HALVES + half + 1)
            units_of(NC_ - 2, 0)
            norm(NC_ - 1)
            units_of(NC_ - 1, 1)

        @block.tensor
        def _(pe):
            pe.wait_ge(loaded.sem, lb + 16 * n_loads)
            pe.wait_ge(prep.sem, pb + n_prep)
            with pe.Fori(0, B) as b:
                for half in range(HALVES):
                    i = b * HALVES + half
                    pe.wait_ge(normed.sem, normed.at(i, 1))
                    pe.wait_ge(xT_ready.sem, xT_ready.at(i, 0))
                    for t in range(CH):
                        ins_ = pe.transpose(pT[:, t * P:(t + 1) * P], xn[:, t, :], c.ident[:])
                    ins_.then_inc(turned.sem, 1)
                    pe.wait_ge(xT_ready.sem, xT_ready.at(i, 1))
                    for u, (g, op) in enumerate(units):
                        w = u % 2
                        pe.wait_ge(vals.sem, vals.at(i, u - 1) if u else vals.at(i, 0))
                        if low:
                            pe.matmul(pA[w][:], wide[op][0][:, g, :], xnT[:], start=True, stop=True)
                            ins_ = pe.matmul(pB[w][:], wide[op][1][:, g, :], xnT[:], start=True, stop=True)
                        elif kind == "rope":
                            pe.matmul(pA[w][:], (wq, wk)[op][:], xnT[:], start=True, stop=True)
                            ins_ = pe.matmul(pB[w][:], wide[0][op][:, 0, :], xnT[:], start=True, stop=True)
                        else:
                            ins_ = pe.matmul(pA[w][:], (wq, wk)[op][:], xnT[:], start=True, stop=True)
                        ins_.then_inc(a_ready.sem, 1)
                    for t in range(CH):
                        pe.wait_ge(v_out.sem, v_out.at(i, t - 1) if t else v_out.at(i, 0))
                        pe.matmul(pV[t % 2][:], xnT[:, t * P:(t + 1) * P], wvp[:], start=True, stop=False)
                        pe.matmul(pV[t % 2][:], c.ones[:], vrow[:], start=False, stop=True).then_inc(v_ready.sem, 1)

        @block.scalar
        def _(act):
            act.wait_ge(loaded.sem, lb + 16 * n_loads)

            def take(i, u):
                if kind != "mha":
                    act.wait_ge(a_ready.sem, a_ready.at(i, u + 1))
                    act.wait_ge(vals.sem, vals.at(i, max(u - 1, 0)))
                    act.activation(part[u % 2][:], pA[u % 2][:], ACT.Copy,
                                   scale=scale if units[u][1] == 0 else 1.0).then_inc(first.sem, 1)

            with act.Fori(0, B) as b:
                for half in range(HALVES):
                    i = b * HALVES + half
                    act.wait_ge(turned.sem, turned.at(i, 1))
                    act.wait_ge(v_ready.sem, v_ready.at(i, 0))
                    act.activation(xnT[:], pT[:], ACT.Copy, scale=gain[:] if kind == "rope" else 1.0).then_inc(xT_ready.sem, 1)
                    take(i, 0)
                    for u in range(NU + 1):
                        if u + 1 < NU:
                            take(i, u + 1)
                        if u < NU:
                            act.wait_ge(vals.sem, vals.at(i, u + 1))
                            n = place(half, u)
                            act.wait_ge(stored[n].sem, stored[n].at(b, 16 * stores * ((half * NU + u) // 4)))
                            act.activation(split[n][:, 0, :], val[u % 2][:], ACT.Copy).then_inc(s1.sem, 1)
                        if u > 0:
                            act.wait_ge(r1.sem, r1.at(i, u))
                            act.activation(split[place(half, u - 1)][:, 1, :], rest[(u - 1) % 2][:], ACT.Copy).then_inc(s2.sem, 1)
                    act.wait_ge(v_stored.sem, v_stored.at(i, 0))
                    for t in range(CH):
                        act.wait_ge(v_ready.sem, v_ready.at(i, t + 1))
                        act.activation(vout[half][:, t, :], pV[t % 2][:], ACT.Copy).then_inc(v_out.sem, 1)

        loaded.base += 16 * n_loads
        prep.base += n_prep
        for s in (chain, normed, turned, xT_ready, a_ready, vals, s1, r1, s2, s3, v_ready, v_out, v_stored):
            s.end(NC_)
        for s in stored:
            s.end(B)
        roots.end(NC_)
        if kind != "mha":
            first.end(NC_)
        if kind == "rope":
            dchain.end(NC_)


NINE = (tuple(((m + m // 3) % 3, m % 3) for m in range(9)),)
SIX = (((0, 0), (0, 1), (1, 0)), ((0, 2), (1, 1), (2, 0)))


def runs(parts):
    out = []
    for place, part in enumerate(parts):
        if out and part == out[-1][1] + out[-1][2]:
            out[-1][2] += 1
        else:
            out.append([place, part, 1])
    return out


def attend(c, kind, scr):
    nc = c.nc
    low = kind == "low_rank"
    dk = 32 if low else 8
    slots = SIX if low else NINE
    passes = len(slots)
    rows = len(slots[0]) * dk
    TURNS = B * NG
    pieces = []
    for h in range(HG):
        for qt in range(TB):
            if qt < CH:
                pieces.append((h, qt, qt, 0, (qt + 1) * P))
            else:
                pieces.append((h, qt, qt, 0, CW))
                pieces.append((h, qt + CH, qt, CW, (qt + 1) * P))
    NPIECE = len(pieces)
    steps = [(qc, kt, hp) for qc in range(HALVES) for kt in range(CH * (qc + 1)) for hp in range(HG // 2)]
    NS = len(steps)
    START, AHEAD = 4, 3
    LAST0 = 2 * CH - 1
    TURN0 = LAST0 + 4
    PEAK = START + NPIECE // AHEAD
    with ExitStack() as st_:
        def sb(name, shape, dt=FP32):
            return st_.enter_context(nc.sbuf_tensor(f"{name}_{kind}", shape, dt))

        def ps(name, shape, dt=FP32):
            return st_.enter_context(nc.psum_tensor(f"{name}_{kind}", shape, dt))

        q = [sb(f"q{n}", [rows + 2, passes, HG, S], BF16) for n in range(2)]
        k = [sb(f"k{n}", [rows + 2, passes, HG, S], BF16) for n in range(2)]
        v = [sb(f"v{n}", [P, TB, HG * VC]) for n in range(2)]
        peaks = sb("peaks", [P, HG, TB + CH])
        peak = sb("peak", [P, HG, TB])
        npk = sb("npk", [P, 4, HG * TB], BF16)
        npkT = sb("npkT", [2 * HG * TB, P], BF16)
        prob = [sb(f"prob{n}", [P, 2, CW]) for n in range(4)]
        outT = [sb(f"outT{n}", [P, CW]) for n in range(2)]
        rec = sb("rec", [P, CH, HG])
        s1 = [ps(f"s1_{n}", [P, CW]) for n in range(2)]
        s2 = [ps(f"s2_{n}", [P, 2, CW]) for n in range(2)]
        o = ps("o", [P, CW])
        m = ps("m", [P, CH, HG * VC])
        mb = m[:].rearrange("p a b -> p (a b)").bitcast(BF16)[:, 0:P]

        ones_set = c.new_signal("ones_set", 0)
        NL = 16 * (1 + sum(len(runs([s[op] for s in slots[r]])) for op in range(2) for r in range(passes)))
        loaded = [c.new_signal(f"stack_loaded{n}", NL) for n in range(2)]
        peak_in = [c.new_signal(f"peak_rows{n}", 32) for n in range(2)]
        scored = c.new_signal("scored", NPIECE)
        peaked = c.new_signal("peaked", NPIECE)
        pchain = c.new_signal("peak_chain", 2)
        negated = c.new_signal("negated", 1)
        peak_T = c.new_signal("peak_turned", 1)
        peak_c = c.new_signal("peak_copied", 1)
        s_ready = c.new_signal("s_ready", NS)
        exped = c.new_signal("exped", NS)
        pv = c.new_signal("pv_done", NS)
        o_copied = c.new_signal("o_copied", HALVES)
        o_turned = c.new_signal("o_turned", HALVES)
        rchain = c.new_signal("rec_chain", HALVES)
        o_out = c.new_signal("o_normalized", HALVES)
        block = st_.enter_context(nc.Block())
        ones_base = ones_set.base

        def turns(eng, ahead, body):
            ahead(0, 0, 0)
            with eng.Fori(0, TURNS // 2 - 1) as i:
                for w in range(2):
                    body(2 * i + w, w, i, True)
            body(TURNS - 2, 0, TURNS // 2 - 1, True)
            body(TURNS - 1, 1, TURNS // 2 - 1, False)

        def next_set(w, idx):
            return 1 - w, idx + w

        @block.sync
        def _(sp):
            c.lift(sp)

            def load(n, w):
                if not (isinstance(n, int) and n <= 1):
                    sp.wait_ge(s_ready.sem, s_ready.at(n - 1, 0))
                for op, dst in ((0, q[w]), (1, k[w])):
                    for r in range(passes):
                        for place, part, length in runs([s[op] for s in slots[r]]):
                            src = scr[kind][op, bass.ds(n, 1), part:part + length] \
                                .rearrange("o p (d h) t -> (o p d) h t", h=HG)
                            sp.dma_start(dst[place * dk:(place + length) * dk, r, :, :], src).then_inc(loaded[w].sem, 16)
                if not (isinstance(n, int) and n <= 1):
                    sp.wait_ge(pv.sem, pv.at(n - 1, 0))
                sp.dma_start(v[w][:], scr["v"][bass.ds(n * S, S), :].rearrange("(t p) n -> p t n", p=P)) \
                    .then_inc(loaded[w].sem, 16)

            def peak_rows(n, w, idx):
                sp.wait_ge(peak_c.sem, peak_c.at(n, 1))
                for part in range(2):
                    sp.dma_start(q[w][rows + part:rows + part + 1, passes - 1, :, :],
                                 npkT[part * HG * TB:(part + 1) * HG * TB, :]).then_inc(peak_in[w].sem, 16)

            def body(n, w, idx, more):
                if more:
                    w1, idx1 = next_set(w, idx)
                    load(n + 1, w1)
                    peak_rows(n + 1, w1, idx1)

            sp.wait_ge(ones_set.sem, ones_base + 1)
            load(0, 0)
            sp.wait_ge(ones_set.sem, ones_base + 2)
            turns(sp, peak_rows, body)
            for w in range(2):
                sp.wait_ge(peak_in[w].sem, peak_in[w].at(TURNS // 2, 0))

        @block.gpsimd
        def _(pool):
            for w in range(2):
                pool.memset(k[w][rows // 32 * 32:rows + 2, passes - 1], 1.0).then_inc(ones_set.sem, 1)
            pool.wait_ge(ones_set.sem, ones_base + 2)
            pool.memset(npk[:], 0.0).then_inc(ones_set.sem, 1)

        @block.tensor
        def _(pe):
            def piece(n, w, idx, j):
                h, place, qt, k0, k1 = pieces[j]
                if j == 0:
                    pe.wait_ge(loaded[w].sem, loaded[w].at(idx, NL))
                pe.wait_ge(peaked.sem, peaked.at(n, max(j - 1, 0)))
                diag = k1 == (qt + 1) * P
                dst = s1[j % 2]
                for r in range(passes):
                    ins_ = pe.matmul(dst[:, 0:k1 - k0], q[w][0:rows, r, h, qt * P:(qt + 1) * P], k[w][0:rows, r, h, k0:k1],
                                     start=r == 0, stop=r == passes - 1 and not diag)
                if diag:
                    ins_ = pe.matmul(dst[:, k1 - k0 - P:k1 - k0], c.identb[:], c.mask_k[:], start=False, stop=True)
                ins_.then_inc(scored.sem, 1)

            def turn_peaks(n):
                pe.wait_ge(negated.sem, negated.at(n, 1))
                pe.transpose(mb, npk[:].rearrange("p a b -> p (a b)"), c.identb[:]).then_inc(peak_T.sem, 1)

            def ahead(n, w, idx):
                for j in range(NPIECE):
                    piece(n, w, idx, j)
                turn_peaks(n)
                for s in range(2):
                    score(n, w, idx, s)

            def score(n, w, idx, s, between=None):
                qc, kt, hp = steps[s]
                if s == 0:
                    pe.wait_ge(peak_in[w].sem, peak_in[w].at(idx, 32))
                off = max(kt * P - qc * CW, 0)
                diag = kt >= qc * CH
                for j in range(2):
                    if between:
                        between(j)
                    if j == 0:
                        pe.wait_ge(exped.sem, exped.at(n, max(s - 1, 0)))
                    h = 2 * hp + j
                    for r in range(passes):
                        kr = rows + 2 if r == passes - 1 else rows
                        ins_ = pe.matmul(s2[s % 2][:, j, off:CW], k[w][0:kr, r, h, kt * P:(kt + 1) * P],
                                         q[w][0:kr, r, h, qc * CW + off:(qc + 1) * CW], start=r == 0,
                                         stop=r == passes - 1 and not diag)
                    if diag:
                        ins_ = pe.matmul(s2[s % 2][:, j, off:off + P], c.identb[:], c.mask_q[:], start=False, stop=True)
                ins_.then_inc(s_ready.sem, 1)
                if between:
                    between(2)

            def mix(n, w, s):
                pe.wait_ge(exped.sem, exped.at(n, s + 2))
                qc, kt, _ = steps[s]
                off = max(kt * P - qc * CW, 0)
                if kt == 0:
                    pe.wait_ge(o_copied.sem, o_copied.at(n, qc))
                for h in range(HG):
                    ins_ = pe.matmul(o[h * VC:(h + 1) * VC, off:CW], v[w][:, kt, h * VC:(h + 1) * VC],
                                     prob[(s + h // 2) % 4][:, h % 2, off:CW], start=kt == 0, stop=kt == CH * (qc + 1) - 1)
                    if h % 2:
                        ins_.then_inc(pv.sem, 1)

            def turn_out(n, qc, more):
                pe.wait_ge(o_copied.sem, o_copied.at(n, qc + 1))
                pe.wait_ge(o_out.sem, o_out.at(n, qc))
                if more:
                    pe.wait_ge(peak_c.sem, peak_c.at(n, 1 + qc))
                for t in range(CH):
                    ins_ = pe.transpose(m[:, t, :], outT[qc][:, t * P:(t + 1) * P], c.ident[:])
                ins_.then_inc(o_turned.sem, 1)

            def body(n, w, idx, more):
                w1, idx1 = next_set(w, idx)
                for s in range(2, NS):
                    between = None
                    if more and START <= s < PEAK:
                        def between(j, s=s):
                            piece(n + 1, w1, idx1, (s - START) * AHEAD + j)
                    score(n, w, idx, s, between)
                    if s % 2:
                        mix(n, w, s - 3)
                    if s == TURN0:
                        turn_out(n, 0, more)
                    if s == PEAK and more:
                        pe.wait_ge(o_out.sem, o_out.at(n, 1))
                        turn_peaks(n + 1)
                if more:
                    for s in range(2):
                        score(n + 1, w1, idx1, s)
                mix(n, w, NS - 2)
                turn_out(n, 1, more)

            turns(pe, ahead, body)

        @block.vector
        def _(dve):
            def piece(n, j):
                h, place, qt, k0, k1 = pieces[j]
                if j == 0:
                    dve.wait_ge(negated.sem, negated.at(n, 0))
                dve.wait_ge(scored.sem, scored.at(n, j + 1))
                dve.reduce_max(peaks[:, h, place:place + 1], s1[j % 2][:, 0:k1 - k0], AX.X).then_inc(peaked.sem, 1)

            def negate(n):
                ch = Chain(dve, pchain, n)
                dve.wait_ge(peaked.sem, peaked.at(n, NPIECE))
                dve.tensor_copy(peak[:, :, 0:CH], peaks[:, :, 0:CH])
                ch.link(dve.tensor_tensor(peak[:, :, CH:TB], peaks[:, :, CH:TB], peaks[:, :, TB:TB + CH], ALU.max))
                ch.wait()
                dve.wait_ge(ones_set.sem, ones_base + 3)
                dve.wait_ge(peak_T.sem, peak_T.at(n, 0))
                ch.link(dve.tensor_scalar(npk[:, 0, :], peak[:].rearrange("p h t -> p (h t)"), -1.0, None, ALU.mult))
                ch.wait()
                dve.scalar_tensor_tensor(out=npk[:, 1, :], in0=peak[:].rearrange("p h t -> p (h t)"), scalar=-1.0,
                                         in1=npk[:, 0, :], op0=ALU.mult, op1=ALU.subtract).then_inc(negated.sem, 1)

            def ahead(n, w, idx):
                for j in range(NPIECE):
                    piece(n, j)
                negate(n)

            def normalize(n, qc):
                dve.wait_ge(o_turned.sem, o_turned.at(n, qc + 1))
                mv = m[:].rearrange("p t (h c) -> p t h c", c=VC)
                dve.reciprocal(rec[:], mv[:, :, :, 8]).then_inc(rchain.sem, 1)
                dve.wait_ge(rchain.sem, rchain.at(n, qc + 1))
                dve.tensor_tensor(c.heads_out[:, n, qc * CH:(qc + 1) * CH, :].rearrange("p t (h d) -> p t h d", h=HG),
                                  mv[:, :, :, 0:8], rec[:].unsqueeze(3).broadcast_to([P, CH, HG, 8]), ALU.mult) \
                    .then_inc(o_out.sem, 1)

            def body(n, w, idx, more):
                for s in range(NS):
                    if more and START <= s < PEAK:
                        for j in range((s - START) * AHEAD, (s - START + 1) * AHEAD):
                            piece(n + 1, j)
                    if s == TURN0:
                        normalize(n, 0)
                    if s == PEAK and more:
                        negate(n + 1)
                normalize(n, 1)

            turns(dve, ahead, body)

        @block.scalar
        def _(act):
            def copy_peaks(n, w):
                act.wait_ge(peak_T.sem, peak_T.at(n, 1))
                act.activation(npkT[:], mb[0:2 * HG * TB, :], ACT.Copy).then_inc(peak_c.sem, 1)

            def ahead(n, w, idx):
                copy_peaks(n, w)

            def copy_out(n, qc):
                act.wait_ge(pv.sem, pv.at(n, LAST0 + 1 if qc == 0 else NS))
                act.wait_ge(o_turned.sem, o_turned.at(n, qc))
                act.activation(outT[qc][:], o[:], ACT.Copy).then_inc(o_copied.sem, 1)

            def body(n, w, idx, more):
                for s in range(NS):
                    qc, kt, hp = steps[s]
                    off = max(kt * P - qc * CW, 0)
                    act.wait_ge(s_ready.sem, s_ready.at(n, s + 1))
                    act.wait_ge(pv.sem, pv.at(n, max(s - 3, 0)))
                    act.activation(prob[s % 4][:, :, off:CW], s2[s % 2][:, :, off:CW], ACT.Exp).then_inc(exped.sem, 1)
                    if s == LAST0 + 2:
                        copy_out(n, 0)
                    if s == PEAK and more:
                        act.wait_ge(peak_in[w].sem, peak_in[w].at(idx, 32))
                        copy_peaks(n + 1, w)
                copy_out(n, 1)

            act.preload_act_table(ACT.Exp)
            turns(act, ahead, body)

        ones_set.base += 3
        for w in range(2):
            loaded[w].end(TURNS // 2)
            peak_in[w].end(TURNS // 2)
        for s in (scored, peaked, pchain, negated, peak_T, peak_c, s_ready, exped, pv, o_copied, o_turned, rchain, o_out):
            s.end(TURNS)


def post(c, kind):
    nc, ins = c.nc, c.ins
    NCHAIN = 5
    last = kind == "rope"
    with ExitStack() as st_:
        def sb(name, shape, dt=FP32):
            return st_.enter_context(nc.sbuf_tensor(f"{name}_post_{kind}", shape, dt))

        def ps(name, shape, dt=FP32):
            return st_.enter_context(nc.psum_tensor(f"{name}_post_{kind}", shape, dt))

        wo = sb("wo", [P, D])
        bo = sb("bo", [1, D])
        hs = sb("hs", [P, CH, D])
        hT = sb("hT", [P, CW])
        y = sb("y", [P, CH, D])
        stats = sb("stats", [P, CH, 6])
        work = sb("work", [P, 9, CH])
        pT = ps("pT", [P, CW])
        pO = [ps(f"pO{n}", [P, CH, D]) for n in range(2)]
        loaded = c.new_signal("wo_loaded", 0)
        lb = loaded.base
        gathered = c.new_signal("heads_gathered", 1)
        turned = c.new_signal("heads_turned", 1)
        hT_ready = c.new_signal("hT_ready", 1)
        wo_done = c.new_signal("wo_done", 1)
        chain = c.new_signal("post_chain", NCHAIN)
        roots = Roots(c, 1)
        added = c.new_signal("post_added", 1)
        block = st_.enter_context(nc.Block())

        @block.sync
        def _(sp):
            c.lift(sp)
            sp.dma_start(wo[:], ins[f"{kind}_wo"]).then_inc(loaded.sem, 16)
            if not last:
                sp.dma_start(bo[:], ins[f"{kind}_bo"]).then_inc(loaded.sem, 16)

        nl = 16 if last else 32

        if not last:
            @block.gpsimd
            def _(pool):
                with pool.Fori(0, NC_) as i:
                    roots.give(pool, c, i, 1, work[:, 6, :])

        @block.scalar
        def _(act):
            with act.Fori(0, B) as b:
                for half in range(HALVES):
                    i = b * HALVES + half
                    act.wait_ge(turned.sem, turned.at(i, 0))
                    act.activation(hs[:].rearrange("p t (g d) -> p g t d", g=NG),
                                   c.heads_out[:, bass.ds(b * NG, NG), half * CH:(half + 1) * CH, :], ACT.Copy) \
                        .then_inc(gathered.sem, 1)
                    act.wait_ge(turned.sem, turned.at(i, 1))
                    act.wait_ge(wo_done.sem, wo_done.at(i, 0))
                    act.activation(hT[:], pT[:], ACT.Copy).then_inc(hT_ready.sem, 1)

        @block.tensor
        def _(pe):
            pe.wait_ge(loaded.sem, lb + nl)
            with pe.Fori(0, B) as b:
                for half in range(HALVES):
                    i = b * HALVES + half
                    pe.wait_ge(gathered.sem, gathered.at(i, 1))
                    pe.wait_ge(hT_ready.sem, hT_ready.at(i, 0))
                    for t in range(CH):
                        ins_ = pe.transpose(pT[:, t * P:(t + 1) * P], hs[:, t, :], c.ident[:])
                    ins_.then_inc(turned.sem, 1)
                    pe.wait_ge(hT_ready.sem, hT_ready.at(i, 1))
                    pe.wait_ge(added.sem, added.at(i, 0))
                    for t in range(CH):
                        ins_ = pe.matmul(pO[half][:, t, :], hT[:, t * P:(t + 1) * P], wo[:], start=True, stop=last)
                        if not last:
                            ins_ = pe.matmul(pO[half][:, t, :], c.ones[:], bo[:], start=False, stop=True)
                    ins_.then_inc(wo_done.sem, 1)

        @block.vector
        def _(dve):
            with dve.Fori(0, B) as b:
                for half in range(HALVES):
                    i = b * HALVES + half
                    dve.wait_ge(wo_done.sem, wo_done.at(i, 1))
                    if last:
                        xl = c.xl[:, bass.ds(i * CH, CH), :]
                        dve.tensor_tensor(xl, pO[half][:], xl, ALU.add).then_inc(added.sem, 1)
                        continue
                    layernorm_add(dve, Chain(dve, chain, i), roots, pO[half], y, stats, work, c.x, i, added)

        loaded.base += nl
        for s in (gathered, turned, hT_ready, wo_done, added):
            s.end(NC_)
        if not last:
            chain.end(NC_)
            roots.end(NC_)


def layernorm_add(dve, ch, roots, src, y, stats, work, x, i, added, more=False):
    for t in range(CH):
        ins_ = dve.bn_stats(stats[:, t, :], src[:, t, :])
    ch.link(ins_)
    row_stats(dve, ch, stats, work, CH)
    if not more:
        roots.count = 0
    ask_root(dve, ch, roots, work[:, 6, :], work[:, 1, :], EPS_LN)
    for t in range(CH):
        ins_ = dve.tensor_scalar(y[:, t, :], src[:, t, :], work[:, 0, t:t + 1], work[:, 6, t:t + 1], ALU.subtract, ALU.mult)
    ch.link(ins_)
    ch.wait()
    rows = x[:, bass.ds(i * CH, CH), :]
    dve.tensor_tensor(rows, rows, y[:], ALU.add).then_inc(added.sem, 1)


DEPTH = 6
WIN = 32
NWT = P // WIN
DH = 64
HP = H // 2
NF = 3
QKC = 4


def enter_local(c, xw):
    nc = c.nc
    with ExitStack() as st_:
        def sb(name, shape, dt=FP32):
            return st_.enter_context(nc.sbuf_tensor(f"{name}_enter", shape, dt))

        stats, work = sb("stats", [P, CH, 6]), sb("work", [P, 9, CH])
        chain, roots = c.new_signal("enter_chain", 4), Roots(c, 1)
        block = st_.enter_context(nc.Block())

        @block.gpsimd
        def _(pool):
            c.lift(pool)
            with pool.Fori(0, NC_) as i:
                roots.give(pool, c, i, 1, work[:, 6, :])

        @block.vector
        def _(dve):
            with dve.Fori(0, B) as b:
                for half in range(HALVES):
                    i = b * HALVES + half
                    ch = Chain(dve, chain, i)
                    for t in range(CH):
                        ins_ = dve.bn_stats(stats[:, t, :], c.x[:, i * CH + t, :])
                    ch.link(ins_)
                    row_stats(dve, ch, stats, work, CH)
                    roots.count = 0
                    ask_root(dve, ch, roots, work[:, 6, :], work[:, 1, :], EPS_LN)
                    for t in range(CH):
                        dve.tensor_scalar(xw[:, b * (TB + 1) + (1 + half * CH + t), :], c.x[:, i * CH + t, :],
                                          work[:, 0, t:t + 1], work[:, 6, t:t + 1], ALU.subtract, ALU.mult)

        chain.end(NC_)
        roots.end(NC_)


def leave_local(c, xw):
    nc = c.nc
    with ExitStack() as st_:
        def sb(name, shape, dt=FP32):
            return st_.enter_context(nc.sbuf_tensor(f"{name}_leave", shape, dt))

        stats, work, y = sb("stats", [P, CH, 6]), sb("work", [P, 9, CH]), sb("y", [P, CH, D])
        chain, roots, added = c.new_signal("leave_chain", 5), Roots(c, 1), c.new_signal("leave_added", 1)
        block = st_.enter_context(nc.Block())

        @block.gpsimd
        def _(pool):
            c.lift(pool)
            with pool.Fori(0, NC_) as i:
                roots.give(pool, c, i, 1, work[:, 6, :])

        @block.vector
        def _(dve):
            with dve.Fori(0, B) as b:
                for half in range(HALVES):
                    i = b * HALVES + half
                    layernorm_add(dve, Chain(dve, chain, i), roots, xw[:, bass.ds(b * (TB + 1) + (1 + half * CH), CH), :], y,
                                  stats, work, c.x, i, added)

        chain.end(NC_)
        roots.end(NC_)
        added.end(NC_)


def local_stack(c, xw, x1w):
    nc, ins = c.nc, c.ins
    with ExitStack() as st_:
        def sb(name, shape, dt=FP32):
            return st_.enter_context(nc.sbuf_tensor(f"{name}_local", shape, dt))

        def ps(name, shape, dt=FP32):
            return st_.enter_context(nc.psum_tensor(f"{name}_local", shape, dt))

        wqkv = sb("wqkv", [P, 3 * H * DH])
        wo = sb("wo", [P, HP, D])
        w1 = sb("w1", [P, 2, NF * P])
        w2 = sb("w2", [P, NF, D])
        b1 = sb("b1", [P, 2, NF])
        b2 = sb("b2", [1, D])
        gain, shift_ = sb("gain", [P, 1]), sb("shift", [P, 1])
        qks = sb("qks", [P, 2, DH])
        base = [sb(f"base{n}", [P, TB, DH]) for n in range(4)]
        tab = sb("tab", [P, TB, 5, DH])
        cur = sb("cur", [P, 5, DH])
        mask = sb("mask", [P, TB, DH], BF16)
        down1 = sb("down1", [P, P])
        last1 = sb("last1", [P, P])
        xin = sb("xin", [P, 2, D])
        xsT = sb("xsT", [P, WIN + P])
        raw = sb("raw", [P, QKC, CW])
        sq = sb("sq", [P, QKC, CW])
        rot = sb("rot", [P, QKC, CW])
        qk = sb("qk", [P, QKC, CW])
        ssq = sb("ssq", [P, 2 * H])
        inv = sb("inv", [P, 2 * H])
        qT = sb("qT", [P, HP, P])
        kT = sb("kT", [P, HP, WIN + P])
        pr = sb("pr", [P, HP, 2, DH])
        mx, tot = sb("mx", [P, H]), sb("tot", [P, H])
        PT = sb("PT", [P, HP, P])
        v2 = sb("v2", [P, NWT, HP * DH])
        att = sb("att", [P, H * DH])
        aoT = sb("aoT", [P, HP, P])
        xs1, xn1, xnT = sb("xs1", [P, 1, D]), sb("xn1", [P, D]), sb("xnT", [P, P])
        stats, work = sb("stats", [P, 1, 6]), sb("work", [P, 9, 1])
        gl, hid = sb("gl", [P, NF, P]), sb("hid", [P, NF, P])
        turn_table = sb("turn_table", [1, 1])
        pA = [ps(f"pA{n}", [P, CW]) for n in range(2)]
        pS = ps("pS", [P, 2, HP, DH])
        xs_in = pS[:, 0].rearrange("p b d -> p (b d)")[:, 0:P]
        pT = [ps(f"pT{n}", [P, CH, P]) for n in range(2)]
        pC = [ps(f"pC{n}", [P, CH, P]) for n in range(2)]

        G = lambda n, k=1: c.new_signal(n, k)
        base_in, made = G("local_tables", 0), G("local_made", 0)
        NWL = 16 * 10
        wts, tabs = G("layer_weights", NWL), G("layer_tables", 6)
        xin_ready, xs_built, xtail, xsT_ready = G("xin_ready"), G("xs_built"), G("xtail"), G("xsT_ready")
        qk_done, raw_ready, sq_ready, rot_ready = G("qk_done", QKC), G("raw_ready", QKC), G("sq_ready", QKC), G("rot_ready", QKC)
        cur_ready = G("cur_ready")
        u_ready, added_rot, summed = G("u_ready", QKC), G("rot_added", 1), G("ssq_summed", 2)
        qroots, qk_ready = Roots2(c, "qk_root"), G("qk_ready", 2)
        t_done, t_copied, ktail = G("qkT_done", 4), G("qkT_copied", 4), G("ktail")
        s_done, mxd, sub_ready, exp_ready, totd, inv_ready = (G("ls_done"), G("ls_max", 2), G("ls_sub", 2), G("ls_exp", 2), G("ls_sum"),
                                                              G("ls_inv"))
        PT_done, PT_ready, pv_done, att_ready = G("PT_done", 2), G("PT_ready", 2), G("lpv_done"), G("att_ready", 2)
        aT_done, aoT_ready = G("attT_done", 2), G("aoT_ready", 2)
        v_done, v_ready = G("v2_done", NWT), G("v2_ready", NWT)
        wo_done, x1_ready, sh_done, n_ready, nT_done, xnT_ready = (G("lwo_done"), G("x1_ready"), G("shifted"), G("n_ready"),
                                                                   G("nT_done"), G("lxnT_ready"))
        cchain, croots = G("ffn_chain", 5), Roots2(c, "ffn_root")
        w1_done, gl_ready, h_ready, w2_done, x2_done = G("w1_done"), G("gelu_ready"), G("hidden_ready"), G("w2_done"), G("x2_done")
        block = st_.enter_context(nc.Block())
        mb = made.base

        def layers(eng, start, body):
            with eng.Fori(0, DEPTH) as L:
                start(L)
                n = L * NT
                body(n, 0, None, None)
                body(n, 1, 0, None)
                with eng.Fori(2, NT - 1) as t:
                    body(n, t, t - 1, t - 2)
                body(n, NT - 1, NT - 2, NT - 3)
                body(n, None, NT - 1, NT - 2)
                body(n, None, None, NT - 1)

        def row(t):
            return t + t // TB + 1

        def wait_layer(eng, L):
            eng.wait_ge(wts.sem, wts.at(L, NWL))

        @block.sync
        def _(sp):
            c.lift(sp)
            for n in range(4):
                sp.dma_start(base[n][:], ins[f"local_table{n}"].rearrange("(t p) d -> p t d", p=P)).then_inc(base_in.sem, 16)
            sp.wait_ge(base_in.sem, base_in.base + 64)
            with sp.Fori(0, DEPTH) as L:
                sp.wait_ge(x2_done.sem, x2_done.at(L * NT, 0))
                one = bass.ds(L, 1)
                for dst, src in ((wqkv[:], ins["local_wqkv"][one].rearrange("o p n -> (o p) n")),
                                 (wo[:], ins["local_wo"][one].rearrange("o (c p) n -> p (o c) n", p=P)),
                                 (w1[:], ins["local_w1"][one].rearrange("o p a n -> (o p) a n")),
                                 (w2[:], ins["local_w2"][one].rearrange("o (c p) n -> p (o c) n", p=P)),
                                 (b1[:], ins["local_b1"][one].rearrange("o p a n -> (o p) a n")),
                                 (b2[:], ins["local_b2"][one]),
                                 (gain[:], ins["local_g"][one].rearrange("o p n -> (o p) n")),
                                 (shift_[:], ins["local_b"][one].rearrange("o p n -> (o p) n")),
                                 (qks[:, 0, :], ins["local_qs"][one].broadcast_to([P, DH])),
                                 (qks[:, 1, :], ins["local_ks"][one].broadcast_to([P, DH]))):
                    sp.dma_start(dst, src).then_inc(wts.sem, 16)

        @block.gpsimd
        def _(pool):
            pool.memset(mask[:], 0.0).then_inc(made.sem, 1)
            for m in (down1, last1):
                pool.memset(m[:], 0.0).then_inc(made.sem, 1)
            pool.memset(xsT[:], 0.0).then_inc(made.sem, 1)
            pool.memset(kT[:], 0.0).then_inc(made.sem, 1)
            pool.memset(tab[:, 0, 4, :], 0.0).then_inc(made.sem, 1)
            pool.memset(tab[:, 1:TB, 4, :], 1.0).then_inc(made.sem, 1)
            done = 7

            def select(m, fill, op, base_, pattern, slope):
                nonlocal done
                pool.wait_ge(made.sem, mb + done)
                pool.affine_select(out=m, in_=m, compare_op=op, fill=fill, base=base_, pattern=pattern,
                                   channel_multiplier=slope).then_inc(made.sem, 1)
                done += 1

            select(down1[:], 1.0, ALU.not_equal, 1, [[-1, P]], 1)
            select(last1[:], 1.0, ALU.not_equal, -(P - 1), [[-1, P]], 1)
            for w in range(NWT):
                part = mask[w * WIN:(w + 1) * WIN]
                select(part, NEG, ALU.is_ge, 0, [[0, TB], [1, DH]], -1)
                select(part, NEG, ALU.is_ge, WIN, [[0, TB], [-1, DH]], 1)
            pool.wait_ge(made.sem, mb + done)
            pool.memset(mask[0:WIN, 0, 0:WIN], NEG).then_inc(made.sem, 1)
            assert done == 17

            def start(L):
                pool.wait_ge(tabs.sem, tabs.at(L, 6))

            def body(n, ta, tb, tc):
                if ta is not None:
                    pool.wait_ge(v_done.sem, v_done.at(n + ta, 0))
                    pool.tensor_tensor(xsT[:, 0:WIN], xsT[:, P:P + WIN], c.one[:, 0:WIN], ALU.mult).then_inc(xtail.sem, 1)
                for j in range(QKC):
                    if ta is not None:
                        pool.wait_ge(raw_ready.sem, raw_ready.at(n + ta, j + 1))
                        if j == 0:
                            pool.wait_ge(added_rot.sem, added_rot.at(n + ta, 0))
                            pool.wait_ge(cur_ready.sem, cur_ready.at(n + ta, 1))
                        rw = raw[:, j, :].rearrange("p (h d) -> p h d", d=DH)
                        ro = rot[:, j, :].rearrange("p (h d) -> p h d", d=DH)
                        half = DH // 2
                        for a in range(2):
                            tb_ = cur[:, 2 * (j // 2) + 1, a * half:(a + 1) * half].unsqueeze(1) \
                                .broadcast_to([P, CW // DH, half])
                            ins_ = pool.tensor_tensor(ro[:, :, a * half:(a + 1) * half],
                                                      rw[:, :, (1 - a) * half:(2 - a) * half], tb_, ALU.mult)
                        ins_.then_inc(rot_ready.sem, 1)
                    if j == 0 and tc is not None:
                        croots.give(pool, c, n + tc, work[:, 6, :])
                if ta is not None:
                    qroots.give(pool, c, n + ta, inv[:])
                    pool.wait_ge(s_done.sem, s_done.at(n + ta, 0))
                    pool.tensor_tensor(kT[:, :, 0:WIN], kT[:, :, P:P + WIN],
                                       cur[:, 4, 0:WIN].unsqueeze(1).broadcast_to([P, HP, WIN]), ALU.mult).then_inc(ktail.sem, 1)

            layers(pool, start, body)

        @block.tensor
        def _(pe):
            pe.wait_ge(made.sem, mb + 18)

            def start(L):
                wait_layer(pe, L)

            def project_qk(n, t, j):
                if j == 0:
                    pe.wait_ge(xsT_ready.sem, xsT_ready.at(n + t, 1))
                    pe.wait_ge(v_ready.sem, v_ready.at(n + t, 0))
                elif j >= 2:
                    pe.wait_ge(u_ready.sem, u_ready.at(n + t, j - 1))
                    pe.wait_ge(sq_ready.sem, sq_ready.at(n + t, j - 1))
                pe.matmul(pA[(j + 1) % 2][:], xsT[:, WIN:WIN + P], wqkv[:, j * CW:(j + 1) * CW], start=True, stop=True) \
                    .then_inc(qk_done.sem, 1)

            def turn_qk(n, t, g):
                if g < 2:
                    pe.wait_ge(aoT_ready.sem, aoT_ready.at(n + t, 0))
                else:
                    pe.wait_ge(t_copied.sem, t_copied.at(n + t, g - 1))
                if g % 2 == 0:
                    pe.wait_ge(qk_ready.sem, qk_ready.at(n + t, g // 2 + 1))
                src = qk[:, 2 * (g // 2):2 * (g // 2) + 2, :].rearrange("p a (b d) -> p (a b) d", d=P)
                for p in range(4):
                    ins_ = pe.transpose(pT[g % 2][:, p, :], src[:, 4 * (g % 2) + p, :], c.ident[:])
                ins_.then_inc(t_done.sem, 1)

            def scores(g):
                for p in range(4 * g, 4 * g + 4):
                    for w in range(NWT):
                        for a in range(2):
                            lo = a * DH
                            ins_ = pe.matmul(pS[w * WIN:(w + 1) * WIN, a, p, :], qT[lo:lo + DH, p, w * WIN:(w + 1) * WIN],
                                             kT[lo:lo + DH, p, w * WIN:w * WIN + DH], start=False,
                                             stop=True, skip_group_check=True)
                return ins_

            def mix(g):
                for p in range(4 * g, 4 * g + 4):
                    for w in range(NWT):
                        for a in range(2):
                            lo = a * DH
                            ins_ = pe.matmul(pS[w * WIN:(w + 1) * WIN, a, p, :], PT[lo:lo + DH, p, w * WIN:(w + 1) * WIN],
                                             v2[lo:lo + DH, w, p * DH:(p + 1) * DH], start=True, stop=True)
                return ins_

            def values(n, t, w):
                wv = wqkv[:, 2 * H * DH:3 * H * DH].rearrange("p (b a d) -> p a b d", a=2, d=DH)
                if w < 2:
                    pe.wait_ge(u_ready.sem, u_ready.at(n + t, 3 + w))
                    pe.wait_ge(sq_ready.sem, sq_ready.at(n + t, 3 + w))
                else:
                    pe.wait_ge(v_ready.sem, v_ready.at(n + t, w - 1))
                for a in range(2):
                    ins_ = pe.matmul(pA[(w + 1) % 2][a * DH:(a + 1) * DH, :], xsT[:, w * WIN:w * WIN + DH], wv[:, a],
                                     start=True, stop=True)
                ins_.then_inc(v_done.sem, 1)

            def body(n, ta, tb, tc):
                if ta is not None:
                    pe.wait_ge(xin_ready.sem, xin_ready.at(n + ta, 1))
                    pe.wait_ge(att_ready.sem, att_ready.at(n + ta - 1 if not (isinstance(ta, int) and ta == 0) else n, 0))
                    pe.matmul(xs_in[0:D // 2], xin[:, 1, 0:D // 2], c.ident[:], start=True, stop=True)
                    pe.matmul(xs_in[D // 2:D], xin[:, 1, D // 2:D], down1[:], start=True, stop=False)
                    pe.matmul(xs_in[D // 2:D], xin[:, 0, D // 2:D], last1[:], start=False, stop=True).then_inc(xs_built.sem, 1)
                if tc is not None:
                    pe.wait_ge(aoT_ready.sem, aoT_ready.at(n + tc, 2))
                    pe.wait_ge(h_ready.sem, h_ready.at(n + tc, 0))
                    for p in range(HP):
                        ins_ = pe.matmul(pC[0][:, 0, :], aoT[:, p, :], wo[:, p, :], start=p == 0, stop=p == HP - 1)
                    ins_.then_inc(wo_done.sem, 1)
                if ta is not None:
                    project_qk(n, ta, 0)
                if tb is not None:
                    turn_qk(n, tb, 0)
                    turn_qk(n, tb, 1)
                if tc is not None:
                    pe.wait_ge(x1_ready.sem, x1_ready.at(n + tc, 1))
                    pe.wait_ge(x2_done.sem, x2_done.at(n + tc, 0))
                    pe.matmul(pC[1][:, 0, 0:D // 2], down1[:], x1w[:, row(tc), D // 2:D], start=True, stop=False)
                    pe.matmul(pC[1][:, 0, 0:D // 2], last1[:], x1w[:, row(tc) - 1, D // 2:D], start=False, stop=True) \
                        .then_inc(sh_done.sem, 1)
                if tb is not None:
                    turn_qk(n, tb, 2)
                    turn_qk(n, tb, 3)
                if tb is not None:
                    pe.wait_ge(att_ready.sem, att_ready.at(n + tb, 0))
                    mk = mask[:, tb % TB, :].unsqueeze(1).broadcast_to([P, HP, DH])
                    for a in range(2):
                        if a == 1:
                            pe.wait_ge(t_copied.sem, t_copied.at(n + tb, 3))
                        pe.matmul(pS[:, a], c.identb[:], mk, start=True, stop=False, skip_group_check=True)
                    scores(0)
                if ta is not None:
                    project_qk(n, ta, 1)
                if tb is not None:
                    pe.wait_ge(t_copied.sem, t_copied.at(n + tb, 4))
                    pe.matmul(pT[0][:, 0, 0:2], c.identb[:], c.identb[:, 0:2], start=True, stop=True)
                    scores(1).then_inc(s_done.sem, 1)
                if ta is not None:
                    project_qk(n, ta, 2)
                if tc is not None:
                    pe.wait_ge(n_ready.sem, n_ready.at(n + tc, 1))
                    pe.transpose(pC[0][:, 0, :], xn1[:], c.ident[:]).then_inc(nT_done.sem, 1)
                if ta is not None:
                    project_qk(n, ta, 3)
                if tc is not None:
                    pe.wait_ge(xnT_ready.sem, xnT_ready.at(n + tc, 1))
                    for a in range(2):
                        for f in range(NF):
                            ins_ = pe.matmul(pC[a][:, f, :], w1[:, a, f * P:(f + 1) * P], xnT[:], start=True, stop=True)
                    ins_.then_inc(w1_done.sem, 1)
                if tb is not None:
                    pe.wait_ge(t_copied.sem, t_copied.at(n + tb, 4))
                    for p in range(HP):
                        if p % 4 == 0:
                            pe.wait_ge(exp_ready.sem, exp_ready.at(n + tb, p // 4 + 1))
                        ins_ = pe.transpose(pT[p // 4][:, p % 4, :], pr[:, p, :, :].rearrange("p a d -> p (a d)"), c.ident[:])
                        if p % 4 == 3:
                            ins_.then_inc(PT_done.sem, 1)
                if ta is not None:
                    values(n, ta, 0)
                if tb is not None:
                    pe.wait_ge(PT_ready.sem, PT_ready.at(n + tb, 1))
                    pe.wait_ge(v_ready.sem, v_ready.at(n + tb, NWT))
                    pe.matmul(pS[:, 0, 0, 0:2], c.identb[:], c.identb[:, 0:2], start=True, stop=True)
                    mix(0)
                if ta is not None:
                    values(n, ta, 1)
                if tb is not None:
                    pe.wait_ge(PT_ready.sem, PT_ready.at(n + tb, 2))
                    pe.matmul(pT[0][:, 0, 0:2], c.identb[:], c.identb[:, 0:2], start=True, stop=True)
                    mix(1).then_inc(pv_done.sem, 1)
                if tc is not None:
                    pe.wait_ge(h_ready.sem, h_ready.at(n + tc, 1))
                    for f in range(NF):
                        pe.matmul(pC[1][:, 0, :], hid[:, f, :], w2[:, f, :], start=f == 0, stop=False)
                    pe.matmul(pC[1][:, 0, :], c.ones[:], b2[:], start=False, stop=True).then_inc(w2_done.sem, 1)
                if ta is not None:
                    values(n, ta, 2)
                if tb is not None:
                    pe.wait_ge(PT_ready.sem, PT_ready.at(n + tb, 2))
                    for p in range(HP):
                        if p % 4 == 0:
                            pe.wait_ge(att_ready.sem, att_ready.at(n + tb, p // 4 + 1))
                        ins_ = pe.transpose(pT[p // 4][:, p % 4, :], att[:, p * P:(p + 1) * P], c.ident[:])
                        if p % 4 == 3:
                            ins_.then_inc(aT_done.sem, 1)
                if ta is not None:
                    values(n, ta, 3)

            layers(pe, start, body)

        @block.scalar
        def _(act):
            def start(L):
                wait_layer(act, L)
                act.wait_ge(x2_done.sem, x2_done.at(L * NT, 0))

            def piece(n, t, j):
                act.wait_ge(qk_done.sem, qk_done.at(n + t, j + 1))
                act.wait_ge(rot_ready.sem, rot_ready.at(n + t, 0))
                act.wait_ge(summed.sem, summed.at(n + t, 0))
                act.activation(raw[:, j, :], pA[(j + 1) % 2][:], ACT.Copy).then_inc(raw_ready.sem, 1)
                act.activation(sq[:, j, :], pA[(j + 1) % 2][:], ACT.Square).then_inc(sq_ready.sem, 1)

            def turned_qk(n, t, g):
                act.wait_ge(t_done.sem, t_done.at(n + t, g + 1))
                dst = (qT[:, 4 * (g % 2):4 * (g % 2) + 4, :] if g < 2 else
                       kT[:, 4 * (g % 2):4 * (g % 2) + 4, WIN:WIN + P])
                act.activation(dst, pT[g % 2][:], ACT.Copy).then_inc(t_copied.sem, 1)

            def value(n, t, w):
                act.wait_ge(v_done.sem, v_done.at(n + t, w + 1))
                act.activation(v2[:, w, :], pA[(w + 1) % 2][:], ACT.Copy).then_inc(v_ready.sem, 1)

            def fetch(n, t):
                act.wait_ge(xs_built.sem, xs_built.at(n + t, 0))
                act.activation(xin[:], xw[:, bass.ds(row(t) - 1, 2), :], ACT.Copy).then_inc(xin_ready.sem, 1)

            def body(n, ta, tb, tc):
                if ta is not None:
                    if isinstance(ta, int) and ta == 0:
                        fetch(n, 0)
                    act.wait_ge(xs_built.sem, xs_built.at(n + ta, 1))
                    act.wait_ge(xtail.sem, xtail.at(n + ta, 1))
                    act.activation(xsT[:, WIN:WIN + P], xs_in, ACT.Copy).then_inc(xsT_ready.sem, 1)
                if tb is not None:
                    turned_qk(n, tb, 0)
                    turned_qk(n, tb, 1)
                if tb is not None:
                    act.wait_ge(ktail.sem, ktail.at(n + tb, 1))
                    turned_qk(n, tb, 2)
                    turned_qk(n, tb, 3)
                if ta is not None:
                    piece(n, ta, 0)
                    piece(n, ta, 1)
                if tc is not None:
                    act.wait_ge(nT_done.sem, nT_done.at(n + tc, 1))
                    act.activation(xnT[:], pC[0][:, 0, :], ACT.Identity, scale=gain[:], bias=shift_[:]).then_inc(xnT_ready.sem, 1)
                if ta is not None:
                    piece(n, ta, 2)
                if tb is not None:
                    for g in range(2):
                        act.wait_ge(sub_ready.sem, sub_ready.at(n + tb, g + 1))
                        half = pr[:, 4 * g:4 * g + 4]
                        act.activation(half, half, ACT.Exp).then_inc(exp_ready.sem, 1)
                if tb is not None:
                    for g in range(2):
                        act.wait_ge(PT_done.sem, PT_done.at(n + tb, g + 1))
                        act.activation(PT[:, 4 * g:4 * g + 4, :], pT[g][:], ACT.Copy).then_inc(PT_ready.sem, 1)
                if ta is not None:
                    piece(n, ta, 3)
                if tc is not None:
                    act.wait_ge(w1_done.sem, w1_done.at(n + tc, 1))
                    for f in range(NF):
                        ins_ = act.activation(gl[:, f, :], pC[1][:, f, :], ACT.Gelu, bias=b1[:, 1, f:f + 1])
                    ins_.then_inc(gl_ready.sem, 1)
                act.activation(turn_table[:], c.ones[0:1, 0:1], ACT.Exp)
                if ta is not None and not (isinstance(ta, int) and ta == NT - 1):
                    fetch(n, ta + 1)
                if ta is not None:
                    if tb is not None:
                        act.wait_ge(pv_done.sem, pv_done.at(n + tb, 1))
                    for w in range(NWT - 1):
                        value(n, ta, w)
                if tb is not None:
                    for g in range(2):
                        act.wait_ge(aT_done.sem, aT_done.at(n + tb, g + 1))
                        if g == 0 and tc is not None:
                            act.wait_ge(wo_done.sem, wo_done.at(n + tc, 1))
                        act.activation(aoT[:, 4 * g:4 * g + 4, :], pT[g][:], ACT.Copy).then_inc(aoT_ready.sem, 1)
                if ta is not None:
                    value(n, ta, NWT - 1)

            layers(act, start, body)

        @block.vector
        def _(dve):
            dve.wait_ge(base_in.sem, base_in.base + 64)
            dve.wait_ge(made.sem, mb + 18)

            def start(L):
                wait_layer(dve, L)
                for op in range(2):
                    dve.tensor_tensor(tab[:, :, 2 * op, :], base[2 * op][:], qks[:, op, :].unsqueeze(1).broadcast_to([P, TB, DH]),
                                      ALU.mult).then_inc(tabs.sem, 1)
                    half = DH // 2
                    for a in range(2):
                        dve.tensor_tensor(tab[:, :, 2 * op + 1, a * half:(a + 1) * half],
                                          base[2 * op + 1][:, :, a * half:(a + 1) * half],
                                          qks[:, op, (1 - a) * half:(2 - a) * half].unsqueeze(1).broadcast_to([P, TB, half]),
                                          ALU.mult).then_inc(tabs.sem, 1)
                dve.wait_ge(tabs.sem, tabs.at(L, 6))

            def turn_piece(n, t, j):
                if j == 0:
                    dve.wait_ge(t_done.sem, t_done.at(n + t, 0))
                    dve.wait_ge(cur_ready.sem, cur_ready.at(n + t, 1))
                dve.wait_ge(qk_done.sem, qk_done.at(n + t, j + 1))
                dve.wait_ge(sq_ready.sem, sq_ready.at(n + t, j + 1))
                cosine = cur[:, 2 * (j // 2), :].unsqueeze(1).broadcast_to([P, CW // DH, DH])
                dve.tensor_tensor(qk[:, j, :].rearrange("p (h d) -> p h d", d=DH),
                                  pA[(j + 1) % 2][:].rearrange("p (h d) -> p h d", d=DH), cosine, ALU.mult).then_inc(u_ready.sem, 1)

            def squares(n, t, a):
                dve.wait_ge(sq_ready.sem, sq_ready.at(n + t, 2 * a + 2))
                if a == 0:
                    dve.wait_ge(qk_ready.sem, qk_ready.at(n + t, 0))
                dve.reduce_sum(ssq[:, a * H:(a + 1) * H], sq[:, 2 * a:2 * a + 2, :].rearrange("p a (h d) -> p (a h) d", d=DH),
                               AX.X).then_inc(summed.sem, 1)

            def body(n, ta, tb, tc):
                if ta is not None:
                    dve.wait_ge(rot_ready.sem, rot_ready.at(n + ta, 0))
                    dve.wait_ge(u_ready.sem, u_ready.at(n + ta, 0))
                    dve.wait_ge(ktail.sem, ktail.at(n + ta, 0))
                    dve.tensor_scalar(cur[:], tab[:, ta % TB], 1.0, None, ALU.mult).then_inc(cur_ready.sem, 1)
                if tc is not None:
                    ch = Chain(dve, cchain, n + tc)
                    dve.wait_ge(wo_done.sem, wo_done.at(n + tc, 1))
                    dve.tensor_tensor(x1w[:, row(tc), :], pC[0][:, 0, :], xw[:, row(tc), :], ALU.add).then_inc(x1_ready.sem, 1)
                    dve.wait_ge(x1_ready.sem, x1_ready.at(n + tc, 1))
                    dve.tensor_scalar(xs1[:, 0, 0:D // 2], x1w[:, row(tc), 0:D // 2], 1.0, None, ALU.mult)
                    dve.wait_ge(sh_done.sem, sh_done.at(n + tc, 1))
                    ch.link(dve.tensor_copy(xs1[:, 0, D // 2:D], pC[1][:, 0, 0:D // 2]))
                    ch.wait()
                    ins_ = dve.bn_stats(stats[:, 0, :], xs1[:, 0, :])
                    croot_stats(dve, ch, ins_, stats, work)
                    ch.wait()
                    croots.request(dve, work[:, 6, :], work[:, 1, :], EPS_LN, ALU.add)
                if ta is not None:
                    turn_piece(n, ta, 0)
                if tc is not None:
                    croots.receive(dve, n + tc)
                    dve.tensor_scalar(xn1[:], xs1[:, 0, :], work[:, 0, 0:1], work[:, 6, 0:1], ALU.subtract, ALU.mult) \
                        .then_inc(n_ready.sem, 1)
                if ta is not None:
                    turn_piece(n, ta, 1)
                if tb is not None:
                    dve.wait_ge(s_done.sem, s_done.at(n + tb, 1))
                    for g in range(2):
                        part = pS[:, :, 4 * g:4 * g + 4, :]
                        mg = mx[:].rearrange("p (a b) -> p a b", a=2)[:, :, 4 * g:4 * g + 4]
                        dve.reduce_max(mg, part, AX.X).then_inc(mxd.sem, 1)
                        dve.wait_ge(mxd.sem, mxd.at(n + tb, g + 1))
                        dve.tensor_tensor(pr[:, 4 * g:4 * g + 4].rearrange("p b a d -> p a b d"), part,
                                          mg.unsqueeze(3).broadcast_to([P, 2, HP // 2, DH]), ALU.subtract) \
                            .then_inc(sub_ready.sem, 1)
                if ta is not None:
                    turn_piece(n, ta, 2)
                    squares(n, ta, 0)
                    turn_piece(n, ta, 3)
                    squares(n, ta, 1)
                    dve.wait_ge(summed.sem, summed.at(n + ta, 2))
                    qroots.request(dve, inv[:], ssq[:], 1e-24, ALU.max)
                if tc is not None:
                    dve.wait_ge(gl_ready.sem, gl_ready.at(n + tc, 1))
                    for f in range(NF):
                        ins_ = dve.scalar_tensor_tensor(out=hid[:, f, :], in0=pC[0][:, f, :], scalar=b1[:, 0, f:f + 1],
                                                        in1=gl[:, f, :], op0=ALU.add, op1=ALU.mult)
                    ins_.then_inc(h_ready.sem, 1)
                if tb is not None:
                    dve.wait_ge(exp_ready.sem, exp_ready.at(n + tb, 2))
                    prv = pr[:].rearrange("p b a d -> p a b d")
                    dve.reduce_sum(tot[:].rearrange("p (a b) -> p a b", a=2), prv, AX.X).then_inc(totd.sem, 1)
                    dve.wait_ge(totd.sem, totd.at(n + tb, 1))
                    dve.reciprocal(tot[:], tot[:]).then_inc(inv_ready.sem, 1)
                if tb is not None:
                    dve.wait_ge(pv_done.sem, pv_done.at(n + tb, 1))
                    dve.wait_ge(inv_ready.sem, inv_ready.at(n + tb, 1))
                    for g in range(2):
                        dve.tensor_tensor(att[:, 4 * g * P:(4 * g + 4) * P].rearrange("p (b a d) -> p a b d", a=2, d=DH),
                                          pS[:, :, 4 * g:4 * g + 4, :],
                                          tot[:].rearrange("p (a b) -> p a b", a=2)[:, :, 4 * g:4 * g + 4].unsqueeze(3)
                                          .broadcast_to([P, 2, HP // 2, DH]), ALU.mult).then_inc(att_ready.sem, 1)
                if tc is not None:
                    dve.wait_ge(w2_done.sem, w2_done.at(n + tc, 1))
                    dve.tensor_tensor(xw[:, row(tc), :], pC[1][:, 0, :], x1w[:, row(tc), :], ALU.add).then_inc(x2_done.sem, 1)
                if ta is not None:
                    dve.wait_ge(rot_ready.sem, rot_ready.at(n + ta, QKC))
                    dve.wait_ge(u_ready.sem, u_ready.at(n + ta, QKC))
                    dve.tensor_tensor(qk[:], qk[:], rot[:], ALU.add).then_inc(added_rot.sem, 1)
                    qroots.receive(dve, n + ta)
                    dve.wait_ge(added_rot.sem, added_rot.at(n + ta, 1))
                    for a in range(2):
                        qv = qk[:, 2 * a:2 * a + 2, :].rearrange("p a (h d) -> p (a h) d", d=DH)
                        dve.tensor_tensor(qv, qv, inv[:, a * H:(a + 1) * H].unsqueeze(2).broadcast_to([P, H, DH]), ALU.mult) \
                            .then_inc(qk_ready.sem, 1)

            layers(dve, start, body)


def croot_stats(dve, ch, ins_, stats, work):
    ch.link(ins_)
    row_stats(dve, ch, stats, work, 1)


class Roots2:

    def __init__(self, c, name):
        self.asked, self.given = c.new_signal(f"{name}_asked", 1), c.new_signal(f"{name}_given", 1)

    def request(self, e, out, value, floor, op):
        e.tensor_scalar(out, value, floor, None, op).then_inc(self.asked.sem, 1)

    def receive(self, e, turn):
        e.wait_ge(self.given.sem, self.given.at(turn, 1))

    def ask(self, e, chain, turn, out, value, floor, op):
        chain.wait()
        self.request(e, out, value, floor, op)
        self.receive(e, turn)

    def give(self, pool, c, turn, value):
        pool.wait_ge(self.asked.sem, self.asked.at(turn, 1))
        pool.tensor_tensor(value, value, c.half[:, 0:value.shape[1]], ALU.pow).then_inc(self.given.sem, 1)


def local(c):
    nc = c.nc
    with ExitStack() as st_:
        xw = st_.enter_context(nc.sbuf_tensor("xw", [P, B * (TB + 1), D], FP32))
        x1w = st_.enter_context(nc.sbuf_tensor("x1w", [P, B * (TB + 1), D], FP32))
        zeroed = c.new_signal("pads_zeroed", 1)
        with nc.Block() as block:
            @block.gpsimd
            def _(pool):
                c.lift(pool)
                for a in (xw, x1w):
                    pool.memset(a[:], 0.0).then_inc(zeroed.sem, 1)
                pool.wait_ge(zeroed.sem, zeroed.base + 2)
        enter_local(c, xw)
        local_stack(c, xw, x1w)
        leave_local(c, xw)


NE, HID = 8, 384
HC = HID // P


def experts(c):
    nc, ins = c.nc, c.ins
    NFRONT, NCHAIN = 17, 6
    T_AT, R_AT = 3, 4
    with ExitStack() as st_:
        def sb(name, shape, dt=FP32):
            return st_.enter_context(nc.sbuf_tensor(f"{name}_moe", shape, dt))

        def ps(name, shape, dt=FP32):
            return st_.enter_context(nc.psum_tensor(f"{name}_moe", shape, dt))

        wg, wu, wd = sb("wg", [P, NE, HID]), sb("wu", [P, NE, HID]), sb("wd", [P, NE * HC, D])
        wr, gain = sb("wr", [P, NE]), sb("gain", [P, 1])
        lower = sb("lower", [P, NE, NE])
        xn, xnT = sb("xn", [P, CH, D]), [sb(f"xnT{n}", [P, CW]) for n in range(2)]
        fstats, fwork = sb("fstats", [P, CH, 6]), sb("fwork", [P, 9, CH])
        stats, work = sb("stats", [P, CH, 6]), sb("work", [P, 9, CH])
        lg, ex, wt = sb("lg", [P, CH, NE]), sb("ex", [P, CH, NE]), sb("wt", [P, CH, NE])
        top, tot, comb = sb("top", [P, CH]), sb("tot", [P, CH]), [sb(f"comb{n}", [P, CH, NE]) for n in range(2)]
        gt, eq = sb("gt", [P, CH, NE, NE]), sb("eq", [P, CH, NE, NE])
        rank = sb("rank", [P, CH, NE])
        act_g = [sb(f"act_g{n}", [P, CW]) for n in range(2)]
        hid = [[sb(f"hid{n}{m}", [P, CW]) for m in range(HC)] for n in range(2)]
        acc, y = sb("acc", [P, CH, D]), sb("y", [P, CH, D])
        pT, pR = ps("pT", [P, CW]), ps("pR", [P, CH, NE])
        pG = [ps(f"pG{n}", [P, CW]) for n in range(2)]
        pU = [ps(f"pU{n}", [P, CW]) for n in range(2)]
        pD = [ps(f"pD{n}", [P, CH, D]) for n in range(2)]

        loaded, made = c.new_signal("moe_loaded", 0), c.new_signal("moe_made", 0)
        chain = c.new_signal("moe_chain", NCHAIN)
        front_chain = c.new_signal("moe_front_chain", NFRONT)
        roots, rms_roots = Roots(c, 1), Roots2(c, "rms_root")
        normed, turned, xT_ready = c.new_signal("moe_normed", 1), c.new_signal("moe_turned", 1), c.new_signal("moe_xT_ready", 1)
        routed, shifted, expd = c.new_signal("routed", 1), c.new_signal("logits_shifted", 1), c.new_signal("logits_exped", 1)
        up = c.new_signal("up_done", NE * HC)
        gated = c.new_signal("gated", NE * HC)
        hid_ready = c.new_signal("hid_ready", NE * HC)
        down = c.new_signal("down_done", NE)
        taken = c.new_signal("down_taken", NE)
        added = c.new_signal("moe_added", 1)
        block = st_.enter_context(nc.Block())

        def chunks(eng, front, body):
            front(0, 0)
            with eng.Fori(0, B - 1) as b:
                for half in range(HALVES):
                    body(b * HALVES + half, half, True)
            body(NC_ - 2, 0, True)
            body(NC_ - 1, 1, False)

        @block.sync
        def _(sp):
            c.lift(sp)
            for dst, src in ((wr, ins["moe_wr"]), (gain, ins["moe_g"]), (wg, ins["moe_wg"].rearrange("x d h -> d x h")),
                             (wu, ins["moe_wu"].rearrange("x d h -> d x h")),
                             (wd, ins["moe_wd"].rearrange("x (c p) d -> p (x c) d", p=P))):
                sp.dma_start(dst[:], src).then_inc(loaded.sem, 16)
            sp.wait_ge(loaded.sem, loaded.base + 80)

        @block.gpsimd
        def _(pool):
            pool.memset(lower[:], 1.0).then_inc(made.sem, 1)
            pool.wait_ge(made.sem, made.base + 1)
            pool.affine_select(out=lower[:], in_=lower[:], compare_op=ALU.is_ge, fill=0.0, base=-1,
                               pattern=[[1, NE], [-1, NE]], channel_multiplier=0).then_inc(made.sem, 1)

            def front(i, n):
                rms_roots.give(pool, c, i, fwork[:, 8, :])

            def body(i, n, more):
                if more:
                    front(i + 1, 1 - n)
                roots.give(pool, c, i, 1, work[:, 6, :])

            chunks(pool, front, body)

        @block.scalar
        def _(act):
            act.wait_ge(loaded.sem, loaded.base + 80)

            def copy_xnT(i, n):
                act.wait_ge(turned.sem, turned.at(i, 1))
                act.wait_ge(up.sem, up.at(i - 1 if not (isinstance(i, int) and i == 0) else 0, 0))
                act.activation(xnT[n][:], pT[:], ACT.Copy, scale=gain[:]).then_inc(xT_ready.sem, 1)

            def exponentials(i):
                act.wait_ge(shifted.sem, shifted.at(i, 1))
                act.activation(ex[:], wt[:], ACT.Exp).then_inc(expd.sem, 1)

            def front(i, n):
                copy_xnT(i, n)
                exponentials(i)

            def body(i, n, more):
                for x in range(NE):
                    if more and x == T_AT + 1:
                        copy_xnT(i + 1, 1 - n)
                    if more and x == R_AT + 2:
                        exponentials(i + 1)
                    for m in range(HC):
                        u = x * HC + m
                        act.wait_ge(up.sem, up.at(i, u + 1))
                        act.wait_ge(hid_ready.sem, hid_ready.at(i, max(u - 1, 0)))
                        act.activation(act_g[u % 2][:], pG[u % 2][:], ACT.Silu).then_inc(gated.sem, 1)

            chunks(act, front, body)

        @block.tensor
        def _(pe):
            pe.wait_ge(loaded.sem, loaded.base + 80)

            def turn(i):
                pe.wait_ge(normed.sem, normed.at(i, 1))
                pe.wait_ge(xT_ready.sem, xT_ready.at(i, 0))
                for t in range(CH):
                    ins_ = pe.transpose(pT[:, t * P:(t + 1) * P], xn[:, t, :], c.ident[:])
                ins_.then_inc(turned.sem, 1)

            def route(i, n):
                pe.wait_ge(xT_ready.sem, xT_ready.at(i, 1))
                for t in range(CH):
                    ins_ = pe.matmul(pR[:, t, :], xnT[n][:, t * P:(t + 1) * P], wr[:], start=True, stop=True)
                ins_.then_inc(routed.sem, 1)

            def front(i, n):
                turn(i)
                route(i, n)

            def go_down(i, x):
                pe.wait_ge(hid_ready.sem, hid_ready.at(i, (x + 1) * HC))
                pe.wait_ge(taken.sem, taken.at(i, max(x - 1, 0)))
                for t in range(CH):
                    for m in range(HC):
                        ins_ = pe.matmul(pD[x % 2][:, t, :], hid[x % 2][m][:, t * P:(t + 1) * P], wd[:, x * HC + m, :],
                                         start=m == 0, stop=m == HC - 1)
                ins_.then_inc(down.sem, 1)

            def body(i, n, more):
                for x in range(NE):
                    for m in range(HC):
                        u = x * HC + m
                        pe.wait_ge(hid_ready.sem, hid_ready.at(i, max(u - 1, 0)))
                        pe.matmul(pG[u % 2][:], wg[:, x, m * P:(m + 1) * P], xnT[n][:], start=True, stop=True)
                        pe.matmul(pU[u % 2][:], wu[:, x, m * P:(m + 1) * P], xnT[n][:], start=True, stop=True) \
                            .then_inc(up.sem, 1)
                    if x:
                        go_down(i, x - 1)
                    if more and x == T_AT:
                        turn(i + 1)
                    if more and x == R_AT:
                        route(i + 1, 1 - n)
                go_down(i, NE - 1)

            chunks(pe, front, body)

        @block.vector
        def _(dve):
            dve.wait_ge(made.sem, made.base + 2)

            def stats_of(i):
                ch = Chain(dve, front_chain, i)
                for t in range(CH):
                    ins_ = dve.bn_stats(fstats[:, t, :], c.xl[:, i * CH + t, :])
                ch.link(ins_)
                row_stats(dve, ch, fstats, fwork, CH)
                return ch

            def norm(i, ch):
                def step(ins_):
                    ch.link(ins_)
                    ch.wait()

                ch.wait()
                step(dve.tensor_tensor(fwork[:, 7, :], fwork[:, 0, :], fwork[:, 0, :], ALU.mult))
                ch.link(dve.tensor_tensor(fwork[:, 7, :], fwork[:, 7, :], fwork[:, 1, :], ALU.add))
                rms_roots.ask(dve, ch, i, fwork[:, 8, :], fwork[:, 7, :], EPS_RMS, ALU.add)
                dve.wait_ge(turned.sem, turned.at(i, 0))
                for t in range(CH):
                    ins_ = dve.tensor_scalar(xn[:, t, :], c.xl[:, i * CH + t, :], fwork[:, 8, t:t + 1], None, ALU.mult)
                ins_.then_inc(normed.sem, 1)

            def rank_experts(i, ch):
                def step(ins_):
                    ch.link(ins_)
                    ch.wait()

                dve.wait_ge(routed.sem, routed.at(i, 1))
                step(dve.tensor_copy(lg[:], pR[:]))
                step(dve.reduce_max(top[:], lg[:], AX.X))
                dve.tensor_tensor(wt[:], lg[:], top[:].unsqueeze(2).broadcast_to([P, CH, NE]), ALU.subtract) \
                    .then_inc(shifted.sem, 1)
                other = lg[:].unsqueeze(2).broadcast_to([P, CH, NE, NE])
                own = lg[:].unsqueeze(3).broadcast_to([P, CH, NE, NE])
                for t in range(CH):
                    dve.tensor_tensor(gt[:, t], other[:, t], own[:, t], ALU.is_gt)
                    ins_ = dve.tensor_tensor(eq[:, t], other[:, t], own[:, t], ALU.is_equal)
                step(ins_)
                for t in range(CH):
                    ins_ = dve.tensor_tensor(eq[:, t], eq[:, t], lower[:], ALU.mult)
                step(ins_)
                step(dve.tensor_tensor(gt[:], gt[:], eq[:], ALU.add))
                step(dve.reduce_sum(rank[:], gt[:], AX.X))
                step(dve.tensor_scalar(rank[:], rank[:], 1.5, None, ALU.is_lt))

            def weigh(i, n, ch):
                def step(ins_):
                    ch.link(ins_)
                    ch.wait()

                dve.wait_ge(expd.sem, expd.at(i, 1))
                step(dve.tensor_tensor(wt[:], ex[:], rank[:], ALU.mult))
                step(dve.reduce_sum(tot[:], wt[:], AX.X))
                step(dve.reciprocal(tot[:], tot[:]))
                step(dve.tensor_tensor(comb[n][:], wt[:], tot[:].unsqueeze(2).broadcast_to([P, CH, NE]), ALU.mult))
                assert ch.count == NFRONT, ch.count

            def front(i, n):
                ch = stats_of(i)
                norm(i, ch)
                rank_experts(i, ch)
                weigh(i, n, ch)

            def take(i, n, x):
                dve.wait_ge(down.sem, down.at(i, x + 1))
                if x:
                    dve.wait_ge(taken.sem, taken.at(i, x))
                for t in range(CH):
                    if x == 0:
                        ins_ = dve.tensor_scalar(acc[:, t, :], pD[0][:, t, :], comb[n][:, t, 0:1], None, ALU.mult)
                    else:
                        ins_ = dve.scalar_tensor_tensor(out=acc[:, t, :], in0=pD[x % 2][:, t, :],
                                                        scalar=comb[n][:, t, x:x + 1], in1=acc[:, t, :],
                                                        op0=ALU.mult, op1=ALU.add)
                ins_.then_inc(taken.sem, 1)

            def body(i, n, more):
                for x in range(NE):
                    for m in range(HC):
                        u = x * HC + m
                        dve.wait_ge(gated.sem, gated.at(i, u + 1))
                        if m == 0:
                            dve.wait_ge(down.sem, down.at(i, max(x - 1, 0)))
                        dve.tensor_tensor(hid[x % 2][m][:], pU[u % 2][:], act_g[u % 2][:], ALU.mult).then_inc(hid_ready.sem, 1)
                    if x:
                        take(i, n, x - 1)
                    if more and x == T_AT - 2:
                        ahead = stats_of(i + 1)
                    if more and x == T_AT - 1:
                        norm(i + 1, ahead)
                    if more and x == R_AT + 1:
                        rank_experts(i + 1, ahead)
                    if more and x == R_AT + 2:
                        weigh(i + 1, 1 - n, ahead)
                take(i, n, NE - 1)
                dve.wait_ge(taken.sem, taken.at(i, NE))
                ch = Chain(dve, chain, i)
                ch.link(dve.tensor_tensor(acc[:], acc[:], c.xl[:, bass.ds(i * CH, CH), :], ALU.add))
                ch.wait()
                roots.count = 0
                layernorm_add(dve, ch, roots, acc, y, stats, work, c.x, i, added, more=True)
                assert ch.count == NCHAIN, ch.count

            chunks(dve, front, body)


def build(nc, ins, out, until=99):
    ctx = ExitStack()
    with ctx:
        c = Core(nc, ins, ctx)
        scr = {"mha": nc.dram_tensor("scratch_mha", (2, B * NG, 3, HG * 8, S), BF16, kind="Internal").ap(),
               "low_rank": nc.dram_tensor("scratch_low", (2, B * NG, 3, HG * 32, S), BF16, kind="Internal").ap(),
               "v": nc.dram_tensor("scratch_v", (B * NG * S, HG * VC), FP32, kind="Internal").ap()}
        scr["rope"] = scr["mha"]
        setup(c, ins["x"])
        for n, kind in enumerate(("mha", "local", "low_rank", "rope")):
            if n >= until:
                break
            if kind == "local":
                local(c)
                continue
            project(c, kind, scr)
            attend(c, kind, scr)
            post(c, kind)
            if kind == "rope":
                experts(c)
        store_out(c, out)


def local_layouts(f):
    import numpy as np

    half = np.arange(0, DH, 2, dtype=np.float32)
    t = np.arange(S, dtype=np.float32)
    freqs = t[:, None] * (np.float32(1.0) / np.float32(10000.0) ** (half / np.float32(DH)))[None, :]
    freqs = np.concatenate([freqs, freqs], -1).astype(np.float32)
    base = (half + np.float32(0.4 * DH)) / np.float32(1.4 * DH)
    scale = base[None, :].astype(np.float32) ** ((t - S // 2) / np.float32(WIN // 2))[:, None].astype(np.float32)
    scale = np.concatenate([scale, scale], -1)
    sign = np.where(np.arange(DH) < DH // 2, -1.0, 1.0).astype(np.float32)
    cos, sin = np.cos(freqs), np.sin(freqs) * sign
    inv = np.float32(1.0) / scale
    HI = 341

    def pad(w, axis):
        wide = list(w.shape)
        wide[axis] = NF * P - HI
        return np.concatenate([w, np.zeros(wide, w.dtype)], axis)

    w1 = pad(f("L0_ffn_W1").reshape(-1, D, 2, HI), 3)
    b1 = pad(f("L0_ffn_b1").reshape(-1, 2, HI), 2).reshape(-1, 2, NF, P).transpose(0, 3, 1, 2)
    return {
        "local_wqkv": f("L0_ffn_Wqkv"), "local_wo": f("L0_ffn_Wo"), "local_w1": w1, "local_b1": b1,
        "local_w2": pad(f("L0_ffn_W2"), 1), "local_b2": f("L0_ffn_b2"), "local_g": f("L0_ffn_ln_g").reshape(-1, D, 1),
        "local_b": f("L0_ffn_ln_b").reshape(-1, D, 1), "local_qs": f("L0_ffn_q_scale"), "local_ks": f("L0_ffn_k_scale"),
        "local_table0": cos * scale * np.float32(8.0), "local_table1": sin * scale * np.float32(8.0),
        "local_table2": cos * inv, "local_table3": sin * inv,
    }


def layouts(inputs):
    import numpy as np

    f = lambda n: np.asarray(inputs[n])
    heads_last = lambda w: np.ascontiguousarray(w.transpose(1, 0, 2).reshape(D, -1))
    t = np.arange(S, dtype=np.float32)
    inv = (1.0 / np.float32(10000.0) ** (np.arange(0, 8, 2, dtype=np.float32) / np.float32(8))).astype(np.float32)
    emb = np.einsum("i,j->ij", t, inv)
    emb = np.concatenate([emb, emb], -1)
    grouped = lambda w: np.ascontiguousarray(w.reshape(-1, NG, HG, 8).transpose(0, 1, 3, 2).reshape(-1, P))
    cos, sin = (np.tile(np.repeat(g(emb).T.astype(np.float32), HG, axis=0), (NG, 1)) for g in (np.cos, np.sin))
    qs = np.float32(8 ** -0.5)
    return {
        "x": f("L0_attn_embeddings").reshape(B * S, D),
        "mha_wq": grouped(heads_last(f("L0_attn_Wq"))), "mha_wk": grouped(heads_last(f("L0_attn_Wk"))), "mha_wv": heads_last(f("L0_attn_Wv")),
        "mha_bq": grouped(f("L0_attn_bq").reshape(1, P)).T, "mha_bk": grouped(f("L0_attn_bk").reshape(1, P)).T,
        "mha_bv": f("L0_attn_bv").reshape(1, P), "mha_wo": f("L0_attn_Wo"), "mha_bo": f("L0_attn_bo").reshape(1, D),
        "low_rank_wq1": f("L1_attn_Wq1").T, "low_rank_wk1": f("L1_attn_Wk1").T, "low_rank_wq2": f("L1_attn_Wq2").T,
        "low_rank_wk2": f("L1_attn_Wk2").T, "low_rank_wv": f("L1_attn_Wv").T, "low_rank_wo": f("L1_attn_Wo").T,
        "low_rank_bo": f("L1_attn_bo").reshape(1, D),
        "rope_wq": grouped(f("L1_ffn_wq")), "rope_wk": grouped(f("L1_ffn_wk")), "rope_wv": f("L1_ffn_wv"), "rope_wo": f("L1_ffn_wo"),
        **local_layouts(f),
        "moe_wr": f("L1_ffn_w_router"), "moe_g": f("L1_ffn_g2").reshape(D, 1), "moe_wg": f("L1_ffn_wg"),
        "moe_wu": f("L1_ffn_wu"), "moe_wd": f("L1_ffn_wd"),
        "rope_g": f("L1_ffn_g1").reshape(D, 1),
        "rope_table0": cos * qs, "rope_table1": sin * qs, "rope_table2": cos, "rope_table3": sin,
    }


def program(nc, shapes, until=99):
    ins = {n: nc.dram_tensor(f"in_{n}", s, FP32, kind="ExternalInput").ap() for n, s in shapes.items()}
    out = nc.dram_tensor("out_x", (B * S, D), FP32, kind="ExternalOutput").ap()
    build(nc, ins, out, until)


def kernel(**inputs):
    import numpy as np
    import concourse.bacc as bacc
    from concourse.bass_utils import run_bass_kernel_spmd

    arrays = {n: np.ascontiguousarray(a) for n, a in layouts(inputs).items()}
    nc = bacc.Bacc("TRN2", target_bir_lowering=False, num_devices=1)
    program(nc, {n: a.shape for n, a in arrays.items()})
    r = run_bass_kernel_spmd(nc, [{f"in_{n}": a for n, a in arrays.items()}], core_ids=[0])
    return r.results[0]["out_x"].reshape(B, S, D)
```
